# Optimizing a Trainium2 kernel written in Bass

```python
import numpy as np
import jax
import jax.numpy as jnp

def _softmax(x, axis=-1):
    return jax.nn.softmax(x, axis=axis)

def _gelu(x):
    return jax.nn.gelu(x, approximate=True)

def _silu(x):
    return jax.nn.silu(x)

def _sigmoid(x):
    return jax.nn.sigmoid(x)

def _layernorm(x, axis=-1, eps=1e-05):
    m = jnp.mean(x, axis=axis, keepdims=True)
    v = jnp.var(x, axis=axis, keepdims=True)
    return (x - m) / jnp.sqrt(v + eps)

def _scatter_add(tgt, idx, src, axis=0):
    return tgt.at[idx].add(src)

def _segment_sum(src, seg, n):
    return jax.ops.segment_sum(src, seg, n)
kernel_name = 'mk_decoder_postln_d2_seqx_r8_a77712'

def setup_inputs(seed: int=0):
    np.random.seed(seed)
    _w = jnp.asarray

    def _rec_inputs():
        import jax
        import jax.numpy as jnp
        _rk = jax.random.key(seed)
        x = -0.0003929 + 0.9999 * jax.random.normal(jax.random.fold_in(_rk, 1), (8, 128, 512), jnp.float32)
        _lenS = 128 - jax.random.randint(jax.random.fold_in(_rk, 7), (8,), 0, max(1, 128 // 4) + 1, jnp.int32)
        _lenS2 = 128 - jax.random.randint(jax.random.fold_in(_rk, 8), (8,), 0, max(1, 128 // 4) + 1, jnp.int32)
        _ctx_4096P = jax.random.normal(jax.random.fold_in(_rk, 11), (8, 16, 512), jnp.float32)
        _ctx_4096c = jax.random.dirichlet(jax.random.fold_in(_rk, 511), 0.3 * jnp.ones((16,), jnp.float32), (8, 128))
        _ctx_4096t = jnp.einsum('bsk,bkd->bsd', _ctx_4096c, _ctx_4096P)
        _ctx_4096t = _ctx_4096t * jax.lax.rsqrt(jnp.mean(jnp.square(_ctx_4096t)) + 1e-12) * 0.953939
        ctx_4096 = 2.81802e-05 + 1.00001 * (_ctx_4096t + 0.3 * jax.random.normal(jax.random.fold_in(_rk, 611), (8, 128, 512), jnp.float32))
        return (x, ctx_4096)
    x, ctx_4096 = _rec_inputs()

    def _L0_attn_setup():
        import jax, jax.numpy as jnp
        import numpy as np
        H = 512
        D = H // 4
        key = jax.random.key(seed)
        k1, k2, k3, k4, k5 = jax.random.split(key, 5)
        x = jax.random.normal(k1, (4, 512, H), dtype=jnp.float32)
        s_in = 1.0 / np.sqrt(H)
        Wqkv = jax.random.normal(k2, (H, 3 * D), dtype=jnp.float32) * s_in
        bqkv = jax.random.normal(k3, (3 * D,), dtype=jnp.float32) * 0.01
        Wo = jax.random.normal(k4, (D, H), dtype=jnp.float32) * (1.0 / np.sqrt(D))
        bo = jax.random.normal(k5, (H,), dtype=jnp.float32) * 0.01
        return {'x': x, 'Wqkv': Wqkv, 'bqkv': bqkv, 'Wo': Wo, 'bo': bo}
    _L0_attn_all = _L0_attn_setup()
    _L0_attn_in = {k: v for k, v in _L0_attn_all.items() if k in ('Wqkv', 'bqkv', 'Wo', 'bo')}
    del _L0_attn_all

    def _L0_xattn_setup():
        import jax, jax.numpy as jnp
        import numpy as np
        EMB_DIM = 64
        HEADS = 8
        key = jax.random.key(seed)
        kq, kk, kv = jax.random.split(key, 3)
        B, C, N = (8, EMB_DIM, 512)
        q = jax.random.normal(kq, (B, C, N), dtype=jnp.float32)
        k = jax.random.normal(kk, (B, C, N), dtype=jnp.float32)
        v = jax.random.normal(kv, (B, C, N), dtype=jnp.float32)
        return {'q': q, 'k': k, 'v': v}
    _L0_xattn_all = _L0_xattn_setup()
    _L0_xattn_in = {k: v for k, v in _L0_xattn_all.items() if k in ()}
    del _L0_xattn_all

    def _L0_ffn_setup():
        import jax, jax.numpy as jnp
        import numpy as np
        RANKS = (8, 16, 32, 64)
        TOPK = 1
        SCALING = 1.0 / 4
        key = jax.random.key(seed)
        ks = jax.random.split(key, 7)
        D_IN, D_OUT, MAX_R, N_RANKS = (512, 512, 64, len(RANKS))
        B_, S_ = (4, 256)
        return {'hidden_states': jax.random.normal(ks[0], (B_, S_, D_IN), jnp.float32), 'W': jax.random.normal(ks[1], (D_OUT, D_IN), jnp.float32) * 0.02, 'b': jax.random.normal(ks[2], (D_OUT,), jnp.float32) * 0.02, 'A': jax.random.normal(ks[3], (MAX_R, D_IN), jnp.float32) * 0.02, 'B': jnp.zeros((D_OUT, MAX_R), jnp.float32) + jax.random.normal(ks[4], (D_OUT, MAX_R), jnp.float32) * 0.02, 'gate_w': jax.random.normal(ks[5], (N_RANKS, D_IN), jnp.float32) * 0.02, 'gate_b': jax.random.normal(ks[6], (N_RANKS,), jnp.float32) * 0.02}
    _L0_ffn_all = _L0_ffn_setup()
    _L0_ffn_in = {k: v for k, v in _L0_ffn_all.items() if k in ('W', 'b', 'A', 'B', 'gate_w', 'gate_b')}
    del _L0_ffn_all

    def _L1_attn_setup():
        import jax, jax.numpy as jnp
        import numpy as np
        H, KV, HD, HID = (32, 8, 128, 512)
        THETA, FACTOR, HI_FF, LO_FF, ORIG_MAX = (500000.0, 8.0, 4.0, 1.0, 1024)

        def _llama3_inv_freq():
            inv = 1.0 / THETA ** (np.arange(0, HD, 2, dtype=np.float64) / HD)
            wavelen = 2.0 * np.pi / inv
            low_wl = ORIG_MAX / LO_FF
            high_wl = ORIG_MAX / HI_FF
            smooth = (ORIG_MAX / wavelen - LO_FF) / (HI_FF - LO_FF)
            scaled = np.where(wavelen > low_wl, inv / FACTOR, inv)
            mid = (wavelen <= low_wl) & (wavelen >= high_wl)
            scaled = np.where(mid, (1 - smooth) * inv / FACTOR + smooth * inv, scaled)
            return scaled.astype(np.float32)

        def _rope_cos_sin(T):
            inv = _llama3_inv_freq()
            pos = np.arange(T, dtype=np.float32)
            freqs = pos[:, None] * inv[None, :]
            emb = np.concatenate([freqs, freqs], axis=-1)
            return (jnp.asarray(np.cos(emb)), jnp.asarray(np.sin(emb)))

        def _rotate_half(x):
            x1, x2 = jnp.split(x, 2, axis=-1)
            return jnp.concatenate([-x2, x1], axis=-1)
        key = jax.random.key(seed)
        ks = jax.random.split(key, 5)
        s = 1.0 / np.sqrt(HID)
        return {'x': jax.random.normal(ks[0], (1, 256, HID), jnp.float32), 'wq': jax.random.normal(ks[1], (HID, H * HD), jnp.float32) * s, 'wk': jax.random.normal(ks[2], (HID, KV * HD), jnp.float32) * s, 'wv': jax.random.normal(ks[3], (HID, KV * HD), jnp.float32) * s, 'wo': jax.random.normal(ks[4], (H * HD, HID), jnp.float32) * s}
    _L1_attn_all = _L1_attn_setup()
    _L1_attn_in = {k: v for k, v in _L1_attn_all.items() if k in ('wq', 'wk', 'wv', 'wo')}
    del _L1_attn_all

    def _L1_xattn_setup():
        import jax, jax.numpy as jnp
        import numpy as np
        HID = 512
        NHEAD = 32
        NKV = 8
        HDIM = 128
        G = NHEAD // NKV
        key = jax.random.key(seed)
        ks = jax.random.split(key, 6)
        s = 0.02
        B, L = (2, 256)
        return {'query': jax.random.normal(ks[0], (B, L, HID), jnp.float32), 'kv': jax.random.normal(ks[1], (B, L, HID), jnp.float32), 'Wq': jax.random.normal(ks[2], (HID, NHEAD * HDIM), jnp.float32) * s, 'bq': jnp.zeros((NHEAD * HDIM,), jnp.float32), 'Wkv': jax.random.normal(ks[3], (HID, 2 * NKV * HDIM), jnp.float32) * s, 'bkv': jnp.zeros((2 * NKV * HDIM,), jnp.float32), 'Wo': jax.random.normal(ks[4], (NHEAD * HDIM, HID), jnp.float32) * s, 'bo': jnp.zeros((HID,), jnp.float32)}
    _L1_xattn_all = _L1_xattn_setup()
    _L1_xattn_in = {k: v for k, v in _L1_xattn_all.items() if k in ('Wq', 'bq', 'Wkv', 'bkv', 'Wo', 'bo')}
    del _L1_xattn_all

    def _L1_ffn_setup():
        import jax, jax.numpy as jnp
        import numpy as np
        N_EXPERTS = 8
        TOP_K = 2
        D_MODEL = 512
        RANK = 64
        key = jax.random.key(seed)
        k0, k1, k2, k3 = jax.random.split(key, 4)
        inputs = jax.random.normal(k0, (4, 256, D_MODEL), dtype=jnp.float32)
        gate_w = jax.random.normal(k1, (N_EXPERTS, D_MODEL), dtype=jnp.float32) * 0.02
        lora_A = jax.random.normal(k2, (N_EXPERTS, RANK, D_MODEL), dtype=jnp.float32) * 0.02
        lora_B = jax.random.normal(k3, (N_EXPERTS, D_MODEL, RANK), dtype=jnp.float32) * 0.02
        return {'inputs': inputs, 'gate_w': gate_w, 'lora_A': lora_A, 'lora_B': lora_B}
    _L1_ffn_all = _L1_ffn_setup()
    _L1_ffn_in = {k: v for k, v in _L1_ffn_all.items() if k in ('gate_w', 'lora_A', 'lora_B')}
    del _L1_ffn_all
    return {'x': x, 'ctx_4096': ctx_4096, 'L0_attn_Wqkv': _L0_attn_in['Wqkv'], 'L0_attn_bqkv': _L0_attn_in['bqkv'], 'L0_attn_Wo': _L0_attn_in['Wo'], 'L0_attn_bo': _L0_attn_in['bo'], 'L0_ffn_W': _L0_ffn_in['W'], 'L0_ffn_b': _L0_ffn_in['b'], 'L0_ffn_A': _L0_ffn_in['A'], 'L0_ffn_B': _L0_ffn_in['B'], 'L0_ffn_gate_w': _L0_ffn_in['gate_w'], 'L0_ffn_gate_b': _L0_ffn_in['gate_b'], 'L1_attn_wq': _L1_attn_in['wq'], 'L1_attn_wk': _L1_attn_in['wk'], 'L1_attn_wv': _L1_attn_in['wv'], 'L1_attn_wo': _L1_attn_in['wo'], 'L1_xattn_Wq': _L1_xattn_in['Wq'], 'L1_xattn_bq': _L1_xattn_in['bq'], 'L1_xattn_Wkv': _L1_xattn_in['Wkv'], 'L1_xattn_bkv': _L1_xattn_in['bkv'], 'L1_xattn_Wo': _L1_xattn_in['Wo'], 'L1_xattn_bo': _L1_xattn_in['bo'], 'L1_ffn_gate_w': _L1_ffn_in['gate_w'], 'L1_ffn_lora_A': _L1_ffn_in['lora_A'], 'L1_ffn_lora_B': _L1_ffn_in['lora_B']}

def reference(x, ctx_4096, L0_attn_Wqkv, L0_attn_bqkv, L0_attn_Wo, L0_attn_bo, L0_ffn_W, L0_ffn_b, L0_ffn_A, L0_ffn_B, L0_ffn_gate_w, L0_ffn_gate_b, L1_attn_wq, L1_attn_wk, L1_attn_wv, L1_attn_wo, L1_xattn_Wq, L1_xattn_bq, L1_xattn_Wkv, L1_xattn_bkv, L1_xattn_Wo, L1_xattn_bo, L1_ffn_gate_w, L1_ffn_lora_A, L1_ffn_lora_B):
    import jax
    import jax.numpy as jnp

    def _L0_attn_ref(x, Wqkv, bqkv, Wo, bo):
        import jax, jax.numpy as jnp
        import numpy as np
        H = 512
        D = H // 4
        B, S, C = x.shape
        d = C // 4
        qkv = jnp.einsum('bsc,cf->bsf', x, Wqkv) + bqkv
        qkv = qkv.reshape(B, S, 3, d)
        q, k, v = (qkv[:, :, 0], qkv[:, :, 1], qkv[:, :, 2])
        scale = 1.0 / jnp.sqrt(jnp.float32(d)).astype(x.dtype)
        attn = jnp.einsum('bqd,bkd->bqk', q, k) * scale
        attn = jax.nn.softmax(attn, axis=-1)
        out = jnp.einsum('bqk,bkd->bqd', attn, v)
        return jnp.einsum('bqd,dc->bqc', out, Wo) + bo

    def _L0_xattn_ref(q, k, v):
        import jax, jax.numpy as jnp
        import numpy as np
        EMB_DIM = 64
        HEADS = 8
        B, C, N = q.shape
        H = HEADS
        dh = C // H
        qh = q.transpose(0, 2, 1).reshape(B, N, H, dh)
        kh = k.transpose(0, 2, 1).reshape(B, N, H, dh)
        vh = v.transpose(0, 2, 1).reshape(B, N, H, dh)
        qh = jax.nn.softmax(qh, axis=3)
        kh = jax.nn.softmax(kh, axis=1)
        kvs = jnp.einsum('bnhd,bnhe->bhde', kh, vh)
        out = jnp.einsum('bnhd,bhde->bnhe', qh, kvs)
        return out.transpose(0, 2, 3, 1).reshape(B, C, N)

    def _L0_ffn_ref(hidden_states, W, b, A, B, gate_w, gate_b):
        import jax, jax.numpy as jnp
        import numpy as np
        RANKS = (8, 16, 32, 64)
        TOPK = 1
        SCALING = 1.0 / 4
        bsz, seq, d_in = hidden_states.shape
        out = jnp.einsum('bsd,od->bso', hidden_states, W) + b
        x = hidden_states.reshape(-1, d_in)
        scores = x @ gate_w.T + gate_b
        probs = jax.nn.softmax(scores, axis=-1)
        routing_weights, selected = jax.lax.top_k(probs, TOPK)
        routing_weights = routing_weights / jnp.sum(routing_weights, axis=-1, keepdims=True)
        lora_outputs = jnp.stack([x @ A[:r, :].T @ B[:, :r].T for r in RANKS], axis=1)
        sel = jnp.take_along_axis(lora_outputs, selected[:, :, None], axis=1)
        final = jnp.sum(sel * routing_weights[:, :, None], axis=1)
        return out + final.reshape(bsz, seq, -1)

    def _L1_attn_ref(x, wq, wk, wv, wo):
        import jax, jax.numpy as jnp
        import numpy as np
        H, KV, HD, HID = (32, 8, 128, 512)
        THETA, FACTOR, HI_FF, LO_FF, ORIG_MAX = (500000.0, 8.0, 4.0, 1.0, 1024)

        def _llama3_inv_freq():
            inv = 1.0 / THETA ** (np.arange(0, HD, 2, dtype=np.float64) / HD)
            wavelen = 2.0 * np.pi / inv
            low_wl = ORIG_MAX / LO_FF
            high_wl = ORIG_MAX / HI_FF
            smooth = (ORIG_MAX / wavelen - LO_FF) / (HI_FF - LO_FF)
            scaled = np.where(wavelen > low_wl, inv / FACTOR, inv)
            mid = (wavelen <= low_wl) & (wavelen >= high_wl)
            scaled = np.where(mid, (1 - smooth) * inv / FACTOR + smooth * inv, scaled)
            return scaled.astype(np.float32)

        def _rope_cos_sin(T):
            inv = _llama3_inv_freq()
            pos = np.arange(T, dtype=np.float32)
            freqs = pos[:, None] * inv[None, :]
            emb = np.concatenate([freqs, freqs], axis=-1)
            return (jnp.asarray(np.cos(emb)), jnp.asarray(np.sin(emb)))

        def _rotate_half(x):
            x1, x2 = jnp.split(x, 2, axis=-1)
            return jnp.concatenate([-x2, x1], axis=-1)
        B, T, _ = x.shape
        q = (x @ wq).reshape(B, T, H, HD).transpose(0, 2, 1, 3)
        k = (x @ wk).reshape(B, T, KV, HD).transpose(0, 2, 1, 3)
        v = (x @ wv).reshape(B, T, KV, HD).transpose(0, 2, 1, 3)
        cos, sin = _rope_cos_sin(T)
        q = q * cos + _rotate_half(q) * sin
        k = k * cos + _rotate_half(k) * sin
        rep = H // KV
        k = jnp.repeat(k, rep, axis=1)
        v = jnp.repeat(v, rep, axis=1)
        scores = jnp.einsum('bhtd,bhsd->bhts', q, k) * (1.0 / np.sqrt(HD))
        mask = jnp.tril(jnp.ones((T, T), dtype=bool))
        scores = jnp.where(mask, scores, -jnp.inf)
        att = jax.nn.softmax(scores, axis=-1)
        out = jnp.einsum('bhts,bhsd->bhtd', att, v)
        out = out.transpose(0, 2, 1, 3).reshape(B, T, H * HD)
        return out @ wo

    def _L1_xattn_ref(query, kv, Wq, bq, Wkv, bkv, Wo, bo):
        import jax, jax.numpy as jnp
        import numpy as np
        HID = 512
        NHEAD = 32
        NKV = 8
        HDIM = 128
        G = NHEAD // NKV
        B, L, _ = query.shape
        Lk = kv.shape[1]
        scale = jnp.asarray(1.0 / np.sqrt(HDIM), query.dtype)
        q = (query @ Wq + bq).reshape(B, L, NKV, G, HDIM)
        k_, v_ = jnp.split(kv @ Wkv + bkv, 2, axis=-1)
        k = k_.reshape(B, Lk, NKV, HDIM)
        v = v_.reshape(B, Lk, NKV, HDIM)
        scores = jnp.einsum('blkgd,bmkd->bkglm', q, k) * scale
        attn = jax.nn.softmax(scores, axis=-1)
        o = jnp.einsum('bkglm,bmkd->blkgd', attn, v).reshape(B, L, NHEAD * HDIM)
        return o @ Wo + bo

    def _L1_ffn_ref(inputs, gate_w, lora_A, lora_B):
        import jax, jax.numpy as jnp
        import numpy as np
        N_EXPERTS = 8
        TOP_K = 2
        D_MODEL = 512
        RANK = 64
        x = inputs.reshape(-1, inputs.shape[-1])
        T = x.shape[0]
        gate_probs = jax.nn.softmax(x @ gate_w.T, axis=-1)
        weights, sel = jax.lax.top_k(gate_probs, TOP_K)
        weights = weights / jnp.sum(weights, axis=-1, keepdims=True)
        w_full = jnp.zeros((T, N_EXPERTS), dtype=x.dtype).at[jnp.arange(T)[:, None], sel].add(weights)
        out = jnp.zeros((T, D_MODEL), dtype=x.dtype)
        for e in range(N_EXPERTS):
            y = x @ lora_A[e].T @ lora_B[e].T
            out = out + w_full[:, e:e + 1] * y
        return out.reshape(inputs.shape[:-1] + (D_MODEL,))
    x = _layernorm(x + _L0_attn_ref(x, L0_attn_Wqkv, L0_attn_bqkv, L0_attn_Wo, L0_attn_bo), axis=-1)
    x = _layernorm(x + _L0_xattn_ref(x, ctx_4096, ctx_4096), axis=-1)
    x = _layernorm(x + _L0_ffn_ref(x, L0_ffn_W, L0_ffn_b, L0_ffn_A, L0_ffn_B, L0_ffn_gate_w, L0_ffn_gate_b), axis=-1)
    x = _layernorm(x + _L1_attn_ref(x, L1_attn_wq, L1_attn_wk, L1_attn_wv, L1_attn_wo), axis=-1)
    x = _layernorm(x + _L1_xattn_ref(x, ctx_4096, L1_xattn_Wq, L1_xattn_bq, L1_xattn_Wkv, L1_xattn_bkv, L1_xattn_Wo, L1_xattn_bo), axis=-1)
    x = _layernorm(x + _L1_ffn_ref(x, L1_ffn_gate_w, L1_ffn_lora_A, L1_ffn_lora_B), axis=-1)
    return x

_drawn_inputs = setup_inputs


def setup_inputs(seed=0):
    import zlib

    import numpy as np

    out = dict(_drawn_inputs(seed))
    spreads = {'L1_xattn_bq': (0.0, 0.8), 'L1_xattn_bkv': (0.0, 0.1), 'L1_xattn_bo': (0.0, 0.1)}
    factors = {'L0_ffn_gate_b': 23.583}
    for name, (base, spread) in spreads.items():
        noise = np.random.default_rng([zlib.crc32(name.encode()), seed]).standard_normal(out[name].shape)
        drawn = base * np.exp(spread * noise) if base else spread * noise
        out[name] = jnp.asarray(drawn.astype(out[name].dtype))
    for name, factor in factors.items():
        out[name] = (out[name] * factor).astype(out[name].dtype)
    return out
```

```python
from contextlib import ExitStack

import concourse.bass as bass
from concourse import mybir

F32 = mybir.dt.float32
F32R = mybir.dt.float32r
U32 = mybir.dt.uint32
ALU = mybir.AluOpType
ACT = mybir.ActivationFunctionType
AX = mybir.AxisListType

P = 128
B = 8
D = 512
NC = D // P
TOK = B * P
HALF = TOK // 2
HB = B // 2
HD = 128
GROUPS = 8
REP = 4
TILES = 2 + REP
WT = NC * TILES * P
WTB = WT + 8
WO = NC * D
NT, NO = WT // D, WO // D
SLOT_FFN0, SLOT_ATTN, SLOT_XATTN, SLOT_MOE = 1, 2, 2 + GROUPS, 2 + 2 * GROUPS
SLOTS = SLOT_MOE + 1
XH, XD = 8, 16
LR, NE0 = 64, 4
NE = 8
SCALE = float(HD) ** -0.5
EPS = 1e-5
NEG = -1e30
C_ID, C_COS, C_SIN, C_CAUSAL, C_BLOCK, C_GROUP, C_SEG, C_IOTA, C_POW = 0, 128, 256, 384, 512, 640, 648, 712, 720
CONSTS = 728
R_BO0, R_B1, R_BO5, R_GATE = 0, D, 2 * D, 3 * D
ROWS = 3 * D + 8


def build(nc, x_in, ctx_in, w_tile, w_out, consts, rows, out):
    with ExitStack() as stack:
        def sb(name, shape, dt=F32):
            return stack.enter_context(nc.sbuf_tensor(name, shape, dt))

        def sem(name):
            return stack.enter_context(nc.semaphore(name))

        x = sb("x", [P, B, D])
        xTh, xTl = sb("xTh", [P, NC, TOK], F32R), sb("xTl", [P, NC, TOK], F32R)
        cTh, cTl = sb("cTh", [P, NC, TOK], F32R), sb("cTl", [P, NC, TOK], F32R)
        raw_t, raw_o = sb("raw_t", [P, WTB]), sb("raw_o", [P, WO])
        wth, wtl = sb("wth", [P, WT], F32R), sb("wtl", [P, WT], F32R)
        woh, wol = sb("woh", [P, WO], F32R), sb("wol", [P, WO], F32R)
        tbias = sb("tbias", [P, 8])
        qT = sb("qT", [P, REP, TOK])
        KT = sb("KT", [P, TOK])
        VT = sb("VT", [P, 2, HALF])
        Vh, Vl = sb("Vh", [P, B, HD], F32R), sb("Vl", [P, B, HD], F32R)
        prob = sb("prob", [P, 2, D])
        sm = sb("sm", [P, 2, D])
        m1, m2 = sb("m1", [P, 2, D]), sb("m2", [P, 2, D])
        PTh, PTl = sb("PTh", [P, D], F32R), sb("PTl", [P, D], F32R)
        OTh, OTl = sb("OTh", [P, D], F32R), sb("OTl", [P, D], F32R)
        kvm = sb("kvm", [P, B, P + XH])
        cst = sb("cst", [P, CONSTS])
        row = sb("row", [P, D + NE])
        stats = sb("stats", [P, B, 6])
        mv = sb("mv", [P, B, 2])
        vare = sb("vare", [P, B])
        rstd = sb("rstd", [P, B])
        nmax = sb("nmax", [P, 2, REP])
        nbias = sb("nbias", [P, 2, REP])
        esum = sb("esum", [P, 2, REP])
        rsum = sb("rsum", [P, 2, REP])
        cmax, csum, crs = sb("cmax", [P, B]), sb("csum", [P, B]), sb("crs", [P, B])
        rden = sb("rden", [P, 2, NC, XH])
        g8 = sb("g8", [P, 2, 8])
        t8 = sb("t8", [P, 2, 8])
        i8 = sb("i8", [P, 2, 8], U32)
        f8 = sb("f8", [P, 2, 8])
        e8 = sb("e8", [P, 2, 8])
        w8 = sb("w8", [P, 2, 2, 8])
        s1 = sb("s1", [P, 2, 4])

        ps = stack.enter_context(nc.psum_tensor("ps", [P, 8, D], F32))
        pA = [ps[:, 0, :], ps[:, 1, :]]
        pS = [ps[:, 2, :], ps[:, 3, :]]
        pT = [ps[:, 4, :], ps[:, 5, :]]
        pO, pY = ps[:, 6, :], ps[:, 7, :]

        ident = cst[:, C_ID:C_ID + P]
        cosT = cst[:, C_COS:C_COS + P].unsqueeze(1).to_broadcast([P, HB, P])
        causal = cst[:, C_CAUSAL:C_CAUSAL + P].unsqueeze(1).to_broadcast([P, REP, P])

        def four(ap):
            return ap.rearrange("p (a b) -> p a b", a=4)

        const_in, row_in = sem("const_in"), sem("row_in")
        x_loaded = [sem(f"x_loaded{b}") for b in range(B)]
        ctx_loaded = [sem(f"ctx_loaded{b}") for b in range(B)]
        t_raw, t_hi, t_lo, t_used = sem("t_raw"), sem("t_hi"), sem("t_lo"), sem("t_used")
        o_raw, o_hi, o_lo, o_used = sem("o_raw"), sem("o_hi"), sem("o_lo"), sem("o_used")
        bias_ready = sem("bias_ready")
        c_set, c_max, c_exp, c_turned = sem("c_set"), sem("c_max"), sem("c_exp"), sem("c_turned")
        c_act, c_dve, c_kv, c_rs, c_kvm = sem("c_act"), sem("c_dve"), sem("c_kv"), sem("c_rs"), sem("c_kvm")
        added, stat_ready, mv_ready, var_ready = sem("added"), sem("stat_ready"), sem("mv_ready"), sem("var_ready")
        rstd_ready, normed, xt_turned = sem("rstd_ready"), sem("normed"), sem("xt_turned")
        xt_hi, xt_lo, res_ready = sem("xt_hi"), sem("xt_lo"), sem("res_ready")
        NORMS = [B * k for k in range(6)]
        HALVES = [2 * k for k in range(6)]
        TURNS = {0: 0, 2: B, 3: 2 * B, 4: 3 * B, 5: 4 * B}
        ADDS = {0: 0, 1: B, 2: 2 * B, 5: 3 * B}
        BIASES = {0: 0, 2: B, 4: 2 * B}
        out_done = sem("out_done")

        def load_slot(sp, s):
            if not isinstance(s, int) or s:
                sp.wait_ge(t_lo, s * NT)
                sp.wait_ge(bias_ready, s)
            sp.dma_start(raw_t[:, :], w_tile[bass.ds(s, 1)].rearrange("a p n -> p (a n)")).then_inc(t_raw, 16)
            if not isinstance(s, int) or s:
                sp.wait_ge(o_lo, s * NO)
            sp.dma_start(raw_o[:, :], w_out[bass.ds(s, 1)].rearrange("a p n -> p (a n)")).then_inc(o_raw, 16)

        def split_tile_hi(act, s, k):
            if k == 0:
                act.wait_ge(t_raw, s * 16 + 16)
                if not isinstance(s, int) or s:
                    act.wait_ge(t_used, s)
                act.activation(tbias[:, :], raw_t[:, WT:WTB], ACT.Copy).then_inc(bias_ready, 1)
            act.activation(wth[:, k * D:(k + 1) * D], raw_t[:, k * D:(k + 1) * D], ACT.Copy).then_inc(t_hi, 1)

        def split_tile_lo(pool, s, k):
            c = slice(k * D, (k + 1) * D)
            pool.wait_ge(t_hi, s * NT + k + 1)
            pool.tensor_tensor(wtl[:, c], raw_t[:, c], wth[:, c].bitcast(F32), ALU.subtract).then_inc(t_lo, 1)

        def split_out_hi(act, s, k):
            if k == 0:
                act.wait_ge(o_raw, s * 16 + 16)
                if not isinstance(s, int) or s:
                    act.wait_ge(o_used, s)
            act.activation(woh[:, k * D:(k + 1) * D], raw_o[:, k * D:(k + 1) * D], ACT.Copy).then_inc(o_hi, 1)

        def split_out_lo(pool, s, k):
            c = slice(k * D, (k + 1) * D)
            pool.wait_ge(o_hi, s * NO + k + 1)
            pool.tensor_tensor(wol[:, c], raw_o[:, c], woh[:, c].bitcast(F32), ALU.subtract).then_inc(o_lo, 1)

        def mm3(pe, o, wh, wl, xh, xl, first, last, before=None):
            mm = pe.matmul(o, wl, xh, start=first, stop=False)
            if before is not None:
                mm.then_inc(before, 1)
            pe.matmul(o, wh, xl, start=False, stop=False)
            return pe.matmul(o, wh, xh, start=False, stop=last)

        def wt_tile(w, c, t):
            return w[:, (c * TILES + t) * P:(c * TILES + t + 1) * P]

        def tile_product(pe, o, t, half, src_h, src_l, before=None):
            cols = slice(half * HALF, (half + 1) * HALF)
            for c in range(NC):
                mm = mm3(pe, o, wt_tile(wth, c, t), wt_tile(wtl, c, t), src_h[:, c, cols], src_l[:, c, cols],
                         c == 0, c == NC - 1, before if c == 0 else None)
            return mm

        def turn_pe(pe, k, b, before=None):
            if k == 0:
                pe.wait_ge(x_loaded[b], 16)
            else:
                pe.wait_ge(normed, NORMS[k - 1] + b + 1)
            if b >= 2:
                pe.wait_ge(xt_lo, TURNS[k] + b - 1)
            for c in range(NC):
                t = pe.transpose(pA[b % 2][:, c * P:(c + 1) * P], x[:, b, c * P:(c + 1) * P], ident)
                if c == 0 and before is not None:
                    t.then_inc(before, 1)
            t.then_inc(xt_turned, 1)

        def turn_act(act, k, b):
            act.wait_ge(xt_turned, TURNS[k] + b + 1)
            act.activation(xTh[:, :, b * P:(b + 1) * P], four(pA[b % 2]), ACT.Copy).then_inc(xt_hi, 1)

        def turn_dve(dve, k, b):
            dve.wait_ge(xt_hi, TURNS[k] + b + 1)
            dve.tensor_tensor(xTl[:, :, b * P:(b + 1) * P], four(pA[b % 2]),
                              xTh[:, :, b * P:(b + 1) * P].bitcast(F32), ALU.subtract).then_inc(xt_lo, 1)

        def residual_bias(pool, k, b, loads):
            if b == 0:
                pool.wait_ge(row_in, 16 * loads)
            pool.wait_ge(xt_turned, TURNS[k] + b + 1)
            pool.tensor_tensor(x[:, b, :], x[:, b, :], row[:, 0:D], ALU.add).then_inc(res_ready, 1)

        def norm_stats(dve, k, b, summed=None):
            if summed is None:
                dve.wait_ge(added, ADDS[k] + b + 1)
            dve.bn_stats(stats[:, b, :], x[:, b, :]).then_inc(stat_ready, 1)
            dve.wait_ge(stat_ready, NORMS[k] + b + 1)
            dve.bn_aggr(mv[:, b, :], stats[:, b, :]).then_inc(mv_ready, 1)
            if b % HB == HB - 1:
                h = slice(b - HB + 1, b + 1)
                dve.wait_ge(mv_ready, NORMS[k] + b + 1)
                dve.tensor_scalar(vare[:, h], mv[:, h, 1], EPS, None, ALU.add).then_inc(var_ready, 1)

        def norm_pow(pool, k, half):
            h = slice(half * HB, (half + 1) * HB)
            pool.wait_ge(var_ready, HALVES[k] + half + 1)
            pool.tensor_tensor(rstd[:, h], vare[:, h], cst[:, C_POW:C_POW + HB], ALU.pow).then_inc(rstd_ready, 1)

        def norm_apply(dve, k, half):
            dve.wait_ge(rstd_ready, HALVES[k] + half + 1)
            for b in range(half * HB, (half + 1) * HB):
                dve.tensor_scalar(x[:, b, :], x[:, b, :], mv[:, b, 0:1], rstd[:, b:b + 1], ALU.subtract, ALU.mult)\
                    .then_inc(normed, 1)

        class Softmax:
            def __init__(self, name):
                self.scores = sem(name + "_scores")
                self.masked = sem(name + "_masked") if name == "ga" else None
                self.max = sem(name + "_max")
                self.bias = sem(name + "_bias")
                self.exp = sem(name + "_exp")
                self.recip = sem(name + "_recip")
                self.prob = sem(name + "_prob")

        def soft_max(dve, sf, u, n, mask, s_free=None):
            dve.wait_ge(sf.scores, u + 1)
            src = four(pS[n])
            if mask:
                dve.tensor_tensor(four(sm[:, n, :]), src, causal, ALU.add).then_inc(sf.masked, 1)
                dve.wait_ge(sf.masked, u + 1)
                src = four(sm[:, n, :])
            dve.tensor_reduce(nmax[:, n, :], src, AX.X, ALU.max, negate=True).then_inc(sf.max, 1)
            dve.wait_ge(sf.max, u + 1)
            dve.tensor_scalar(nbias[:, n, :], nmax[:, n, :], SCALE, None, ALU.mult).then_inc(sf.bias, 1)

        def soft_exp(act, sf, u, n, mask):
            act.wait_ge(sf.bias, u + 1)
            for h in range(4):
                src = (sm[:, n, :] if mask else pS[n])[:, h * P:(h + 1) * P]
                a = act.activation(prob[:, n, h * P:(h + 1) * P], src, ACT.Exp, bias=nbias[:, n, h:h + 1],
                                   scale=SCALE, accum_out=esum[:, n, h:h + 1])
            a.then_inc(sf.exp, 1)

        def soft_recip(dve, sf, u, n):
            dve.wait_ge(sf.exp, u + 1)
            dve.reciprocal(rsum[:, n, :], esum[:, n, :]).then_inc(sf.recip, 1)

        def soft_norm(pool, sf, u, n):
            pool.wait_ge(sf.recip, u + 1)
            pool.tensor_tensor(four(prob[:, n, :]), four(prob[:, n, :]),
                               rsum[:, n, :].unsqueeze(2).to_broadcast([P, 4, P]), ALU.mult).then_inc(sf.prob, 1)

        l0 = Softmax("l0")
        a_ready, a_free = sem("l0_tile_ready"), sem("l0_tile_copied")
        l0_vturned, l0_vcopied = sem("l0_vturned"), sem("l0_vcopied")
        l0_pturned, l0_pcopied = sem("l0_pturned"), sem("l0_pcopied")
        l0_o, l0_ohi, l0_olo, l0_y = sem("l0_o"), sem("l0_ohi"), sem("l0_olo"), sem("l0_y")
        L0_TILES = [(t, half) for half in range(2) for t in range(3)]

        x2_exp, x2_num, x2_rden = sem("x2_exp"), sem("x2_num"), sem("x2_rden")
        x2_mul, x2_turned = sem("x2_mul"), sem("x2_turned")

        f_h, f_hm, f_step = sem("f_h"), sem("f_hm"), sem("f_step")
        f_turned, f_hi, f_lo, f_y = (sem("f_" + n) for n in ("turned", "hi", "lo", "y"))

        e_h, e_neg, e_exp, e_hw = sem("e_h"), sem("e_neg"), sem("e_exp"), sem("e_hw")
        e_step = sem("e_step")
        e_turned, e_hi, e_lo, e_y = (sem("e_" + n) for n in ("turned", "hi", "lo", "y"))

        class Grouped:

            def __init__(self, name, slot, k, cross):
                self.slot, self.k, self.cross = slot, k, cross
                self.soft = Softmax(name)
                self.tile_ready = sem(name + "_tile_ready")
                self.rope_m = None if cross else sem(name + "_rope_m")
                self.tile_done = sem(name + "_tile_done")
                self.vt = None if cross else sem(name + "_vt")
                self.turned = sem(name + "_turned")
                self.t_hi, self.t_lo = sem(name + "_t_hi"), sem(name + "_t_lo")
                self.o, self.o_hi, self.o_lo = sem(name + "_o"), sem(name + "_o_hi"), sem(name + "_o_lo")
                self.y = sem(name + "_y")
                self.y_added = sem(name + "_y_added")

        attn = Grouped("ga", SLOT_ATTN, 3, False)
        xattn = Grouped("gx", SLOT_XATTN, 4, True)
        G_TILES = [(0, 0), (0, 1), (1, 0), (1, 1)] + [(2 + h, 0) for h in range(REP)] + [(2 + h, 1) for h in range(REP)]
        NG = len(G_TILES)
        NR = NG - 2
        ROPES = [sum(t != 1 for t, _ in G_TILES[:j]) for j in range(NG)]
        NU = 2 + B

        def tile_dst(t, half):
            c = slice(half * HALF, (half + 1) * HALF)
            return KT[:, c] if t == 0 else VT[:, half, :] if t == 1 else qT[:, t - 2, c]

        def g_pe(pe, g):
            sf = g.soft
            pe.wait_ge(xt_lo, TURNS[g.k] + B)
            with pe.Fori(0, GROUPS) as i:
                pe.wait_ge(t_lo, i * NT + (g.slot + 1) * NT)

                def turn(n):
                    if n >= 2:
                        pe.wait_ge(sf.prob, i * B + n - 1)
                    elif g.cross:
                        pe.wait_ge(g.tile_done, i * NG + n + 3)
                    else:
                        pe.wait_ge(g.vt, i * 2 + n + 1)
                    if n == 2:
                        pe.wait_ge(g.t_lo, i * NU + 1)
                    for j in range(4):
                        s = VT[:, n, j * P:(j + 1) * P] if n < 2 else prob[:, n % 2, j * P:(j + 1) * P]
                        t = pe.transpose(pT[n % 2][:, j * P:(j + 1) * P], s, ident)
                    t.then_inc(g.turned, 1)

                for j, (t, half) in enumerate(G_TILES):
                    if j >= 2 and g.cross:
                        pe.wait_ge(g.tile_done, i * NG + j - 1)
                    elif j >= 2 and G_TILES[j - 2][0] == 1:
                        pe.wait_ge(g.vt, i * 2 + j - 3)
                    elif j >= 2:
                        pe.wait_ge(g.rope_m, i * NR + ROPES[j - 2] + 1)
                    sh, sl = (cTh, cTl) if g.cross and t < 2 else (xTh, xTl)
                    tile_product(pe, pA[j % 2], t, half, sh, sl, o_used if j == 0 else None).then_inc(g.tile_ready, 1)
                    if j in (4, 5):
                        turn(j - 4)

                def scores(b):
                    done = NG if g.cross else NR
                    pe.wait_ge(g.tile_done, i * done + (done if b >= HB else done - REP))
                    for h in range(REP):
                        mm = pe.matmul(pS[b % 2][:, h * P:(h + 1) * P], qT[:, h, b * P:(b + 1) * P],
                                       KT[:, b * P:(b + 1) * P], start=True, stop=True)
                        if b == 0 and h == 0:
                            mm.then_inc(t_used, 1)
                    mm.then_inc(sf.scores, 1)

                def values(b):
                    pe.wait_ge(g.t_lo, i * NU + b + 3)
                    mm3(pe, pO, Vh[:, b, :], Vl[:, b, :], PTh[:, :], PTl[:, :], True, True).then_inc(g.o, 1)

                def project(b):
                    if b == 0:
                        pe.wait_ge(o_lo, i * NO + (g.slot + 1) * NO)
                    pe.wait_ge(g.o_lo, i * B + b + 1)
                    pe.wait_ge(g.y_added, i * B + b + 1)
                    for h in range(REP):
                        c = slice(h * P, (h + 1) * P)
                        w = slice(h * D, (h + 1) * D)
                        mm = mm3(pe, pY, OTh[:, c], OTl[:, c], woh[:, w], wol[:, w], h == 0, h == REP - 1)
                    mm.then_inc(g.y, 1)

                scores(0)
                for b in range(B):
                    if b < B - 1:
                        scores(b + 1)
                    turn(b + 2)
                    if b:
                        project(b - 1)
                    values(b)
                project(B - 1)

        def g_act(act, g):
            sf = g.soft
            with act.Fori(0, GROUPS) as i:
                def split_high(n):
                    act.wait_ge(g.turned, i * NU + n + 1)
                    o = Vh[:, n * HB:(n + 1) * HB, :] if n < 2 else four(PTh[:, :])
                    act.activation(o, four(pT[n % 2]), ACT.Copy).then_inc(g.t_hi, 1)

                def out_high(b):
                    act.wait_ge(g.o, i * B + b + 1)
                    act.activation(OTh[:, :], pO, ACT.Copy).then_inc(g.o_hi, 1)

                def exps(b):
                    n = b % 2
                    act.wait_ge(g.turned, i * NU + b + 1)
                    act.wait_ge(sf.bias, i * B + b + 1)
                    for h in range(REP):
                        c = slice(h * P, (h + 1) * P)
                        src = pS[n][:, c] if g.cross else sm[:, n, c]
                        a = act.activation(prob[:, n, c], src, ACT.Exp, bias=nbias[:, n, h:h + 1],
                                           scale=SCALE, accum_out=esum[:, n, h:h + 1])
                    a.then_inc(sf.exp, 1)

                for j, (t, half) in enumerate(G_TILES):
                    if g.cross:
                        act.wait_ge(g.tile_ready, i * NG + j + 1)
                        act.activation(tile_dst(t, half), pA[j % 2], ACT.Identity, bias=tbias[:, t:t + 1])\
                            .then_inc(g.tile_done, 1)
                    elif t == 1:
                        act.wait_ge(g.tile_ready, i * NG + j + 1)
                        act.activation(tile_dst(t, half), pA[j % 2], ACT.Copy).then_inc(g.vt, 1)
                    if j in (5, 6):
                        split_high(j - 5)
                    if 4 <= j < 4 + NO:
                        split_out_hi(act, i + g.slot, j - 4)
                exps(0)
                for b in range(B):
                    split_high(b + 2)
                    if b < NT:
                        split_tile_hi(act, i + (g.slot + 1), b)
                    if b < B - 1:
                        exps(b + 1)
                    out_high(b)

        def g_dve(dve, g):
            sf = g.soft
            dve.sem_inc(g.y_added, 1)
            if g.cross:
                dve.wait_ge(res_ready, BIASES[g.k] + B)
            with dve.Fori(0, GROUPS) as i:
                def split_low(n):
                    dve.wait_ge(g.t_hi, i * NU + n + 1)
                    h = slice(n * HB, (n + 1) * HB)
                    o, hi = (Vl[:, h, :], Vh[:, h, :]) if n < 2 else (four(PTl[:, :]), four(PTh[:, :]))
                    dve.tensor_tensor(o, four(pT[n % 2]), hi.bitcast(F32), ALU.subtract).then_inc(g.t_lo, 1)

                def out_low(b):
                    dve.wait_ge(g.o_hi, i * B + b + 1)
                    dve.tensor_tensor(OTl[:, :], pO, OTh[:, :].bitcast(F32), ALU.subtract).then_inc(g.o_lo, 1)

                def add(b):
                    dve.wait_ge(g.y, i * B + b + 1)
                    dve.tensor_tensor(x[:, b, :], pY, x[:, b, :], ALU.add).then_inc(g.y_added, 1)

                def maxima(b):
                    n = b % 2
                    dve.wait_ge(sf.scores, i * B + b + 1)
                    src = four(pS[n])
                    if not g.cross:
                        dve.tensor_tensor(four(sm[:, n, :]), src, causal, ALU.add).then_inc(sf.masked, 1)
                        dve.wait_ge(sf.masked, i * B + b + 1)
                        src = four(sm[:, n, :])
                    dve.tensor_reduce(nmax[:, n, :], src, AX.X, ALU.max, negate=True).then_inc(sf.max, 1)
                    dve.wait_ge(sf.max, i * B + b + 1)
                    dve.tensor_scalar(nbias[:, n, :], nmax[:, n, :], SCALE, None, ALU.mult).then_inc(sf.bias, 1)

                def recip(b):
                    dve.wait_ge(sf.exp, i * B + b + 1)
                    dve.reciprocal(rsum[:, b % 2, :], esum[:, b % 2, :]).then_inc(sf.recip, 1)

                for j, (t, half) in enumerate(G_TILES):
                    if not g.cross and t != 1:
                        r = ROPES[j]
                        n, src = r % 2, pA[j % 2]
                        dve.wait_ge(g.tile_ready, i * NG + j + 1)
                        if r >= 2:
                            dve.wait_ge(g.tile_done, i * NR + r - 1)
                        dve.tensor_tensor(four(m1[:, n, :]), four(src), cosT, ALU.mult)
                        for a in range(2):
                            s, d = slice((1 - a) * 64, (2 - a) * 64), slice(a * 64, a * 64 + 64)
                            sn = cst[s, C_SIN:C_SIN + P].unsqueeze(1).to_broadcast([64, HB, P])
                            op = dve.tensor_tensor(four(m2[d, n, :]), four(src[s, :]), sn, ALU.mult)
                        op.then_inc(g.rope_m, 1)
                    if j in (5, 6):
                        split_low(j - 5)
                maxima(0)
                recip(0)
                for b in range(B):
                    if b:
                        out_low(b - 1)
                    if b < B - 1:
                        maxima(b + 1)
                    split_low(b + 2)
                    if b:
                        add(b - 1)
                    if b < B - 1:
                        recip(b + 1)
                out_low(B - 1)
                add(B - 1)

        def g_pool(pool, g):
            sf = g.soft
            with pool.Fori(0, GROUPS) as i:
                for j, (t, half) in enumerate(G_TILES):
                    if not g.cross and t != 1:
                        n = ROPES[j] % 2
                        pool.wait_ge(g.rope_m, i * NR + ROPES[j] + 1)
                        pool.tensor_tensor(tile_dst(t, half), m1[:, n, :], m2[:, n, :], ALU.add)\
                            .then_inc(g.tile_done, 1)
                    if 4 <= j < 4 + NO:
                        split_out_lo(pool, i + g.slot, j - 4)
                for b in range(B):
                    n = b % 2
                    pool.wait_ge(sf.recip, i * B + b + 1)
                    pool.tensor_tensor(four(prob[:, n, :]), four(prob[:, n, :]),
                                       rsum[:, n, :].unsqueeze(2).to_broadcast([P, 4, P]), ALU.mult)\
                        .then_inc(sf.prob, 1)
                    if b < NT:
                        split_tile_lo(pool, i + (g.slot + 1), b)

        ctx_raw = qT[:, :, :].rearrange("p h t -> p (h t)").rearrange("p (b d) -> p b d", b=B)
        block = stack.enter_context(nc.Block())

        @block.sync
        def _(sp):
            sp.dma_start(cst[:, :], consts).then_inc(const_in, 16)
            for b in range(2):
                sp.dma_start(ctx_raw[:, b, :], ctx_in[b]).then_inc(ctx_loaded[b], 16)
            for b in range(B):
                sp.dma_start(x[:, b, :], x_in[b]).then_inc(x_loaded[b], 16)
            load_slot(sp, 0)
            for b in range(2, B):
                sp.dma_start(ctx_raw[:, b, :], ctx_in[b]).then_inc(ctx_loaded[b], 16)
            sp.dma_start(row[:, 0:D], rows[R_BO0:R_BO0 + D].partition_broadcast(P)).then_inc(row_in, 16)
            sp.dma_start(row[:, D:D + NE], rows[R_GATE:R_GATE + NE].partition_broadcast(P)).then_inc(row_in, 16)
            load_slot(sp, 1)
            with sp.Fori(SLOT_ATTN, SLOTS) as s:
                load_slot(sp, s)
            for b in range(B):
                sp.wait_ge(normed, NORMS[5] + b + 1)
                sp.dma_start(out[b], x[:, b, :]).then_inc(out_done, 16)
            sp.wait_ge(out_done, 16 * B)

        @block.tensor
        def _(pe):
            pe.wait_ge(const_in, 16)

            def ctx_turn(b):
                pe.wait_ge(c_exp, b + 1)
                if b >= 2:
                    pe.wait_ge(c_dve, b - 1)
                for c in range(NC):
                    cc = slice(c * P, (c + 1) * P)
                    pe.transpose(pT[b % 2][:, cc], prob[:, b % 2, cc], ident)
                    t = pe.transpose(pS[b % 2][:, cc], ctx_raw[:, b, cc], ident)
                t.then_inc(c_turned, 1)

            def ctx_kv(b):
                pe.wait_ge(c_dve, b + 1)
                if b:
                    pe.wait_ge(c_kvm, b)
                for c in range(NC):
                    cc = slice(c * P, (c + 1) * P)
                    mm = pe.matmul(pO[:, 0:P], sm[:, b % 2, cc], m1[:, b % 2, cc], start=(c == 0), stop=(c == NC - 1))
                mm.then_inc(c_kv, 1)

            for b in range(B):
                ctx_turn(b)
                if b:
                    ctx_kv(b - 1)
            ctx_kv(B - 1)

            for b in range(B):
                turn_pe(pe, 0, b)
            pe.wait_ge(t_lo, NT)
            pe.wait_ge(c_kvm, B)

            def l0_vturn(half):
                pe.wait_ge(a_free, half * 3 + 2)
                for j in range(4):
                    t = pe.transpose(pT[half][:, j * P:(j + 1) * P], VT[:, half, j * P:(j + 1) * P], ident)
                t.then_inc(l0_vturned, 1)

            for j, (t, half) in enumerate(L0_TILES):
                pe.wait_ge(xt_lo, TURNS[0] + HB * (half + 1) if j >= 2 else B)
                if j >= 2:
                    pe.wait_ge(a_free, j - 1)
                tile_product(pe, pA[j % 2], t, half, xTh, xTl).then_inc(a_ready, 1)
                if t == 2:
                    l0_vturn(half)
            pe.wait_ge(a_free, 6)
            for half in range(2):
                for j in range(4):
                    b = half * HB + j
                    mm = pe.matmul(pS[half][:, j * P:(j + 1) * P], qT[:, 0, b * P:(b + 1) * P],
                                   KT[:, b * P:(b + 1) * P], start=True, stop=True)
                    if b == 0:
                        mm.then_inc(t_used, 1)
                mm.then_inc(l0.scores, 1)
            pe.wait_ge(o_lo, NO)
            for half in range(2):
                pe.wait_ge(l0.prob, half + 1)
                pe.wait_ge(l0_vcopied, half + 1)
                for j in range(4):
                    t = pe.transpose(pT[half][:, j * P:(j + 1) * P], prob[:, half, j * P:(j + 1) * P], ident)
                t.then_inc(l0_pturned, 1)
            for half in range(2):
                pe.wait_ge(l0_pcopied, half + 1)
                if half:
                    pe.wait_ge(l0_olo, half)
                for j in range(4):
                    c = slice(j * P, (j + 1) * P)
                    mm = pe.matmul(pO[:, c], m1[:, half, c], sm[:, half, c], start=True, stop=True)
                mm.then_inc(l0_o, 1)
                pe.wait_ge(l0_olo, half + 1)
                for j in range(4):
                    b = half * HB + j
                    c = slice(j * P, (j + 1) * P)
                    if b >= 2:
                        pe.wait_ge(added, ADDS[0] + b - 1)
                    mm3(pe, pA[b % 2], OTh[:, c], OTl[:, c], woh[:, 0:D], wol[:, 0:D], True, True).then_inc(l0_y, 1)

            def x2_product(b):
                pe.wait_ge(x2_exp, b + 1)
                if b >= 2:
                    pe.wait_ge(x2_mul, 2 * (b - 1))
                pair = 2 + 2 * (b % 2)
                for c in range(NC):
                    o = ps[:, pair + c // 2, (c % 2) * (P + XH):(c % 2 + 1) * (P + XH)]
                    mm = pe.matmul(o, prob[:, b % 2, c * P:(c + 1) * P], kvm[:, b, :], start=True, stop=True)
                    if b == 0 and c == 0:
                        mm.then_inc(o_used, 1)
                mm.then_inc(x2_num, 1)

            def x2_turn(b):
                pe.wait_ge(x2_mul, 2 * (b + 1))
                if b >= 2:
                    pe.wait_ge(added, ADDS[1] + b - 1)
                for c in range(NC):
                    t = pe.transpose(ps[:, 6 + b % 2, c * P:(c + 1) * P], m2[:, b % 2, c * P:(c + 1) * P], ident)
                t.then_inc(x2_turned, 1)

            for b in range(B):
                x2_product(b)
                if b:
                    x2_turn(b - 1)
            x2_turn(B - 1)

            for b in range(B):
                turn_pe(pe, 2, b)
            pe.wait_ge(t_lo, 2 * NT)
            pe.wait_ge(o_lo, 2 * NO)

            def f_up(b):
                pe.wait_ge(xt_lo, TURNS[2] + b + 1)
                if b >= 2:
                    pe.wait_ge(added, ADDS[2] + b - 1)
                for c in range(NC):
                    xc = slice(b * P, (b + 1) * P)
                    w = slice(c * TILES * P, c * TILES * P + LR + NE0)
                    mm = mm3(pe, pT[b % 2][:, 0:LR + NE0], xTh[:, c, xc], xTl[:, c, xc], wth[:, w], wtl[:, w],
                             c == 0, c == NC - 1)
                mm.then_inc(f_h, 1)
                for c in range(NC):
                    w = slice(c * D, (c + 1) * D)
                    mm3(pe, pS[b % 2], xTh[:, c, xc], xTl[:, c, xc], woh[:, w], wol[:, w], c == 0, False)

            def f_turn(b):
                pe.wait_ge(f_hm, b + 1)
                if b:
                    pe.wait_ge(f_lo, b)
                pe.transpose(pO[0:LR, 0:P], m1[:, b % 2, 0:LR], ident).then_inc(f_turned, 1)

            def f_down(b):
                pe.wait_ge(f_lo, b + 1)
                w = slice(P, P + D)
                mm3(pe, pS[b % 2], PTh[0:LR, 0:P], PTl[0:LR, 0:P], wth[0:LR, w], wtl[0:LR, w], False, True)\
                    .then_inc(f_y, 1)

            f_up(0)
            for b in range(B):
                if b < B - 1:
                    f_up(b + 1)
                f_turn(b)
                f_down(b)

            for g in (attn, xattn):
                for b in range(B):
                    turn_pe(pe, g.k, b, t_used if g is attn and b == 0 else None)
                g_pe(pe, g)

            for b in range(B):
                turn_pe(pe, 5, b, o_used if b == 0 else None)
            pe.wait_ge(t_lo, SLOTS * NT)
            pe.wait_ge(o_lo, SLOTS * NO)

            def e_up(b):
                pe.wait_ge(xt_lo, TURNS[5] + b + 1)
                if b >= 2:
                    pe.wait_ge(e_hw, b - 1)
                xc = slice(b * P, (b + 1) * P)
                for o, w0, n in ((pT[b % 2][:, 0:NE], D, NE), (pS[b % 2], 0, D)):
                    for c in range(NC):
                        w = slice(c * TILES * P + w0, c * TILES * P + w0 + n)
                        mm = mm3(pe, o, xTh[:, c, xc], xTl[:, c, xc], wth[:, w], wtl[:, w], c == 0, c == NC - 1)
                mm.then_inc(e_h, 1)

            def e_down(b):
                pe.wait_ge(e_hw, b + 1)
                if b:
                    pe.wait_ge(e_lo, b)
                for c in range(NC):
                    t = pe.transpose(pO[:, c * P:(c + 1) * P], m1[:, b % 2, c * P:(c + 1) * P], ident)
                t.then_inc(e_turned, 1)
                pe.wait_ge(e_lo, b + 1)
                if b:
                    pe.wait_ge(added, ADDS[5] + b)
                for c in range(NC):
                    cc, w = slice(c * P, (c + 1) * P), slice(c * D, (c + 1) * D)
                    mm = mm3(pe, pY, PTh[:, cc], PTl[:, cc], woh[:, w], wol[:, w], c == 0, c == NC - 1)
                mm.then_inc(e_y, 1)

            e_up(0)
            for b in range(B):
                if b < B - 1:
                    e_up(b + 1)
                e_down(b)

        @block.scalar
        def _(act):
            def ctx_exp(b):
                act.wait_ge(c_max, b + 1)
                if b >= 2:
                    act.wait_ge(c_turned, b - 1)
                act.activation(prob[:, b % 2, :], ctx_raw[:, b, :], ACT.Exp, bias=cmax[:, b:b + 1],
                               accum_out=csum[:, b:b + 1]).then_inc(c_exp, 1)

            ctx_exp(0)
            for b in range(B):
                if b < B - 1:
                    ctx_exp(b + 1)
                act.wait_ge(c_turned, b + 1)
                if b >= 2:
                    act.wait_ge(c_kv, b - 1)
                act.activation(sm[:, b % 2, :], pT[b % 2], ACT.Copy)
                act.activation(cTh[:, :, b * P:(b + 1) * P], four(pS[b % 2]), ACT.Copy).then_inc(c_act, 1)
                if b < NT:
                    split_tile_hi(act, 0, b)
            for k in range(NO):
                split_out_hi(act, 0, k)
            for b in range(B):
                turn_act(act, 0, b)
            for j, (t, half) in enumerate(L0_TILES):
                act.wait_ge(a_ready, j + 1)
                act.activation(tile_dst(t, half), pA[j % 2], ACT.Identity, bias=tbias[:, t:t + 1]).then_inc(a_free, 1)
                if t == 2:
                    act.wait_ge(l0_vturned, half + 1)
                    act.activation(m1[:, half, :], pT[half], ACT.Copy).then_inc(l0_vcopied, 1)
            for half in range(2):
                soft_exp(act, l0, half, half, False)
            for k in range(NT):
                split_tile_hi(act, 1, k)
            for half in range(2):
                act.wait_ge(l0_pturned, half + 1)
                act.activation(sm[:, half, :], pT[half], ACT.Copy).then_inc(l0_pcopied, 1)
            for half in range(2):
                act.wait_ge(l0_o, half + 1)
                if half:
                    act.wait_ge(l0_y, HB)
                act.activation(OTh[:, :], pO, ACT.Copy).then_inc(l0_ohi, 1)
            act.wait_ge(res_ready, BIASES[0] + B)
            act.dma_start(row[:, 0:D], rows[R_B1:R_B1 + D].partition_broadcast(P)).then_inc(row_in, 16)
            for b in range(B):
                act.wait_ge(normed, NORMS[0] + b + 1)
                if b >= 2:
                    act.wait_ge(x2_num, b - 1)
                act.activation(prob[:, b % 2, :], x[:, b, :], ACT.Exp).then_inc(x2_exp, 1)
                if 2 <= b < 2 + NO:
                    split_out_hi(act, 1, b - 2)
            for b in range(B):
                turn_act(act, 2, b)
            for b in range(B):
                act.wait_ge(f_turned, b + 1)
                act.activation(PTh[0:LR, 0:P], pO[0:LR, 0:P], ACT.Copy).then_inc(f_hi, 1)
            act.wait_ge(res_ready, BIASES[2] + B)
            act.dma_start(row[:, 0:D], rows[R_BO5:R_BO5 + D].partition_broadcast(P)).then_inc(row_in, 16)
            for k in range(NT):
                split_tile_hi(act, SLOT_ATTN, k)
            for g in (attn, xattn):
                for b in range(B):
                    turn_act(act, g.k, b)
                g_act(act, g)
            for k in range(NO):
                split_out_hi(act, SLOT_MOE, k)
            for b in range(B):
                turn_act(act, 5, b)

            def e_exps(b):
                act.wait_ge(e_neg, b + 1)
                act.activation(g8[:, b % 2, :], pT[b % 2][:, 0:NE], ACT.Exp, bias=s1[:, b % 2, 0:1]).then_inc(e_exp, 1)

            e_exps(0)
            for b in range(B):
                if b < B - 1:
                    e_exps(b + 1)
                act.wait_ge(e_turned, b + 1)
                act.activation(PTh[:, :], pO, ACT.Copy).then_inc(e_hi, 1)

        @block.vector
        def _(dve):
            dve.wait_ge(const_in, 16)
            for b in range(B):
                op = dve.tensor_copy(kvm[:, b, P:P + XH], cst[:, C_GROUP:C_GROUP + XH])
            op.then_inc(c_set, 1)

            def ctx_max(b):
                dve.wait_ge(ctx_loaded[b], 16)
                dve.tensor_reduce(cmax[:, b:b + 1], ctx_raw[:, b, :], AX.X, ALU.max, negate=True).then_inc(c_max, 1)

            def ctx_kvm(b):
                dve.wait_ge(c_exp, b + 1)
                dve.reciprocal(crs[:, b:b + 1], csum[:, b:b + 1]).then_inc(c_rs, 1)
                dve.wait_ge(c_rs, b + 1)
                dve.wait_ge(c_kv, b + 1)
                dve.scalar_tensor_tensor(kvm[:, b, 0:P], pO[:, 0:P], crs[:, b:b + 1], cst[:, C_BLOCK:C_BLOCK + P],
                                         ALU.mult, ALU.mult).then_inc(c_kvm, 1)

            ctx_max(0)
            for b in range(B):
                if b < B - 1:
                    ctx_max(b + 1)
                dve.wait_ge(c_act, b + 1)
                if b >= 2:
                    dve.wait_ge(c_kv, b - 1)
                dve.tensor_copy(m1[:, b % 2, :], pS[b % 2])
                dve.tensor_tensor(cTl[:, :, b * P:(b + 1) * P], four(pS[b % 2]),
                                  cTh[:, :, b * P:(b + 1) * P].bitcast(F32), ALU.subtract).then_inc(c_dve, 1)
                if b:
                    ctx_kvm(b - 1)
            ctx_kvm(B - 1)
            for b in range(B):
                turn_dve(dve, 0, b)
            for half in range(2):
                soft_max(dve, l0, half, half, False)
            for half in range(2):
                soft_recip(dve, l0, half, half)
            for half in range(2):
                dve.wait_ge(l0_ohi, half + 1)
                dve.tensor_tensor(OTl[:, :], pO, OTh[:, :].bitcast(F32), ALU.subtract).then_inc(l0_olo, 1)
                for j in range(HB):
                    b = half * HB + j
                    dve.wait_ge(l0_y, b + 1)
                    dve.wait_ge(res_ready, BIASES[0] + b + 1)
                    dve.tensor_tensor(x[:, b, :], pA[b % 2], x[:, b, :], ALU.add).then_inc(added, 1)
                    norm_stats(dve, 0, b)
                if half:
                    norm_apply(dve, 0, 0)
            norm_apply(dve, 0, 1)
            for b in range(B):
                pair = 2 + 2 * (b % 2)
                dve.wait_ge(x2_num, b + 1)
                both = ps[:, pair:pair + 2, 0:2 * (P + XH)].rearrange("p k (c w) -> p k c w", c=2)
                dve.reciprocal(rden[:, b % 2, :, :].rearrange("p (k c) g -> p k c g", k=2), both[:, :, :, P:P + XH])\
                    .then_inc(x2_rden, 1)
                dve.wait_ge(x2_rden, b + 1)
                if b >= 2:
                    dve.wait_ge(x2_turned, b - 1)
                for k in range(2):
                    o = m2[:, b % 2, 2 * k * P:2 * (k + 1) * P].rearrange("p (c g e) -> p c g e", c=2, g=XH)
                    i0 = both[:, k, :, 0:P].rearrange("p c (g e) -> p c g e", g=XH)
                    r = rden[:, b % 2, 2 * k:2 * k + 2, :].unsqueeze(3).to_broadcast([P, 2, XH, XD])
                    dve.tensor_tensor(o, i0, r, ALU.mult).then_inc(x2_mul, 1)
                dve.wait_ge(x2_turned, b + 1)
                dve.tensor_tensor(x[:, b, :], ps[:, 6 + b % 2, :], x[:, b, :], ALU.add).then_inc(added, 1)
                norm_stats(dve, 1, b)
                if b == 5:
                    norm_apply(dve, 1, 0)
            norm_apply(dve, 1, 1)
            for b in range(B):
                turn_dve(dve, 2, b)
            op = dve.memset(g8[:, :, NE0:8], NEG).then_inc(c_set, 1)
            dve.wait_ge(row_in, 32)
            dve.wait_ge(c_set, 2)

            def f_choose(b):
                n = b % 2
                dve.wait_ge(f_h, b + 1)
                dve.tensor_tensor(g8[:, n, 0:NE0], pT[n][:, LR:LR + NE0], row[:, D:D + NE0], ALU.add)\
                    .then_inc(f_step, 1)
                dve.wait_ge(f_step, 4 * b + 1)
                dve.max(t8[:, n, :], g8[:, n, :]).then_inc(f_step, 1)
                dve.wait_ge(f_step, 4 * b + 2)
                dve.max_index(i8[:, n, :], t8[:, n, :], g8[:, n, :]).then_inc(f_step, 1)
                dve.wait_ge(f_step, 4 * b + 3)
                dve.tensor_copy(f8[:, n, 0:1], i8[:, n, 0:1]).then_inc(f_step, 1)
                dve.wait_ge(f_step, 4 * b + 4)
                dve.scalar_tensor_tensor(m1[:, n, 0:LR], cst[:, C_SEG:C_SEG + LR], f8[:, n, 0:1], pT[n][:, 0:LR],
                                         ALU.is_le, ALU.mult).then_inc(f_hm, 1)

            f_choose(0)
            for b in range(B):
                if b < B - 1:
                    f_choose(b + 1)
                dve.wait_ge(f_hi, b + 1)
                dve.tensor_tensor(PTl[0:LR, 0:P], pO[0:LR, 0:P], PTh[0:LR, 0:P].bitcast(F32), ALU.subtract)\
                    .then_inc(f_lo, 1)
                dve.wait_ge(f_y, b + 1)
                dve.wait_ge(res_ready, BIASES[2] + b + 1)
                dve.tensor_tensor(x[:, b, :], pS[b % 2], x[:, b, :], ALU.add).then_inc(added, 1)
                norm_stats(dve, 2, b)
                if b == 5:
                    norm_apply(dve, 2, 0)
            norm_apply(dve, 2, 1)
            for g in (attn, xattn):
                for b in range(B):
                    turn_dve(dve, g.k, b)
                g_dve(dve, g)
                dve.wait_ge(g.y_added, GROUPS * B + 1)
                for b in range(B):
                    norm_stats(dve, g.k, b, g.y_added)
                    if b == 5:
                        norm_apply(dve, g.k, 0)
                norm_apply(dve, g.k, 1)
            for b in range(B):
                turn_dve(dve, 5, b)

            def e_choose(b):
                n = b % 2
                dve.wait_ge(e_h, b + 1)
                dve.max(t8[:, n, :], pT[n][:, 0:NE]).then_inc(e_step, 1)
                dve.wait_ge(e_step, 9 * b + 1)
                dve.tensor_scalar(s1[:, n, 0:1], t8[:, n, 0:1], -1.0, None, ALU.mult).then_inc(e_neg, 1)
                dve.wait_ge(e_exp, b + 1)
                dve.max(e8[:, n, :], g8[:, n, :]).then_inc(e_step, 1)
                dve.wait_ge(e_step, 9 * b + 2)
                dve.max_index(i8[:, n, :], e8[:, n, :], g8[:, n, :]).then_inc(e_step, 1)
                dve.tensor_tensor(s1[:, n, 1:2], e8[:, n, 0:1], e8[:, n, 1:2], ALU.add).then_inc(e_step, 1)
                dve.wait_ge(e_step, 9 * b + 4)
                dve.reciprocal(s1[:, n, 2:3], s1[:, n, 1:2]).then_inc(e_step, 1)
                dve.tensor_copy(f8[:, n, 0:2], i8[:, n, 0:2]).then_inc(e_step, 1)
                dve.wait_ge(e_step, 9 * b + 5)
                dve.tensor_scalar(f8[:, n, 2:4], e8[:, n, 0:2], s1[:, n, 2:3], None, ALU.mult).then_inc(e_step, 1)
                dve.wait_ge(e_step, 9 * b + 7)
                for r in range(2):
                    op = dve.tensor_scalar(w8[:, n, r, :], cst[:, C_IOTA:C_IOTA + NE], f8[:, n, r:r + 1],
                                           f8[:, n, 2 + r:3 + r], ALU.is_equal, ALU.mult)
                op.then_inc(e_step, 1)
                dve.wait_ge(e_step, 9 * b + 8)
                dve.tensor_tensor(t8[:, n, :], w8[:, n, 0, :], w8[:, n, 1, :], ALU.add).then_inc(e_step, 1)
                dve.wait_ge(e_step, 9 * b + 9)
                if b >= 2:
                    dve.wait_ge(e_turned, b - 1)
                dve.tensor_tensor(m1[:, n, :].rearrange("p (e r) -> p e r", e=NE),
                                  pS[n].rearrange("p (e r) -> p e r", e=NE),
                                  t8[:, n, :].unsqueeze(2).to_broadcast([P, NE, D // NE]), ALU.mult).then_inc(e_hw, 1)

            e_choose(0)
            for b in range(B):
                if b < B - 1:
                    e_choose(b + 1)
                dve.wait_ge(e_hi, b + 1)
                dve.tensor_tensor(PTl[:, :], pO, PTh[:, :].bitcast(F32), ALU.subtract).then_inc(e_lo, 1)
                dve.wait_ge(e_y, b + 1)
                dve.tensor_tensor(x[:, b, :], pY, x[:, b, :], ALU.add).then_inc(added, 1)
                norm_stats(dve, 5, b)
                if b == 5:
                    norm_apply(dve, 5, 0)
            norm_apply(dve, 5, 1)

        @block.gpsimd
        def _(pool):
            pool.wait_ge(const_in, 16)
            for k in range(NT):
                split_tile_lo(pool, 0, k)
            for k in range(NO):
                split_out_lo(pool, 0, k)
            for b in range(B):
                residual_bias(pool, 0, b, 2)
            for half in range(2):
                soft_norm(pool, l0, half, half)
            for k in range(NT):
                split_tile_lo(pool, 1, k)
            norm_pow(pool, 0, 0)
            norm_pow(pool, 0, 1)
            for k in range(NO):
                split_out_lo(pool, 1, k)
            norm_pow(pool, 1, 0)
            norm_pow(pool, 1, 1)
            for b in range(B):
                residual_bias(pool, 2, b, 3)
            norm_pow(pool, 2, 0)
            norm_pow(pool, 2, 1)
            for k in range(NT):
                split_tile_lo(pool, SLOT_ATTN, k)
            g_pool(pool, attn)
            norm_pow(pool, 3, 0)
            norm_pow(pool, 3, 1)
            for b in range(B):
                residual_bias(pool, 4, b, 4)
            g_pool(pool, xattn)
            norm_pow(pool, 4, 0)
            norm_pow(pool, 4, 1)
            for k in range(NO):
                split_out_lo(pool, SLOT_MOE, k)
            norm_pow(pool, 5, 0)
            norm_pow(pool, 5, 1)


def constants():
    import numpy as np

    c = np.zeros((P, CONSTS), np.float32)
    c[:, C_ID:C_ID + P] = np.eye(P)
    inv = 1.0 / 500000.0 ** (np.arange(0, HD, 2, dtype=np.float64) / HD)
    wavelen = 2.0 * np.pi / inv
    smooth = (1024 / wavelen - 1.0) / (4.0 - 1.0)
    scaled = np.where(wavelen > 1024 / 1.0, inv / 8.0, inv)
    mid = (wavelen <= 1024 / 1.0) & (wavelen >= 1024 / 4.0)
    scaled = np.where(mid, (1 - smooth) * inv / 8.0 + smooth * inv, scaled).astype(np.float32)
    emb = np.arange(P, dtype=np.float32)[:, None] * scaled[None, :]
    cos, sin = np.cos(emb).T, np.sin(emb).T
    c[:, C_COS:C_COS + P] = np.concatenate([cos, cos])
    c[:, C_SIN:C_SIN + P] = np.concatenate([sin, -sin])
    c[:, C_CAUSAL:C_CAUSAL + P] = np.where(np.tril(np.ones((P, P))) > 0, 0.0, NEG)
    head = np.arange(P) // XD
    c[:, C_BLOCK:C_BLOCK + P] = head[:, None] == head[None, :]
    c[:, C_GROUP:C_GROUP + XH] = head[:, None] == np.arange(XH)[None, :]
    c[:, C_SEG:C_SEG + LR] = np.searchsorted([8, 16, 32, 64], np.arange(LR), side="right")
    c[:, C_IOTA:C_IOTA + NE] = np.arange(NE)
    c[:, C_POW:C_POW + 8] = -0.5
    return c


def chunks(w):
    return w.reshape(-1, P, w.shape[1]).transpose(1, 0, 2)


def layout(a):
    import numpy as np

    wt = np.zeros((SLOTS, P, WTB), np.float32)
    wo = np.zeros((SLOTS, P, WO), np.float32)
    tiles = wt[:, :, :WT].reshape(SLOTS, P, NC, TILES * P)

    def columns(w, n):
        return w[:, n * P:(n + 1) * P]

    w, bq = a["L0_attn_Wqkv"], a["L0_attn_bqkv"]
    for t, n in enumerate((1, 2, 0)):
        tiles[0, :, :, t * P:(t + 1) * P] = chunks(columns(w, n))
        wt[0, :, WT + t] = bq[n * P:(n + 1) * P]
    wo[0, :, :D] = a["L0_attn_Wo"]
    tiles[1, :, :, :LR] = chunks(a["L0_ffn_A"].T)
    tiles[1, :, :, LR:LR + NE0] = chunks(a["L0_ffn_gate_w"].T)
    tiles[1, :LR, 0, P:P + D] = a["L0_ffn_B"].T
    wo[1] = chunks(a["L0_ffn_W"].T).reshape(P, WO)
    for g in range(GROUPS):
        s = SLOT_ATTN + g
        for t, w in enumerate([columns(a["L1_attn_wk"], g), columns(a["L1_attn_wv"], g)]
                              + [columns(a["L1_attn_wq"], REP * g + h) for h in range(REP)]):
            tiles[s, :, :, t * P:(t + 1) * P] = chunks(w)
        wo[s] = chunks(a["L1_attn_wo"][g * D:(g + 1) * D]).reshape(P, WO)
        s = SLOT_XATTN + g
        for t, (w, bias, n) in enumerate([(a["L1_xattn_Wkv"], a["L1_xattn_bkv"], g),
                                          (a["L1_xattn_Wkv"], a["L1_xattn_bkv"], GROUPS + g)]
                                         + [(a["L1_xattn_Wq"], a["L1_xattn_bq"], REP * g + h) for h in range(REP)]):
            tiles[s, :, :, t * P:(t + 1) * P] = chunks(columns(w, n))
            wt[s, :, WT + t] = bias[n * P:(n + 1) * P]
        wo[s] = chunks(a["L1_xattn_Wo"][g * D:(g + 1) * D]).reshape(P, WO)
    s = SLOT_MOE
    tiles[s, :, :, :D] = chunks(a["L1_ffn_lora_A"].reshape(D, D).T)
    tiles[s, :, :, D:D + NE] = chunks(a["L1_ffn_gate_w"].T)
    wo[s] = chunks(a["L1_ffn_lora_B"].transpose(0, 2, 1).reshape(D, D)).reshape(P, WO)
    rows = np.zeros((ROWS,), np.float32)
    rows[R_BO0:R_BO0 + D] = a["L0_attn_bo"]
    rows[R_B1:R_B1 + D] = a["L0_ffn_b"]
    rows[R_BO5:R_BO5 + D] = a["L1_xattn_bo"]
    rows[R_GATE:R_GATE + NE0] = a["L0_ffn_gate_b"]
    return {"x": a["x"], "ctx": a["ctx_4096"], "w_tile": wt, "w_out": wo, "consts": constants(), "rows": rows}


def kernel(**inputs):
    import numpy as np
    import concourse.bacc as bacc
    from concourse.bass_utils import run_bass_kernel_spmd

    arrays = {"in_" + k: np.ascontiguousarray(v) for k, v in layout({k: np.asarray(v) for k, v in inputs.items()}).items()}
    nc = bacc.Bacc("TRN2", target_bir_lowering=False, num_devices=1)
    aps = [nc.dram_tensor(n, a.shape, F32, kind="ExternalInput").ap() for n, a in arrays.items()]
    out = nc.dram_tensor("out", [B, P, D], F32, kind="ExternalOutput").ap()
    build(nc, *aps, out)
    r = run_bass_kernel_spmd(nc, [arrays], core_ids=[0])
    return r.results[0]["out"]
```

```python
from contextlib import ExitStack

import concourse.bass as bass
from concourse import mybir

F32 = mybir.dt.float32
F32R = mybir.dt.float32r
U32 = mybir.dt.uint32
ALU = mybir.AluOpType
ACT = mybir.ActivationFunctionType
AX = mybir.AxisListType

P = 128
B = 8
D = 512
NC = D // P
TOK = B * P
HALF = TOK // 2
HB = B // 2
HD = 128
GROUPS = 8
REP = 4
TILES = 2 + REP
WT = TILES * D
WO = NC * D
NT, NO = WT // D, WO // D
RING = 5
K_TILE, V_TILE = 0, NT - 1
SLOT_FFN0, SLOT_ATTN, SLOT_XATTN, SLOT_MOE = 1, 2, 2 + GROUPS, 2 + 2 * GROUPS
SLOTS = SLOT_MOE + 1
XH, XD = 8, 16
LR, NE0 = 64, 4
NE = 8
SCALE = float(HD) ** -0.5
EPS = 1e-5
NEG = -1e30
C_ID, C_COS, C_SIN, C_CAUSAL, C_BLOCK, C_GROUP, C_SEG, C_IOTA, C_POW = 0, 128, 256, 384, 512, 640, 648, 712, 720
CONSTS = 728
R_BO0, R_B1, R_BO5, R_GATE = 0, D, 2 * D, 3 * D
ROWS = 3 * D + 8


def build(nc, x_in, ctx_in, w_tile, w_out, biases, consts, rows, out):
    with ExitStack() as stack:
        def sb(name, shape, dt=F32):
            return stack.enter_context(nc.sbuf_tensor(name, shape, dt))

        def sem(name):
            return stack.enter_context(nc.semaphore(name))

        x = sb("x", [P, B, D])
        xTh, xTl = sb("xTh", [P, NC, TOK], F32R), sb("xTl", [P, NC, TOK], F32R)
        cTh, cTl = sb("cTh", [P, NC, TOK], F32R), sb("cTl", [P, NC, TOK], F32R)
        raw = sb("raw", [P, RING, D])
        wth, wtl = sb("wth", [P, WT], F32R), sb("wtl", [P, WT], F32R)
        woh, wol = sb("woh", [P, WO], F32R), sb("wol", [P, WO], F32R)
        tbias = sb("tbias", [P, SLOTS * 8])
        qT = sb("qT", [P, REP, TOK])
        KT = sb("KT", [P, TOK])
        VT = sb("VT", [P, 2, HALF])
        Vh, Vl = sb("Vh", [P, B, HD], F32R), sb("Vl", [P, B, HD], F32R)
        prob = sb("prob", [P, 2, D])
        sm = sb("sm", [P, 2, D])
        m1, m2 = sb("m1", [P, 2, D]), sb("m2", [P, 2, D])
        PTh, PTl = sb("PTh", [P, D], F32R), sb("PTl", [P, D], F32R)
        OTh, OTl = sb("OTh", [P, D], F32R), sb("OTl", [P, D], F32R)
        kvm = sb("kvm", [P, B, P + XH])
        cst = sb("cst", [P, CONSTS])
        row = sb("row", [P, D + NE])
        stats = sb("stats", [P, B, 6])
        mv = sb("mv", [P, B, 2])
        vare = sb("vare", [P, B])
        rstd = sb("rstd", [P, B])
        nmax = sb("nmax", [P, 2, REP])
        nbias = sb("nbias", [P, 2, REP])
        esum = sb("esum", [P, 2, REP])
        rsum = sb("rsum", [P, 2, REP])
        cmax, csum, crs = sb("cmax", [P, B]), sb("csum", [P, B]), sb("crs", [P, B])
        rden = sb("rden", [P, 2, NC, XH])
        logit, below = sb("logit", [P, HB, NE]), sb("below", [P, HB, NE])
        first, second = sb("first", [P, HB, NE]), sb("second", [P, HB, NE])
        weight = sb("weight", [P, 2, HB, NE])
        best = sb("best", [P, 6, HB])
        keep = sb("keep", [P, HB, LR])

        ps = stack.enter_context(nc.psum_tensor("ps", [P, 8, D], F32))
        pA = [ps[:, 0, :], ps[:, 1, :]]
        pS = [ps[:, 2, :], ps[:, 3, :]]
        pT = [ps[:, 4, :], ps[:, 5, :]]
        pO, pY = ps[:, 6, :], ps[:, 7, :]

        ident = cst[:, C_ID:C_ID + P]
        cosT = cst[:, C_COS:C_COS + P].unsqueeze(1).to_broadcast([P, HB, P])
        causal = cst[:, C_CAUSAL:C_CAUSAL + P].unsqueeze(1).to_broadcast([P, REP, P])

        def four(ap):
            return ap.rearrange("p (a b) -> p a b", a=4)

        const_in, row_in, bias_in = sem("const_in"), sem("row_in"), sem("bias_in")
        x_loaded = [sem(f"x_loaded{b}") for b in range(B)]
        ctx_loaded = [sem(f"ctx_loaded{b}") for b in range(B)]
        raw_in = [sem(f"raw_in{p}") for p in range(RING)]
        t_hi, t_lo, t_used = sem("t_hi"), sem("t_lo"), sem("t_used")
        o_hi, o_lo, o_used = sem("o_hi"), sem("o_lo"), sem("o_used")
        c_set, c_max, c_exp, c_turned = sem("c_set"), sem("c_max"), sem("c_exp"), sem("c_turned")
        c_act, c_dve, c_kv, c_rs, c_kvm = sem("c_act"), sem("c_dve"), sem("c_kv"), sem("c_rs"), sem("c_kvm")
        added, stat_ready, mv_ready, var_ready = sem("added"), sem("stat_ready"), sem("mv_ready"), sem("var_ready")
        rstd_ready, normed, xt_turned = sem("rstd_ready"), sem("normed"), sem("xt_turned")
        xt_hi, xt_lo, res_ready = sem("xt_hi"), sem("xt_lo"), sem("res_ready")
        NORMS = [B * k for k in range(6)]
        HALVES = [2 * k for k in range(6)]
        TURNS = {0: 0, 2: B, 3: 2 * B, 4: 3 * B, 5: 4 * B}
        ADDS = {0: 0, 1: B, 2: 2 * B, 5: 3 * B}
        BIASES = {0: 0, 2: B, 4: 2 * B}
        out_done = sem("out_done")

        def load_tile_chunk(sp, s, k):
            sp.dma_start(raw[:, (k + NO) % RING, :], w_tile[bass.ds(s, 1), k].rearrange("a p n -> p (a n)"))\
                .then_inc(raw_in[(k + NO) % RING], 16)

        def load_out_chunk(sp, s, k):
            sp.dma_start(raw[:, k, :], w_out[bass.ds(s, 1), k].rearrange("a p n -> p (a n)")).then_inc(raw_in[k], 16)

        def load_out_part(sp, s):
            for k in range(NO):
                sp.wait_ge(t_lo, s * NT + k + 2)
                load_out_chunk(sp, s, k)

        def load_next_tile_part(sp, s):
            for k in range(NT):
                if k == 0:
                    sp.wait_ge(t_lo, s * NT + NT)
                elif k < NT - 1:
                    sp.wait_ge(o_lo, s * NO + k)
                else:
                    sp.wait_ge(t_lo, s * NT + NT + 1)
                load_tile_chunk(sp, s + 1, k)

        def split_tile_hi(act, s, k, used=None):
            p = (k + NO) % RING
            act.wait_ge(raw_in[p], s * 32 + (32 if k == NT - 1 else 16))
            if used is not None:
                act.wait_ge(*used)
            act.activation(wth[:, k * D:(k + 1) * D], raw[:, p, :], ACT.Copy).then_inc(t_hi, 1)

        def split_tile_lo(pool, s, k):
            c = slice(k * D, (k + 1) * D)
            pool.wait_ge(t_hi, s * NT + k + 1)
            pool.tensor_tensor(wtl[:, c], raw[:, (k + NO) % RING, :], wth[:, c].bitcast(F32), ALU.subtract)\
                .then_inc(t_lo, 1)

        def split_out_hi(act, s, k):
            act.wait_ge(raw_in[k], s * 32 + 32)
            if k == 0 and not (isinstance(s, int) and s == 0):
                act.wait_ge(o_used, s)
            act.activation(woh[:, k * D:(k + 1) * D], raw[:, k, :], ACT.Copy).then_inc(o_hi, 1)

        def split_out_lo(eng, s, k):
            c = slice(k * D, (k + 1) * D)
            eng.wait_ge(o_hi, s * NO + k + 1)
            eng.tensor_tensor(wol[:, c], raw[:, k, :], woh[:, c].bitcast(F32), ALU.subtract).then_inc(o_lo, 1)

        def mm3(pe, o, wh, wl, xh, xl, first, last, before=None):
            mm = pe.matmul(o, wl, xh, start=first, stop=False)
            if before is not None:
                mm.then_inc(before, 1)
            pe.matmul(o, wh, xl, start=False, stop=False)
            return pe.matmul(o, wh, xh, start=False, stop=last)

        def wt_tile(w, c, t):
            return w[:, t * D + c * P:t * D + (c + 1) * P]

        def tile_product(pe, o, t, half, src_h, src_l, before=None):
            cols = slice(half * HALF, (half + 1) * HALF)
            for c in range(NC):
                mm = mm3(pe, o, wt_tile(wth, c, t), wt_tile(wtl, c, t), src_h[:, c, cols], src_l[:, c, cols],
                         c == 0, c == NC - 1, before if c == 0 else None)
            return mm

        def turn_pe(pe, k, b, before=None):
            if k == 0:
                pe.wait_ge(x_loaded[b], 16)
            else:
                pe.wait_ge(normed, NORMS[k - 1] + b + 1)
            if b >= 2:
                pe.wait_ge(xt_lo, TURNS[k] + b - 1)
            for c in range(NC):
                t = pe.transpose(pA[b % 2][:, c * P:(c + 1) * P], x[:, b, c * P:(c + 1) * P], ident)
                if c == 0 and before is not None:
                    t.then_inc(before, 1)
            t.then_inc(xt_turned, 1)

        def turn_act(act, k, b):
            act.wait_ge(xt_turned, TURNS[k] + b + 1)
            act.activation(xTh[:, :, b * P:(b + 1) * P], four(pA[b % 2]), ACT.Copy).then_inc(xt_hi, 1)

        def turn_dve(dve, k, b):
            dve.wait_ge(xt_hi, TURNS[k] + b + 1)
            dve.tensor_tensor(xTl[:, :, b * P:(b + 1) * P], four(pA[b % 2]),
                              xTh[:, :, b * P:(b + 1) * P].bitcast(F32), ALU.subtract).then_inc(xt_lo, 1)

        def residual_bias(pool, k, b, loads):
            if b == 0:
                pool.wait_ge(row_in, 16 * loads)
            pool.wait_ge(xt_turned, TURNS[k] + b + 1)
            pool.tensor_tensor(x[:, b, :], x[:, b, :], row[:, 0:D], ALU.add).then_inc(res_ready, 1)

        def norm_stats(dve, k, b, summed=None):
            if summed is None:
                dve.wait_ge(added, ADDS[k] + b + 1)
            dve.bn_stats(stats[:, b, :], x[:, b, :]).then_inc(stat_ready, 1)
            dve.wait_ge(stat_ready, NORMS[k] + b + 1)
            dve.bn_aggr(mv[:, b, :], stats[:, b, :]).then_inc(mv_ready, 1)
            if b % HB == HB - 1:
                h = slice(b - HB + 1, b + 1)
                dve.wait_ge(mv_ready, NORMS[k] + b + 1)
                dve.tensor_scalar(vare[:, h], mv[:, h, 1], EPS, None, ALU.add).then_inc(var_ready, 1)

        def norm_pow(pool, k, half):
            h = slice(half * HB, (half + 1) * HB)
            pool.wait_ge(var_ready, HALVES[k] + half + 1)
            pool.tensor_tensor(rstd[:, h], vare[:, h], cst[:, C_POW:C_POW + HB], ALU.pow).then_inc(rstd_ready, 1)

        def norm_apply(dve, k, half):
            dve.wait_ge(rstd_ready, HALVES[k] + half + 1)
            for b in range(half * HB, (half + 1) * HB):
                dve.tensor_scalar(x[:, b, :], x[:, b, :], mv[:, b, 0:1], rstd[:, b:b + 1], ALU.subtract, ALU.mult)\
                    .then_inc(normed, 1)

        class Softmax:
            def __init__(self, name):
                self.scores = sem(name + "_scores")
                self.masked = sem(name + "_masked") if name == "ga" else None
                self.max = sem(name + "_max")
                self.bias = sem(name + "_bias")
                self.exp = sem(name + "_exp")
                self.recip = sem(name + "_recip")
                self.prob = sem(name + "_prob")

        def soft_max(dve, sf, u, n, mask, s_free=None):
            dve.wait_ge(sf.scores, u + 1)
            src = four(pS[n])
            if mask:
                dve.tensor_tensor(four(sm[:, n, :]), src, causal, ALU.add).then_inc(sf.masked, 1)
                dve.wait_ge(sf.masked, u + 1)
                src = four(sm[:, n, :])
            dve.tensor_reduce(nmax[:, n, :], src, AX.X, ALU.max, negate=True).then_inc(sf.max, 1)
            dve.wait_ge(sf.max, u + 1)
            dve.tensor_scalar(nbias[:, n, :], nmax[:, n, :], SCALE, None, ALU.mult).then_inc(sf.bias, 1)

        def soft_exp(act, sf, u, n, mask):
            act.wait_ge(sf.bias, u + 1)
            for h in range(4):
                src = (sm[:, n, :] if mask else pS[n])[:, h * P:(h + 1) * P]
                a = act.activation(prob[:, n, h * P:(h + 1) * P], src, ACT.Exp, bias=nbias[:, n, h:h + 1],
                                   scale=SCALE, accum_out=esum[:, n, h:h + 1])
            a.then_inc(sf.exp, 1)

        def soft_recip(dve, sf, u, n):
            dve.wait_ge(sf.exp, u + 1)
            dve.reciprocal(rsum[:, n, :], esum[:, n, :]).then_inc(sf.recip, 1)

        def soft_norm(pool, sf, u, n):
            pool.wait_ge(sf.recip, u + 1)
            pool.tensor_tensor(four(prob[:, n, :]), four(prob[:, n, :]),
                               rsum[:, n, :].unsqueeze(2).to_broadcast([P, 4, P]), ALU.mult).then_inc(sf.prob, 1)

        l0 = Softmax("l0")
        a_ready, a_free = sem("l0_tile_ready"), sem("l0_tile_copied")
        l0_vturned, l0_vcopied = sem("l0_vturned"), sem("l0_vcopied")
        l0_pturned, l0_pcopied = sem("l0_pturned"), sem("l0_pcopied")
        l0_o, l0_ohi, l0_olo, l0_y = sem("l0_o"), sem("l0_ohi"), sem("l0_olo"), sem("l0_y")
        L0_TILES = [(t, half) for half in range(2) for t in (K_TILE, V_TILE, 1)]

        x2_exp, x2_num, x2_rden = sem("x2_exp"), sem("x2_num"), sem("x2_rden")
        x2_mul, x2_turned = sem("x2_mul"), sem("x2_turned")

        f_ah, f_hm = sem("f_ah"), sem("f_hm")
        f_step = sem("f_step")
        f_turned, f_hi, f_lo, f_y = (sem("f_" + n) for n in ("turned", "hi", "lo", "y"))

        e_gate, e_up, e_diff, e_exp, e_hw = (sem("e_" + n) for n in ("gate", "up", "diff", "exp", "hw"))
        e_step = sem("e_step")
        e_scale = sem("e_scale")
        e_turned, e_hi, e_lo, e_y = (sem("e_" + n) for n in ("turned", "hi", "lo", "y"))

        def cast4(ap, n):
            return ap.unsqueeze(2).to_broadcast([P, HB, n])

        def of_all(c, n):
            return cst[:, c:c + n].unsqueeze(1).to_broadcast([P, HB, n])

        def halves_of(bufs, half, rows=P):
            return bufs[2 * half][0:rows, :], bufs[2 * half + 1][0:rows, :]

        down_bufs = [PTh, PTl, OTh, OTl]

        class Grouped:

            def __init__(self, name, slot, k, cross):
                self.slot, self.k, self.cross = slot, k, cross
                self.soft = Softmax(name)
                self.tile_ready = sem(name + "_tile_ready")
                self.rope_m = None if cross else sem(name + "_rope_m")
                self.tile_done = sem(name + "_tile_done")
                self.vt = None if cross else sem(name + "_vt")
                self.turned = sem(name + "_turned")
                self.t_hi, self.t_lo = sem(name + "_t_hi"), sem(name + "_t_lo")
                self.o, self.o_hi, self.o_lo = sem(name + "_o"), sem(name + "_o_hi"), sem(name + "_o_lo")
                self.y = sem(name + "_y")
                self.y_added = sem(name + "_y_added")

        attn = Grouped("ga", SLOT_ATTN, 3, False)
        xattn = Grouped("gx", SLOT_XATTN, 4, True)
        TILES_OF = 2 * NT
        NR = TILES_OF - 2
        NU = 2 + B
        STEP_TILES = [[0, 1, 2], [3, 4], [5], [6], [7], [8], [9], [10, 11]]
        def use(b):
            return b + 1 if b < 5 else b + 2
        V1_USE = 6

        def rope_index(j):
            return NR // 2 + j - (j > 5)

        def tile_dst(t, half):
            c = slice(half * HALF, (half + 1) * HALF)
            return KT[:, c] if t == K_TILE else VT[:, half, :] if t == V_TILE else qT[:, t - 1, c]

        def tile_evacuated(g, i, j):
            if g.cross:
                return g.tile_done, i * TILES_OF + NT + j + 1
            if j % NT == V_TILE:
                return g.vt, i * 2 + (2 if j < NT else 3)
            return g.rope_m, i * NR + rope_index(j) + 1

        def pe_first_tile(pe, g, k):
            pe.wait_ge(t_lo, g.slot * NT + k + 1)
            if k == (1 if g.cross else 0):
                pe.wait_ge(xt_lo, TURNS[g.k] + HB)
            if k >= 2:
                pe.wait_ge(g.tile_done if g.cross else g.rope_m, k - 1)
            sh, sl = (cTh, cTl) if g.cross and k in (K_TILE, V_TILE) else (xTh, xTl)
            tile_product(pe, pA[k % 2], k, 0, sh, sl).then_inc(g.tile_ready, 1)

        def pe_first(pe, g, tiles):
            for k in tiles:
                pe_first_tile(pe, g, k)

        def pe_second_turns(pe, k, g=None):
            if g is not None and g.cross:
                pe.wait_ge(g.tile_done, NT)
            elif g is not None:
                pe.wait_ge(g.rope_m, NT - 1)
                pe.wait_ge(g.vt, 1)
            for b in range(HB, B):
                turn_pe(pe, k, b)

        def g_pe(pe, g, i, last, nxt):
            sf = g.soft

            def tile(j):
                t, half = j % NT, 0 if j >= NT else 1
                if j >= NT:
                    pe.wait_ge(t_lo, i * NT + (g.slot + 1) * NT + t + 1)
                elif j == 0:
                    pe.wait_ge(xt_lo, TURNS[g.k] + B)
                if j >= 2:
                    pe.wait_ge(*tile_evacuated(g, i, j - 2))
                sh, sl = (cTh, cTl) if g.cross and t in (K_TILE, V_TILE) else (xTh, xTl)
                tile_product(pe, pA[j % 2], t, half, sh, sl).then_inc(g.tile_ready, 1)

            def tiles(n):
                for j in STEP_TILES[n]:
                    if not (last and j >= NT):
                        tile(j)

            def turn(n, src):
                for j in range(4):
                    t = pe.transpose(pT[n % 2][:, j * P:(j + 1) * P], src[:, j * P:(j + 1) * P], ident)
                t.then_inc(g.turned, 1)

            def turn_v(half):
                pe.wait_ge(*tile_evacuated(g, i, V_TILE - NT + half * NT)
                           if half or g.cross else (g.vt, i * 2 + 1))
                turn(V1_USE if half else 0, VT[:, half, :])

            def turn_p(b):
                pe.wait_ge(sf.prob, i * B + b + 1)
                turn(use(b), prob[:, b % 2, :])

            def scores(b):
                if g.cross:
                    pe.wait_ge(g.tile_done, i * TILES_OF + (NT if b >= HB else 0) + NT - 1)
                else:
                    pe.wait_ge(g.tile_done, i * NR + (NR if b >= HB else NR // 2))
                for h in range(REP):
                    mm = pe.matmul(pS[b % 2][:, h * P:(h + 1) * P], qT[:, h, b * P:(b + 1) * P],
                                   KT[:, b * P:(b + 1) * P], start=True, stop=True)
                    if b == 0 and h == 0:
                        mm.then_inc(o_used, 1)
                mm.then_inc(sf.scores, 1)

            def values(b):
                n = V1_USE if b == HB else use(b)
                pe.wait_ge(g.t_lo, i * NU + n + 1)
                mm3(pe, pO, Vh[:, b, :], Vl[:, b, :], PTh[:, :], PTl[:, :], True, True).then_inc(g.o, 1)

            def project(b):
                if b == 0:
                    pe.wait_ge(o_lo, i * NO + (g.slot + 1) * NO)
                pe.wait_ge(g.o_lo, i * B + b + 1)
                pe.wait_ge(g.y_added, i * B + b + 1)
                for h in range(REP):
                    c = slice(h * P, (h + 1) * P)
                    w = slice(h * D, (h + 1) * D)
                    mm = mm3(pe, pY, OTh[:, c], OTl[:, c], woh[:, w], wol[:, w], h == 0, h == REP - 1)
                mm.then_inc(g.y, 1)

            scores(0)
            scores(1)
            tile(0)
            turn_v(0)
            tile(1)
            turn_p(0)
            tile(2)
            values(0)
            for b in range(1, B):
                if b < B - 1:
                    scores(b + 1)
                turn_p(b)
                if b == HB:
                    turn_v(1)
                if b < B - 1:
                    tiles(b)
                    if last and b == HB and not g.cross:
                        pe_first(pe, nxt[1], [0])
                    project(b - 1)
                    if last and b == 6 and not g.cross:
                        pe.wait_ge(nxt[1].tile_done, 1)
                        for c in range(HB):
                            turn_pe(pe, nxt[0], c)
                elif not last:
                    tile(10)
                    project(b - 1)
                else:
                    if nxt[1] is not None:
                        pe_first(pe, nxt[1], [1])
                    project(b - 1)
                    if g.cross:
                        for c in range(HB):
                            turn_pe(pe, nxt[0], c)
                values(b)
            if not last:
                tile(11)
            elif nxt[1] is not None:
                pe_first(pe, nxt[1], [2])
            project(B - 1)
            if last and nxt[1] is not None:
                pe_first(pe, nxt[1], range(3, NT))
                pe_second_turns(pe, *nxt)

        def act_evacuate(act, g, t, half, bank, n, bias=None):
            act.wait_ge(g.tile_ready, n)
            if g.cross:
                act.activation(tile_dst(t, half), bank, ACT.Identity, bias=bias).then_inc(g.tile_done, 1)
            else:
                act.activation(tile_dst(t, half), bank, ACT.Copy).then_inc(g.vt, 1)

        def act_first(act, g, tiles):
            for k in tiles:
                if g.cross or k == V_TILE:
                    c = g.slot * 8 + k
                    act_evacuate(act, g, k, 0, pA[k % 2], k + 1, tbias[:, c:c + 1])

        def g_act(act, g, i, last, nxt):
            sf = g.soft

            def evacuate(j):
                t = j % NT
                if (last and j >= NT) or not (g.cross or t == V_TILE):
                    return
                c = i * 8 + ((g.slot + j // NT) * 8 + t)
                act_evacuate(act, g, t, 0 if j >= NT else 1, pA[j % 2], i * TILES_OF + (NT + j + 1),
                             tbias[:, bass.ds(c, 1)])

            def split_high(n, o):
                act.wait_ge(g.turned, i * NU + n + 1)
                act.activation(o, four(pT[n % 2]), ACT.Copy).then_inc(g.t_hi, 1)

            def split_v(half):
                split_high(V1_USE if half else 0, Vh[:, half * HB:(half + 1) * HB, :])

            def exps(b):
                n = b % 2
                if b >= 2:
                    act.wait_ge(g.turned, i * NU + use(b - 2) + 1)
                act.wait_ge(sf.bias, i * B + b + 1)
                for h in range(REP):
                    c = slice(h * P, (h + 1) * P)
                    src = pS[n][:, c] if g.cross else sm[:, n, c]
                    a = act.activation(prob[:, n, c], src, ACT.Exp, bias=nbias[:, n, h:h + 1],
                                       scale=SCALE, accum_out=esum[:, n, h:h + 1])
                a.then_inc(sf.exp, 1)

            def next_tile(k):
                split_tile_hi(act, i + (g.slot + 1), k, (g.tile_ready, i * TILES_OF + (NT + k + 1)))

            def out_chunks(ks):
                for k in ks:
                    split_out_hi(act, i + g.slot, k)

            out_chunks([0, 1])
            exps(0)
            evacuate(0)
            exps(1)
            split_v(0)
            evacuate(1)
            out_chunks([2, 3])
            split_high(use(0), four(PTh[:, :]))
            evacuate(2)
            next_tile(0)
            for b in range(B):
                if b:
                    split_high(use(b), four(PTh[:, :]))
                    if b == HB:
                        split_v(1)
                    if b < B - 1:
                        exps(b + 1)
                        for j in STEP_TILES[b]:
                            evacuate(j)
                        if b < NT:
                            next_tile(b)
                        if last and b == HB and not g.cross:
                            act_first(act, nxt[1], [0])
                        if last and b == 6 and not g.cross:
                            for c in range(HB):
                                turn_act(act, nxt[0], c)
                    else:
                        evacuate(10)
                        if last and nxt[1] is not None:
                            act_first(act, nxt[1], [1])
                        if last and g.cross:
                            for c in range(HB):
                                turn_act(act, nxt[0], c)
                act.wait_ge(g.o, i * B + b + 1)
                act.activation(OTh[:, :], pO, ACT.Copy).then_inc(g.o_hi, 1)
            evacuate(11)
            if last and nxt[1] is not None:
                act_first(act, nxt[1], range(2, NT))
                for b in range(HB, B):
                    turn_act(act, nxt[0], b)

        def dve_rope(dve, g, bank, ready, r, added_before):
            n = r % 2
            dve.wait_ge(g.tile_ready, ready)
            if added_before is not None:
                dve.wait_ge(g.tile_done, added_before)
            dve.tensor_tensor(four(m1[:, n, :]), four(bank), cosT, ALU.mult)
            for a in range(2):
                s, d = slice((1 - a) * 64, (2 - a) * 64), slice(a * 64, a * 64 + 64)
                sn = cst[s, C_SIN:C_SIN + P].unsqueeze(1).to_broadcast([64, HB, P])
                op = dve.tensor_tensor(four(m2[d, n, :]), four(bank[s, :]), sn, ALU.mult)
            op.then_inc(g.rope_m, 1)

        def dve_first(dve, g, tiles):
            for k in tiles:
                if not g.cross and k != V_TILE:
                    dve_rope(dve, g, pA[k % 2], k + 1, k, k - 1 if k >= 2 else None)

        def g_dve(dve, g, i, last, nxt):
            sf = g.soft

            def rope(j):
                if not (last and j >= NT) and not g.cross and j % NT != V_TILE:
                    r = rope_index(j)
                    dve_rope(dve, g, pA[j % 2], i * TILES_OF + (NT + j + 1), r, i * NR + (r - 1))

            def split_low(n, o, hi):
                dve.wait_ge(g.t_hi, i * NU + n + 1)
                dve.tensor_tensor(o, four(pT[n % 2]), hi.bitcast(F32), ALU.subtract).then_inc(g.t_lo, 1)

            def split_v(half):
                h = slice(half * HB, (half + 1) * HB)
                split_low(V1_USE if half else 0, Vl[:, h, :], Vh[:, h, :])

            def split_p(b):
                split_low(use(b), four(PTl[:, :]), four(PTh[:, :]))

            def out_low(b):
                dve.wait_ge(g.o_hi, i * B + b + 1)
                dve.tensor_tensor(OTl[:, :], pO, OTh[:, :].bitcast(F32), ALU.subtract).then_inc(g.o_lo, 1)

            def stats_of(b):
                if g.cross:
                    dve.wait_ge(res_ready, BIASES[g.k] + b + 1)
                else:
                    dve.wait_ge(g.y_added, (GROUPS - 1) * B + b + 2)
                norm_stats(dve, g.k, b, True)

            def add(b):
                dve.wait_ge(g.y, i * B + b + 1)
                dve.tensor_tensor(x[:, b, :], pY, x[:, b, :], ALU.add).then_inc(g.y_added, 1)
                if last and not g.cross:
                    stats_of(b)
                elif last and b:
                    stats_of(b - 1)

            def maxima(b):
                n = b % 2
                dve.wait_ge(sf.scores, i * B + b + 1)
                src = four(pS[n])
                if not g.cross:
                    dve.tensor_tensor(four(sm[:, n, :]), src, causal, ALU.add).then_inc(sf.masked, 1)
                    dve.wait_ge(sf.masked, i * B + b + 1)
                    src = four(sm[:, n, :])
                dve.tensor_reduce(nmax[:, n, :], src, AX.X, ALU.max, negate=True).then_inc(sf.max, 1)
                dve.wait_ge(sf.max, i * B + b + 1)
                dve.tensor_scalar(nbias[:, n, :], nmax[:, n, :], SCALE, None, ALU.mult).then_inc(sf.bias, 1)

            def recip(b):
                dve.wait_ge(sf.exp, i * B + b + 1)
                dve.reciprocal(rsum[:, b % 2, :], esum[:, b % 2, :]).then_inc(sf.recip, 1)

            def out_chunks(ks):
                for k in ks:
                    split_out_lo(dve, i + g.slot, k)

            def turns(bs):
                for b in bs:
                    turn_dve(dve, nxt[0], b)

            maxima(0)
            maxima(1)
            recip(0)
            rope(0)
            recip(1)
            split_v(0)
            rope(1)
            split_p(0)
            out_chunks([0, 1])
            rope(2)
            out_chunks([2, 3])
            for b in range(1, B):
                out_low(b - 1)
                if b < B - 1:
                    maxima(b + 1)
                split_p(b)
                if b == HB:
                    split_v(1)
                if b < B - 1:
                    recip(b + 1)
                    for j in STEP_TILES[b]:
                        rope(j)
                    add(b - 1)
                    if last and b == 5 and not g.cross:
                        norm_apply(dve, g.k, 0)
                    if last and b == 6:
                        if g.cross:
                            norm_apply(dve, g.k, 0)
                        else:
                            turns(range(HB))
                else:
                    add(b - 1)
                    rope(10)
                    if last and g.cross:
                        turns(range(HB))
            out_low(B - 1)
            add(B - 1)
            if last and g.cross:
                stats_of(B - 1)
            if last and nxt[1] is not None:
                norm_apply(dve, g.k, 1)
                turns(range(HB, B))

        def pool_rope(pool, g, t, half, r, value):
            pool.wait_ge(g.rope_m, value)
            pool.tensor_tensor(tile_dst(t, half), m1[:, r % 2, :], m2[:, r % 2, :], ALU.add).then_inc(g.tile_done, 1)

        def pool_first(pool, g, tiles):
            for k in tiles:
                if not g.cross and k != V_TILE:
                    pool_rope(pool, g, k, 0, k, k + 1)

        def g_pool(pool, g, i, last, nxt):
            sf = g.soft

            def rope(j):
                if not (last and j >= NT) and not g.cross and j % NT != V_TILE:
                    r = rope_index(j)
                    pool_rope(pool, g, j % NT, 0 if j >= NT else 1, r, i * NR + (r + 1))

            def norm(b):
                n = b % 2
                pool.wait_ge(sf.recip, i * B + b + 1)
                pool.tensor_tensor(four(prob[:, n, :]), four(prob[:, n, :]),
                                   rsum[:, n, :].unsqueeze(2).to_broadcast([P, 4, P]), ALU.mult).then_inc(sf.prob, 1)

            def bias(b):
                pool.wait_ge(g.y_added, (GROUPS - 1) * B + b + 2)
                pool.tensor_tensor(x[:, b, :], x[:, b, :], row[:, 0:D], ALU.add).then_inc(res_ready, 1)

            norm(0)
            rope(0)
            norm(1)
            rope(1)
            rope(2)
            split_tile_lo(pool, i + (g.slot + 1), 0)
            for b in range(1, B):
                if b < B - 1:
                    norm(b + 1)
                for j in STEP_TILES[b]:
                    rope(j)
                if b < NT:
                    split_tile_lo(pool, i + (g.slot + 1), b)
                if last and g.cross and b >= 2:
                    bias(b - 2)
                if last and b == (6 if g.cross else HB):
                    norm_pow(pool, g.k, 0)
            if last:
                if g.cross:
                    bias(B - 2)
                    bias(B - 1)
                norm_pow(pool, g.k, 1)

        def grouped(eng, one, g, nxt):
            with eng.Fori(0, GROUPS - 1) as i:
                one(eng, g, i, False, None)
            one(eng, g, GROUPS - 1, True, nxt)

        ctx_raw = qT[:, :, :].rearrange("p h t -> p (h t)").rearrange("p (b d) -> p b d", b=B)
        block = stack.enter_context(nc.Block())

        @block.sync
        def _(sp):
            sp.dma_start(cst[:, :], consts).then_inc(const_in, 16)
            for b in range(2):
                sp.dma_start(ctx_raw[:, b, :], ctx_in[b]).then_inc(ctx_loaded[b], 16)
            for b in range(B):
                sp.dma_start(x[:, b, :], x_in[b]).then_inc(x_loaded[b], 16)
            for k in range(NT - 1):
                load_tile_chunk(sp, 0, k)
            sp.dma_start(tbias[:, :], biases).then_inc(bias_in, 16)
            for b in range(2, B):
                sp.dma_start(ctx_raw[:, b, :], ctx_in[b]).then_inc(ctx_loaded[b], 16)
            sp.wait_ge(t_lo, 1)
            load_tile_chunk(sp, 0, NT - 1)
            sp.dma_start(row[:, 0:D], rows[R_BO0:R_BO0 + D].partition_broadcast(P)).then_inc(row_in, 16)
            sp.dma_start(row[:, D:D + NE], rows[R_GATE:R_GATE + NE].partition_broadcast(P)).then_inc(row_in, 16)
            with sp.Fori(0, SLOTS - 1) as s:
                load_out_part(sp, s)
                load_next_tile_part(sp, s)
            load_out_part(sp, SLOTS - 1)
            for b in range(B):
                sp.wait_ge(normed, NORMS[5] + b + 1)
                sp.dma_start(out[b], x[:, b, :]).then_inc(out_done, 16)
            sp.wait_ge(out_done, 16 * B)

        @block.tensor
        def _(pe):
            pe.wait_ge(const_in, 16)

            def ctx_turn(b):
                pe.wait_ge(c_exp, b + 1)
                if b >= 2:
                    pe.wait_ge(c_dve, b - 1)
                for c in range(NC):
                    cc = slice(c * P, (c + 1) * P)
                    pe.transpose(pT[b % 2][:, cc], prob[:, b % 2, cc], ident)
                    t = pe.transpose(pS[b % 2][:, cc], ctx_raw[:, b, cc], ident)
                t.then_inc(c_turned, 1)

            def ctx_kv(b):
                pe.wait_ge(c_dve, b + 1)
                if b:
                    pe.wait_ge(c_kvm, b)
                for c in range(NC):
                    cc = slice(c * P, (c + 1) * P)
                    mm = pe.matmul(pO[:, 0:P], sm[:, b % 2, cc], m1[:, b % 2, cc], start=(c == 0), stop=(c == NC - 1))
                mm.then_inc(c_kv, 1)

            for b in range(B):
                ctx_turn(b)
                if b:
                    ctx_kv(b - 1)
            ctx_kv(B - 1)

            for b in range(B):
                turn_pe(pe, 0, b)
            pe.wait_ge(t_lo, NT)
            pe.wait_ge(c_kvm, B)

            def l0_vturn(half):
                pe.wait_ge(a_free, half * 3 + 2)
                for j in range(4):
                    t = pe.transpose(pT[half][:, j * P:(j + 1) * P], VT[:, half, j * P:(j + 1) * P], ident)
                t.then_inc(l0_vturned, 1)

            for j, (t, half) in enumerate(L0_TILES):
                pe.wait_ge(xt_lo, TURNS[0] + HB * (half + 1) if j >= 2 else B)
                if j >= 2:
                    pe.wait_ge(a_free, j - 1)
                tile_product(pe, pA[j % 2], t, half, xTh, xTl).then_inc(a_ready, 1)
                if t == 1:
                    l0_vturn(half)
            pe.wait_ge(a_free, 6)
            for half in range(2):
                for j in range(4):
                    b = half * HB + j
                    mm = pe.matmul(pS[half][:, j * P:(j + 1) * P], qT[:, 0, b * P:(b + 1) * P],
                                   KT[:, b * P:(b + 1) * P], start=True, stop=True)
                    if b == 0:
                        mm.then_inc(t_used, 1)
                mm.then_inc(l0.scores, 1)
            pe.wait_ge(o_lo, NO)
            for half in range(2):
                pe.wait_ge(l0.prob, half + 1)
                pe.wait_ge(l0_vcopied, half + 1)
                for j in range(4):
                    t = pe.transpose(pT[half][:, j * P:(j + 1) * P], prob[:, half, j * P:(j + 1) * P], ident)
                t.then_inc(l0_pturned, 1)
            for half in range(2):
                pe.wait_ge(l0_pcopied, half + 1)
                if half:
                    pe.wait_ge(l0_olo, half)
                for j in range(4):
                    c = slice(j * P, (j + 1) * P)
                    mm = pe.matmul(pO[:, c], m1[:, half, c], sm[:, half, c], start=True, stop=True)
                mm.then_inc(l0_o, 1)
                pe.wait_ge(l0_olo, half + 1)
                for j in range(4):
                    b = half * HB + j
                    c = slice(j * P, (j + 1) * P)
                    if b >= 2:
                        pe.wait_ge(added, ADDS[0] + b - 1)
                    mm3(pe, pA[b % 2], OTh[:, c], OTl[:, c], woh[:, 0:D], wol[:, 0:D], True, True).then_inc(l0_y, 1)

            def x2_product(b):
                pe.wait_ge(x2_exp, b + 1)
                if b >= 2:
                    pe.wait_ge(x2_mul, 2 * (b - 1))
                pair = 2 + 2 * (b % 2)
                for c in range(NC):
                    o = ps[:, pair + c // 2, (c % 2) * (P + XH):(c % 2 + 1) * (P + XH)]
                    mm = pe.matmul(o, prob[:, b % 2, c * P:(c + 1) * P], kvm[:, b, :], start=True, stop=True)
                    if b == 0 and c == 0:
                        mm.then_inc(o_used, 1)
                mm.then_inc(x2_num, 1)

            def x2_turn(b):
                pe.wait_ge(x2_mul, 2 * (b + 1))
                if b >= 2:
                    pe.wait_ge(added, ADDS[1] + b - 1)
                for c in range(NC):
                    t = pe.transpose(ps[:, 6 + b % 2, c * P:(c + 1) * P], m2[:, b % 2, c * P:(c + 1) * P], ident)
                t.then_inc(x2_turned, 1)

            for b in range(B):
                x2_product(b)
                if b:
                    x2_turn(b - 1)
            for b in range(HB):
                turn_pe(pe, 2, b)
            x2_turn(B - 1)

            UP = [pS[0], pS[1], pO, pY]
            pe.wait_ge(t_lo, 2 * NT)
            pe.wait_ge(o_lo, 2 * NO)

            def f_ranks(half):
                pe.wait_ge(xt_lo, TURNS[2] + (half + 1) * HB)
                for j in range(HB):
                    b = half * HB + j
                    for c in range(NC):
                        xc = slice(b * P, (b + 1) * P)
                        w = slice(c * P, c * P + LR + NE0)
                        mm = mm3(pe, pT[half][:, j * P:j * P + LR + NE0], xTh[:, c, xc], xTl[:, c, xc],
                                 wth[:, w], wtl[:, w], c == 0, c == NC - 1)
                mm.then_inc(f_ah, 1)

            def f_up(b):
                pe.wait_ge(xt_lo, TURNS[2] + b + 1)
                if b >= 4:
                    pe.wait_ge(added, ADDS[2] + b - 3)
                xc = slice(b * P, (b + 1) * P)
                for c in range(NC):
                    w = slice(c * D, (c + 1) * D)
                    mm3(pe, UP[b % 4], xTh[:, c, xc], xTl[:, c, xc], woh[:, w], wol[:, w], c == 0, False)

            def f_turn(half):
                pe.wait_ge(f_hm, half + 1)
                for j in range(HB):
                    t = pe.transpose(pT[half][0:LR, j * P:(j + 1) * P], m1[:, half, j * LR:(j + 1) * LR], ident)
                t.then_inc(f_turned, 1)

            def f_down(b):
                pe.wait_ge(f_lo, b // HB + 1)
                c, w = slice((b % HB) * P, (b % HB + 1) * P), slice(V_TILE * D, (V_TILE + 1) * D)
                th, tl = halves_of(down_bufs, b // HB, LR)
                mm3(pe, UP[b % 4], th[:, c], tl[:, c], wth[0:LR, w], wtl[0:LR, w], False, True).then_inc(f_y, 1)

            f_ranks(0)
            f_up(0)
            f_up(1)
            for b in range(HB, B):
                turn_pe(pe, 2, b)
            f_ranks(1)
            for b in range(B):
                if b % HB == 0:
                    f_turn(b // HB)
                if b < B - 2:
                    f_up(b + 2)
                if b == B - 1:
                    for c in range(HB):
                        turn_pe(pe, attn.k, c)
                f_down(b)

            pe_first(pe, attn, range(NT))
            pe_second_turns(pe, attn.k, attn)
            grouped(pe, g_pe, attn, (xattn.k, xattn))
            grouped(pe, g_pe, xattn, (5, None))

            pe.wait_ge(t_lo, SLOTS * NT)

            def e_gates(half):
                pe.wait_ge(xt_lo, TURNS[5] + (half + 1) * HB)
                for j in range(HB):
                    b = half * HB + j
                    xc = slice(b * P, (b + 1) * P)
                    o = (pA if half else pT)[0][:, j * NE:(j + 1) * NE]
                    for c in range(NC):
                        w = slice(NC * D + c * P, NC * D + c * P + NE)
                        mm = mm3(pe, o, xTh[:, c, xc], xTl[:, c, xc], wth[:, w], wtl[:, w], c == 0, c == NC - 1,
                                 o_used if b == 0 and c == 0 else None)
                mm.then_inc(e_gate, 1)

            def e_hidden(b):
                pe.wait_ge(xt_lo, TURNS[5] + b + 1)
                if b >= 2:
                    pe.wait_ge(e_hw, b - 1)
                xc = slice(b * P, (b + 1) * P)
                for c in range(NC):
                    w = slice(c * D, (c + 1) * D)
                    mm = mm3(pe, pS[b % 2], xTh[:, c, xc], xTl[:, c, xc], wth[:, w], wtl[:, w], c == 0, c == NC - 1)
                mm.then_inc(e_up, 1)

            def e_turn(b):
                pe.wait_ge(e_hw, b + 1)
                if b >= 2:
                    pe.wait_ge(e_lo, b - 1)
                for c in range(NC):
                    t = pe.transpose(pT[b % 2][:, c * P:(c + 1) * P], m1[:, b % 2, c * P:(c + 1) * P], ident)
                t.then_inc(e_turned, 1)

            def e_down(b):
                pe.wait_ge(e_lo, b + 1)
                if b >= 2:
                    pe.wait_ge(added, ADDS[5] + b - 1)
                th, tl = halves_of(down_bufs, b % 2)
                for c in range(NC):
                    cc, w = slice(c * P, (c + 1) * P), slice(c * D, (c + 1) * D)
                    mm = mm3(pe, ps[:, 6 + b % 2, :], th[:, cc], tl[:, cc], woh[:, w], wol[:, w], c == 0, c == NC - 1)
                mm.then_inc(e_y, 1)

            e_gates(0)
            e_hidden(0)
            e_hidden(1)
            pe_second_turns(pe, 5)
            for b in range(B):
                e_turn(b)
                if b < B - 2:
                    e_hidden(b + 2)
                if b == 1:
                    e_gates(1)
                if b == 0:
                    pe.wait_ge(o_lo, SLOTS * NO)
                e_down(b)

        @block.scalar
        def _(act):
            def ctx_exp(b):
                act.wait_ge(c_max, b + 1)
                if b >= 2:
                    act.wait_ge(c_turned, b - 1)
                act.activation(prob[:, b % 2, :], ctx_raw[:, b, :], ACT.Exp, bias=cmax[:, b:b + 1],
                               accum_out=csum[:, b:b + 1]).then_inc(c_exp, 1)

            ctx_exp(0)
            for b in range(B):
                if b < B - 1:
                    ctx_exp(b + 1)
                act.wait_ge(c_turned, b + 1)
                if b >= 2:
                    act.wait_ge(c_kv, b - 1)
                act.activation(sm[:, b % 2, :], pT[b % 2], ACT.Copy)
                act.activation(cTh[:, :, b * P:(b + 1) * P], four(pS[b % 2]), ACT.Copy).then_inc(c_act, 1)
                if b < NT:
                    split_tile_hi(act, 0, b)
            act.wait_ge(bias_in, 16)
            for k in range(NO):
                split_out_hi(act, 0, k)
            for b in range(B):
                turn_act(act, 0, b)
            for j, (t, half) in enumerate(L0_TILES):
                act.wait_ge(a_ready, j + 1)
                act.activation(tile_dst(t, half), pA[j % 2], ACT.Identity, bias=tbias[:, t:t + 1]).then_inc(a_free, 1)
                if t == 1:
                    act.wait_ge(l0_vturned, half + 1)
                    act.activation(m1[:, half, :], pT[half], ACT.Copy).then_inc(l0_vcopied, 1)
            for half in range(2):
                soft_exp(act, l0, half, half, False)
            for k in range(NT):
                split_tile_hi(act, 1, k, (t_used, 1))
            for half in range(2):
                act.wait_ge(l0_pturned, half + 1)
                act.activation(sm[:, half, :], pT[half], ACT.Copy).then_inc(l0_pcopied, 1)
            for half in range(2):
                act.wait_ge(l0_o, half + 1)
                if half:
                    act.wait_ge(l0_y, HB)
                act.activation(OTh[:, :], pO, ACT.Copy).then_inc(l0_ohi, 1)
            act.wait_ge(res_ready, BIASES[0] + B)
            act.dma_start(row[:, 0:D], rows[R_B1:R_B1 + D].partition_broadcast(P)).then_inc(row_in, 16)
            for b in range(B):
                act.wait_ge(normed, NORMS[0] + b + 1)
                if b >= 2:
                    act.wait_ge(x2_num, b - 1)
                act.activation(prob[:, b % 2, :], x[:, b, :], ACT.Exp).then_inc(x2_exp, 1)
                if 1 <= b < 1 + NO:
                    split_out_hi(act, 1, b - 1)
            for b in range(B):
                turn_act(act, 2, b)

            def f_split(half):
                act.wait_ge(f_turned, half + 1)
                act.activation(halves_of(down_bufs, half, LR)[0], pT[half][0:LR, :], ACT.Copy).then_inc(f_hi, 1)

            f_split(0)
            for k in range(NT - 1):
                split_tile_hi(act, SLOT_ATTN, k, (f_ah, 2))
            f_split(1)
            act.wait_ge(res_ready, BIASES[2] + B)
            act.dma_start(row[:, 0:D], rows[R_BO5:R_BO5 + D].partition_broadcast(P)).then_inc(row_in, 16)
            for b in range(HB):
                turn_act(act, attn.k, b)
            split_tile_hi(act, SLOT_ATTN, NT - 1, (f_y, B))
            act_first(act, attn, range(NT))
            for b in range(HB, B):
                turn_act(act, attn.k, b)
            grouped(act, g_act, attn, (xattn.k, xattn))
            grouped(act, g_act, xattn, (5, None))
            for k in range(NO):
                split_out_hi(act, SLOT_MOE, k)

            def e_exps(half):
                act.wait_ge(e_diff, half + 1)
                act.activation(logit[:, :, :], logit[:, :, :], ACT.Exp).then_inc(e_exp, 1)

            e_exps(0)
            for b in range(HB, B):
                turn_act(act, 5, b)
            for b in range(B):
                act.wait_ge(e_turned, b + 1)
                act.activation(halves_of(down_bufs, b % 2)[0], pT[b % 2], ACT.Copy).then_inc(e_hi, 1)
                if b == 2:
                    e_exps(1)

        @block.vector
        def _(dve):
            dve.wait_ge(const_in, 16)
            for b in range(B):
                op = dve.tensor_copy(kvm[:, b, P:P + XH], cst[:, C_GROUP:C_GROUP + XH])
            op.then_inc(c_set, 1)

            def ctx_max(b):
                dve.wait_ge(ctx_loaded[b], 16)
                dve.tensor_reduce(cmax[:, b:b + 1], ctx_raw[:, b, :], AX.X, ALU.max, negate=True).then_inc(c_max, 1)

            def ctx_kvm(b):
                dve.wait_ge(c_exp, b + 1)
                dve.reciprocal(crs[:, b:b + 1], csum[:, b:b + 1]).then_inc(c_rs, 1)
                dve.wait_ge(c_rs, b + 1)
                dve.wait_ge(c_kv, b + 1)
                dve.scalar_tensor_tensor(kvm[:, b, 0:P], pO[:, 0:P], crs[:, b:b + 1], cst[:, C_BLOCK:C_BLOCK + P],
                                         ALU.mult, ALU.mult).then_inc(c_kvm, 1)

            ctx_max(0)
            for b in range(B):
                if b < B - 1:
                    ctx_max(b + 1)
                dve.wait_ge(c_act, b + 1)
                if b >= 2:
                    dve.wait_ge(c_kv, b - 1)
                dve.tensor_copy(m1[:, b % 2, :], pS[b % 2])
                dve.tensor_tensor(cTl[:, :, b * P:(b + 1) * P], four(pS[b % 2]),
                                  cTh[:, :, b * P:(b + 1) * P].bitcast(F32), ALU.subtract).then_inc(c_dve, 1)
                if b:
                    ctx_kvm(b - 1)
            ctx_kvm(B - 1)
            for b in range(B):
                turn_dve(dve, 0, b)
            for half in range(2):
                soft_max(dve, l0, half, half, False)
            for half in range(2):
                soft_recip(dve, l0, half, half)
            for half in range(2):
                dve.wait_ge(l0_ohi, half + 1)
                dve.tensor_tensor(OTl[:, :], pO, OTh[:, :].bitcast(F32), ALU.subtract).then_inc(l0_olo, 1)
                for j in range(HB):
                    b = half * HB + j
                    dve.wait_ge(l0_y, b + 1)
                    dve.wait_ge(res_ready, BIASES[0] + b + 1)
                    dve.tensor_tensor(x[:, b, :], pA[b % 2], x[:, b, :], ALU.add).then_inc(added, 1)
                    norm_stats(dve, 0, b)
                if half:
                    norm_apply(dve, 0, 0)
            norm_apply(dve, 0, 1)
            def x2_divide(b):
                pair = 2 + 2 * (b % 2)
                dve.wait_ge(x2_num, b + 1)
                both = ps[:, pair:pair + 2, 0:2 * (P + XH)].rearrange("p k (c w) -> p k c w", c=2)
                dve.reciprocal(rden[:, b % 2, :, :].rearrange("p (k c) g -> p k c g", k=2), both[:, :, :, P:P + XH])\
                    .then_inc(x2_rden, 1)
                dve.wait_ge(x2_rden, b + 1)
                if b >= 2:
                    dve.wait_ge(x2_turned, b - 1)
                for k in range(2):
                    o = m2[:, b % 2, 2 * k * P:2 * (k + 1) * P].rearrange("p (c g e) -> p c g e", c=2, g=XH)
                    i0 = both[:, k, :, 0:P].rearrange("p c (g e) -> p c g e", g=XH)
                    r = rden[:, b % 2, 2 * k:2 * k + 2, :].unsqueeze(3).to_broadcast([P, 2, XH, XD])
                    dve.tensor_tensor(o, i0, r, ALU.mult).then_inc(x2_mul, 1)

            x2_divide(0)
            for b in range(B):
                if b < B - 1:
                    x2_divide(b + 1)
                if b == B - 1:
                    for c in range(HB):
                        turn_dve(dve, 2, c)
                dve.wait_ge(x2_turned, b + 1)
                dve.tensor_tensor(x[:, b, :], ps[:, 6 + b % 2, :], x[:, b, :], ALU.add).then_inc(added, 1)
                norm_stats(dve, 1, b)
                if b == 5:
                    norm_apply(dve, 1, 0)
            dve.wait_ge(row_in, 32)

            def f_choose(half):
                s0 = 6 * half
                four_seqs = pT[half].rearrange("p (j n) -> p j n", j=HB)
                lg, bl = logit[:, :, 0:NE0], below[:, :, 0:NE0]
                top, index = best[:, 0, :], best[:, 1, :]
                dve.wait_ge(f_ah, half + 1)
                dve.tensor_tensor(lg, four_seqs[:, :, LR:LR + NE0],
                                  row[:, D:D + NE0].unsqueeze(1).to_broadcast([P, HB, NE0]), ALU.add)\
                    .then_inc(f_step, 1)
                dve.wait_ge(f_step, s0 + 1)
                dve.tensor_reduce(top, lg, AX.X, ALU.max).then_inc(f_step, 1)
                dve.wait_ge(f_step, s0 + 2)
                dve.tensor_tensor(bl, lg, cast4(top, NE0), ALU.is_lt).then_inc(f_step, 1)
                dve.wait_ge(f_step, s0 + 3)
                dve.scalar_tensor_tensor(bl, bl, float(NE), of_all(C_IOTA, NE0), ALU.mult, ALU.add).then_inc(f_step, 1)
                dve.wait_ge(f_step, s0 + 4)
                dve.tensor_reduce(index, bl, AX.X, ALU.min).then_inc(f_step, 1)
                dve.wait_ge(f_step, s0 + 5)
                dve.tensor_tensor(keep[:, :, :], of_all(C_SEG, LR), cast4(index, LR), ALU.is_le).then_inc(f_step, 1)
                dve.wait_ge(f_step, s0 + 6)
                dve.tensor_tensor(m1[:, half, 0:HB * LR].rearrange("p (j r) -> p j r", j=HB), keep[:, :, :],
                                  four_seqs[:, :, 0:LR], ALU.mult).then_inc(f_hm, 1)

            f_choose(0)
            norm_apply(dve, 1, 1)
            for b in range(HB, B):
                turn_dve(dve, 2, b)
            for b in range(B):
                if b % HB == 0:
                    dve.wait_ge(f_hi, b // HB + 1)
                    th, tl = halves_of(down_bufs, b // HB, LR)
                    dve.tensor_tensor(tl, pT[b // HB][0:LR, :], th.bitcast(F32), ALU.subtract).then_inc(f_lo, 1)
                if b == 0:
                    f_choose(1)
                if b == B - 1:
                    for c in range(HB):
                        turn_dve(dve, attn.k, c)
                dve.wait_ge(f_y, b + 1)
                dve.wait_ge(res_ready, BIASES[2] + b + 1)
                dve.tensor_tensor(x[:, b, :], [pS[0], pS[1], pO, pY][b % 4], x[:, b, :], ALU.add).then_inc(added, 1)
                norm_stats(dve, 2, b)
                if b == 5:
                    norm_apply(dve, 2, 0)
            dve_first(dve, attn, range(2))
            norm_apply(dve, 2, 1)
            dve_first(dve, attn, range(2, NT))
            for b in range(HB, B):
                turn_dve(dve, attn.k, b)
            for g in (attn, xattn):
                dve.sem_inc(g.y_added, 1)
            grouped(dve, g_dve, attn, (xattn.k, xattn))
            grouped(dve, g_dve, xattn, (5, None))

            def e_choose(half):
                s0 = 14 * half
                lg = logit[:, :, :]
                bank = (pA if half else pT)[0][:, 0:HB * NE].rearrange("p (j e) -> p j e", j=HB)

                def first_best(n, src, one_hot, top, index):
                    dve.tensor_reduce(top, src, AX.X, ALU.max).then_inc(e_step, 1)
                    dve.wait_ge(e_step, n + 1)
                    dve.tensor_tensor(below[:, :, :], src, cast4(top, NE), ALU.is_lt).then_inc(e_step, 1)
                    dve.wait_ge(e_step, n + 2)
                    dve.scalar_tensor_tensor(below[:, :, :], below[:, :, :], float(NE), of_all(C_IOTA, NE),
                                             ALU.mult, ALU.add).then_inc(e_step, 1)
                    dve.wait_ge(e_step, n + 3)
                    dve.tensor_reduce(index, below[:, :, :], AX.X, ALU.min).then_inc(e_step, 1)
                    dve.wait_ge(e_step, n + 4)
                    dve.tensor_tensor(one_hot, of_all(C_IOTA, NE), cast4(index, NE), ALU.is_equal).then_inc(e_step, 1)
                    dve.wait_ge(e_step, n + 5)

                dve.wait_ge(e_gate, half + 1)
                dve.tensor_reduce(best[:, 0, :], bank, AX.X, ALU.max, negate=True).then_inc(e_step, 1)
                dve.wait_ge(e_step, s0 + 1)
                dve.tensor_tensor(lg, bank, cast4(best[:, 0, :], NE), ALU.add).then_inc(e_diff, 1)
                dve.wait_ge(e_exp, half + 1)
                first_best(s0 + 1, lg, first[:, :, :], best[:, 1, :], best[:, 2, :])
                dve.scalar_tensor_tensor(second[:, :, :], first[:, :, :], -4.0, lg, ALU.mult, ALU.add)\
                    .then_inc(e_step, 1)
                dve.wait_ge(e_step, s0 + 7)
                first_best(s0 + 7, second[:, :, :], second[:, :, :], best[:, 3, :], best[:, 4, :])
                dve.tensor_tensor(best[:, 5, :], best[:, 1, :], best[:, 3, :], ALU.add).then_inc(e_step, 1)
                dve.tensor_tensor(first[:, :, :], first[:, :, :], second[:, :, :], ALU.add).then_inc(e_step, 1)
                dve.wait_ge(e_step, s0 + 14)
                dve.reciprocal(best[:, 5, :], best[:, 5, :]).then_inc(e_scale, 1)
                dve.tensor_tensor(lg, lg, first[:, :, :], ALU.mult).then_inc(e_scale, 1)
                dve.wait_ge(e_scale, 3 * half + 2)
                dve.tensor_tensor(weight[:, half, :, :], lg, cast4(best[:, 5, :], NE), ALU.mult).then_inc(e_scale, 1)

            def e_weigh(b):
                dve.wait_ge(e_up, b + 1)
                if b % HB == 0:
                    dve.wait_ge(e_scale, 3 * (b // HB) + 3)
                if b >= 2:
                    dve.wait_ge(e_turned, b - 1)
                dve.tensor_tensor(m1[:, b % 2, :].rearrange("p (e r) -> p e r", e=NE),
                                  pS[b % 2].rearrange("p (e r) -> p e r", e=NE),
                                  weight[:, b // HB, b % HB, :].unsqueeze(2).to_broadcast([P, NE, D // NE]),
                                  ALU.mult).then_inc(e_hw, 1)

            e_choose(0)
            norm_apply(dve, xattn.k, 1)
            e_weigh(0)
            e_weigh(1)
            for b in range(HB, B):
                turn_dve(dve, 5, b)
            for b in range(B):
                dve.wait_ge(e_hi, b + 1)
                th, tl = halves_of(down_bufs, b % 2)
                dve.tensor_tensor(tl, pT[b % 2], th.bitcast(F32), ALU.subtract).then_inc(e_lo, 1)
                if b == 2:
                    e_choose(1)
                if b < B - 2:
                    e_weigh(b + 2)
                dve.wait_ge(e_y, b + 1)
                dve.tensor_tensor(x[:, b, :], ps[:, 6 + b % 2, :], x[:, b, :], ALU.add).then_inc(added, 1)
                norm_stats(dve, 5, b)
                if b == 5:
                    norm_apply(dve, 5, 0)
            norm_apply(dve, 5, 1)

        @block.gpsimd
        def _(pool):
            pool.wait_ge(const_in, 16)
            for k in range(NT):
                split_tile_lo(pool, 0, k)
            for k in range(NO):
                split_out_lo(pool, 0, k)
            for b in range(B):
                residual_bias(pool, 0, b, 2)
            for half in range(2):
                soft_norm(pool, l0, half, half)
            for k in range(NT):
                split_tile_lo(pool, 1, k)
            norm_pow(pool, 0, 0)
            norm_pow(pool, 0, 1)
            for k in range(NO):
                split_out_lo(pool, 1, k)
            norm_pow(pool, 1, 0)
            norm_pow(pool, 1, 1)
            for b in range(B):
                residual_bias(pool, 2, b, 3)
            for k in range(NT - 1):
                split_tile_lo(pool, SLOT_ATTN, k)
            norm_pow(pool, 2, 0)
            norm_pow(pool, 2, 1)
            split_tile_lo(pool, SLOT_ATTN, NT - 1)
            pool_first(pool, attn, range(NT))
            grouped(pool, g_pool, attn, (xattn.k, xattn))
            pool.wait_ge(row_in, 64)
            grouped(pool, g_pool, xattn, (5, None))
            for k in range(NO):
                split_out_lo(pool, SLOT_MOE, k)
            norm_pow(pool, 5, 0)
            norm_pow(pool, 5, 1)


def constants():
    import numpy as np

    c = np.zeros((P, CONSTS), np.float32)
    c[:, C_ID:C_ID + P] = np.eye(P)
    inv = 1.0 / 500000.0 ** (np.arange(0, HD, 2, dtype=np.float64) / HD)
    wavelen = 2.0 * np.pi / inv
    smooth = (1024 / wavelen - 1.0) / (4.0 - 1.0)
    scaled = np.where(wavelen > 1024 / 1.0, inv / 8.0, inv)
    mid = (wavelen <= 1024 / 1.0) & (wavelen >= 1024 / 4.0)
    scaled = np.where(mid, (1 - smooth) * inv / 8.0 + smooth * inv, scaled).astype(np.float32)
    emb = np.arange(P, dtype=np.float32)[:, None] * scaled[None, :]
    cos, sin = np.cos(emb).T, np.sin(emb).T
    c[:, C_COS:C_COS + P] = np.concatenate([cos, cos])
    c[:, C_SIN:C_SIN + P] = np.concatenate([sin, -sin])
    c[:, C_CAUSAL:C_CAUSAL + P] = np.where(np.tril(np.ones((P, P))) > 0, 0.0, NEG)
    head = np.arange(P) // XD
    c[:, C_BLOCK:C_BLOCK + P] = head[:, None] == head[None, :]
    c[:, C_GROUP:C_GROUP + XH] = head[:, None] == np.arange(XH)[None, :]
    c[:, C_SEG:C_SEG + LR] = np.searchsorted([8, 16, 32, 64], np.arange(LR), side="right")
    c[:, C_IOTA:C_IOTA + NE] = np.arange(NE)
    c[:, C_POW:C_POW + 8] = -0.5
    return c


def chunks(w):
    return w.reshape(-1, P, w.shape[1]).transpose(1, 0, 2)


def layout(a):
    import numpy as np

    wt = np.zeros((SLOTS, NT, P, D), np.float32)
    wo = np.zeros((SLOTS, NO, P, D), np.float32)
    bias = np.zeros((P, SLOTS, 8), np.float32)

    def tile(s, t, w):
        wt[s, t] = chunks(w).reshape(P, D)

    def columns(w, n):
        return w[:, n * P:(n + 1) * P]

    for t, n in ((K_TILE, 1), (V_TILE, 2), (1, 0)):
        tile(0, t, columns(a["L0_attn_Wqkv"], n))
        bias[:, 0, t] = a["L0_attn_bqkv"][n * P:(n + 1) * P]
    wo[0, 0] = a["L0_attn_Wo"]
    first = wt[1, 0].reshape(P, NC, P)
    first[:, :, :LR] = chunks(a["L0_ffn_A"].T)
    first[:, :, LR:LR + NE0] = chunks(a["L0_ffn_gate_w"].T)
    wt[1, V_TILE, :LR] = a["L0_ffn_B"].T
    wo[1] = a["L0_ffn_W"].T.reshape(NO, P, D)
    for g in range(GROUPS):
        s = SLOT_ATTN + g
        tile(s, K_TILE, columns(a["L1_attn_wk"], g))
        tile(s, V_TILE, columns(a["L1_attn_wv"], g))
        for h in range(REP):
            tile(s, 1 + h, columns(a["L1_attn_wq"], REP * g + h))
        wo[s] = a["L1_attn_wo"][g * D:(g + 1) * D].reshape(NO, P, D)
        s = SLOT_XATTN + g
        for t, n in ((K_TILE, g), (V_TILE, GROUPS + g)):
            tile(s, t, columns(a["L1_xattn_Wkv"], n))
            bias[:, s, t] = a["L1_xattn_bkv"][n * P:(n + 1) * P]
        for h in range(REP):
            n = REP * g + h
            tile(s, 1 + h, columns(a["L1_xattn_Wq"], n))
            bias[:, s, 1 + h] = a["L1_xattn_bq"][n * P:(n + 1) * P]
        wo[s] = a["L1_xattn_Wo"][g * D:(g + 1) * D].reshape(NO, P, D)
    s = SLOT_MOE
    wt[s, :NC] = a["L1_ffn_lora_A"].reshape(D, D).T.reshape(NC, P, D)
    wt[s, NC].reshape(P, NC, P)[:, :, :NE] = chunks(a["L1_ffn_gate_w"].T)
    wo[s] = a["L1_ffn_lora_B"].transpose(0, 2, 1).reshape(NO, P, D)
    rows = np.zeros((ROWS,), np.float32)
    rows[R_BO0:R_BO0 + D] = a["L0_attn_bo"]
    rows[R_B1:R_B1 + D] = a["L0_ffn_b"]
    rows[R_BO5:R_BO5 + D] = a["L1_xattn_bo"]
    rows[R_GATE:R_GATE + NE0] = a["L0_ffn_gate_b"]
    return {"x": a["x"], "ctx": a["ctx_4096"], "w_tile": wt, "w_out": wo,
            "biases": bias.reshape(P, SLOTS * 8), "consts": constants(), "rows": rows}


def kernel(**inputs):
    import numpy as np
    import concourse.bacc as bacc
    from concourse.bass_utils import run_bass_kernel_spmd

    arrays = {"in_" + k: np.ascontiguousarray(v) for k, v in layout({k: np.asarray(v) for k, v in inputs.items()}).items()}
    nc = bacc.Bacc("TRN2", target_bir_lowering=False, num_devices=1)
    aps = [nc.dram_tensor(n, a.shape, F32, kind="ExternalInput").ap() for n, a in arrays.items()]
    out = nc.dram_tensor("out", [B, P, D], F32, kind="ExternalOutput").ap()
    build(nc, *aps, out)
    r = run_bass_kernel_spmd(nc, [arrays], core_ids=[0])
    return r.results[0]["out"]
```

```python
from contextlib import ExitStack

import concourse.bass as bass
from concourse import mybir

F32 = mybir.dt.float32
F32R = mybir.dt.float32r
ALU = mybir.AluOpType
ACT = mybir.ActivationFunctionType
AX = mybir.AxisListType

P = 128
B = 8
D = 512
NC = D // P
TOK = B * P
HALF = TOK // 2
HB = B // 2
HD = 128
GROUPS = 8
REP = 4
TILES = 2 + REP
WT = TILES * D
WO = NC * D
NT, NO = WT // D, WO // D
RING = 5
K_TILE, V_TILE = 0, NT - 1
L0_K, L0_Q, L0_V, L0_RANKS, L0_OUT, L0_B = range(NT)
SLOT_ATTN, SLOT_XATTN, SLOT_MOE = 1, 1 + GROUPS, 1 + 2 * GROUPS
SLOTS = SLOT_MOE + 1
XH, XD = 8, 16
LR, NE0 = 64, 4
NE = 8
SCALE = float(HD) ** -0.5
EPS = 1e-5
NEG = -1e30
C_ID, C_COS, C_SIN, C_CAUSAL, C_BLOCK, C_GROUP, C_SEG, C_IOTA, C_POW = 0, 128, 256, 384, 512, 640, 648, 712, 720
CONSTS = 728
R_BO0, R_B1, R_BO5, R_GATE = 0, D, 2 * D, 3 * D
ROWS = 3 * D + 8


def build(nc, x_in, ctx_in, w_tile, w_out, biases, consts, rows, out):
    with ExitStack() as stack:
        def sb(name, shape, dt=F32):
            return stack.enter_context(nc.sbuf_tensor(name, shape, dt))

        def sem(name):
            return stack.enter_context(nc.semaphore(name))

        x = sb("x", [P, B, D])
        xTh, xTl = sb("xTh", [P, NC, TOK], F32R), sb("xTl", [P, NC, TOK], F32R)
        cTh, cTl = sb("cTh", [P, NC, TOK], F32R), sb("cTl", [P, NC, TOK], F32R)
        raw = sb("raw", [P, RING, D])
        wth, wtl = sb("wth", [P, WT], F32R), sb("wtl", [P, WT], F32R)
        woh, wol = sb("woh", [P, WO], F32R), sb("wol", [P, WO], F32R)
        tbias = sb("tbias", [P, SLOTS * 8])
        qT = sb("qT", [P, REP, TOK])
        KT = sb("KT", [P, TOK])
        VT = sb("VT", [P, 2, HALF])
        Vh, Vl = sb("Vh", [P, B, HD], F32R), sb("Vl", [P, B, HD], F32R)
        prob = sb("prob", [P, 2, D])
        sm = sb("sm", [P, 2, D])
        m1, m2 = sb("m1", [P, 2, D]), sb("m2", [P, 2, D])
        PTh, PTl = sb("PTh", [P, D], F32R), sb("PTl", [P, D], F32R)
        OTh, OTl = sb("OTh", [P, D], F32R), sb("OTl", [P, D], F32R)
        kvm = sb("kvm", [P, B, P + XH])
        cst = sb("cst", [P, CONSTS])
        row = sb("row", [P, D + NE])
        stats = sb("stats", [P, B, 6])
        mv = sb("mv", [P, B, 2])
        vare = sb("vare", [P, B])
        rstd = sb("rstd", [P, B])
        nmax = sb("nmax", [P, 2, REP])
        nbias = sb("nbias", [P, 2, REP])
        esum = sb("esum", [P, 2, REP])
        rsum = sb("rsum", [P, 2, REP])
        cmax, csum, crs = sb("cmax", [P, B]), sb("csum", [P, B]), sb("crs", [P, B])
        rden = sb("rden", [P, 2, NC, XH])
        shift = sb("shift", [P, B])
        logit, below = sb("logit", [P, HB, NE]), sb("below", [P, HB, NE])
        first, second = sb("first", [P, HB, NE]), sb("second", [P, HB, NE])
        weight = sb("weight", [P, 2, HB, NE])
        best = sb("best", [P, 6, HB])
        keep = sb("keep", [P, HB, LR])

        ps = stack.enter_context(nc.psum_tensor("ps", [P, 8, D], F32))
        pA = [ps[:, 0, :], ps[:, 1, :]]
        pS = [ps[:, 2, :], ps[:, 3, :]]
        pT = [ps[:, 4, :], ps[:, 5, :]]
        pO, pY = ps[:, 6, :], ps[:, 7, :]

        ident = cst[:, C_ID:C_ID + P]
        cosT = cst[:, C_COS:C_COS + P].unsqueeze(1).to_broadcast([P, HB, P])
        causal = cst[:, C_CAUSAL:C_CAUSAL + P].unsqueeze(1).to_broadcast([P, REP, P])

        def four(ap):
            return ap.rearrange("p (a b) -> p a b", a=4)

        const_in, row_in, bias_in = sem("const_in"), sem("row_in"), sem("bias_in")
        x_loaded = [sem(f"x_loaded{b}") for b in range(B)]
        ctx_loaded = [sem(f"ctx_loaded{b}") for b in range(B)]
        raw_in = [sem(f"raw_in{p}") for p in range(RING)]
        t_hi, t_lo = sem("t_hi"), sem("t_lo")
        o_hi, o_lo, o_used = sem("o_hi"), sem("o_lo"), sem("o_used")
        c_set, c_max, c_exp, c_turned = sem("c_set"), sem("c_max"), sem("c_exp"), sem("c_turned")
        c_act, c_low, c_keys, c_copied = (sem("c_" + n) for n in ("act", "low", "keys", "copied"))
        c_kv, c_rs, c_kvm = (sem("c_" + n) for n in ("kv", "rs", "kvm"))
        added, stat_ready, mv_ready, var_ready = sem("added"), sem("stat_ready"), sem("mv_ready"), sem("var_ready")
        shift_ready = sem("shift_ready")
        rstd_ready, normed, xt_turned = sem("rstd_ready"), sem("normed"), sem("xt_turned")
        xt_hi, xt_lo, res_ready = sem("xt_hi"), sem("xt_lo"), sem("res_ready")
        NORMS = [B * k for k in range(6)]
        HALVES = [2 * k for k in range(6)]
        TURNS = {0: 0, 2: B, 3: 2 * B, 4: 3 * B, 5: 4 * B}
        ADDS = {0: 0, 1: B, 2: 2 * B, 5: 3 * B}
        BIASES = {0: 0, 2: B, 4: 2 * B}
        out_done = sem("out_done")

        def load_tile_chunk(sp, s, k):
            sp.dma_start(raw[:, (k + NO) % RING, :], w_tile[bass.ds(s, 1), k].rearrange("a p n -> p (a n)"))\
                .then_inc(raw_in[(k + NO) % RING], 16)

        def load_out_chunk(sp, s, k):
            sp.dma_start(raw[:, k, :], w_out[bass.ds(s, 1), k].rearrange("a p n -> p (a n)")).then_inc(raw_in[k], 16)

        def load_out_part(sp, s):
            for k in range(NO):
                sp.wait_ge(t_lo, s * NT + k + 2)
                load_out_chunk(sp, s, k)

        def load_next_tile_part(sp, s):
            for k in range(NT):
                if k == 0:
                    sp.wait_ge(t_lo, s * NT + NT)
                elif k < NT - 1:
                    sp.wait_ge(o_lo, s * NO + k)
                else:
                    sp.wait_ge(t_lo, s * NT + NT + 1)
                load_tile_chunk(sp, s + 1, k)

        def split_tile_hi(act, s, k, used=None):
            p = (k + NO) % RING
            act.wait_ge(raw_in[p], s * 32 + (32 if k == NT - 1 else 16))
            if used is not None:
                act.wait_ge(*used)
            act.activation(wth[:, k * D:(k + 1) * D], raw[:, p, :], ACT.Copy).then_inc(t_hi, 1)

        def split_tile_lo(pool, s, k):
            c = slice(k * D, (k + 1) * D)
            pool.wait_ge(t_hi, s * NT + k + 1)
            pool.tensor_tensor(wtl[:, c], raw[:, (k + NO) % RING, :], wth[:, c].bitcast(F32), ALU.subtract)\
                .then_inc(t_lo, 1)

        def split_out_hi(act, s, k):
            act.wait_ge(raw_in[k], s * 32 + 32)
            if k == 0 and not (isinstance(s, int) and s == 0):
                act.wait_ge(o_used, s)
            act.activation(woh[:, k * D:(k + 1) * D], raw[:, k, :], ACT.Copy).then_inc(o_hi, 1)

        def split_out_lo(eng, s, k):
            c = slice(k * D, (k + 1) * D)
            eng.wait_ge(o_hi, s * NO + k + 1)
            eng.tensor_tensor(wol[:, c], raw[:, k, :], woh[:, c].bitcast(F32), ALU.subtract).then_inc(o_lo, 1)

        def mm3(pe, o, wh, wl, xh, xl, first, last, before=None):
            mm = pe.matmul(o, wl, xh, start=first, stop=False)
            if before is not None:
                mm.then_inc(before, 1)
            pe.matmul(o, wh, xl, start=False, stop=False)
            return pe.matmul(o, wh, xh, start=False, stop=last)

        def wt_tile(w, c, t):
            return w[:, t * D + c * P:t * D + (c + 1) * P]

        def tile_product(pe, o, t, half, src_h, src_l):
            cols = slice(half * HALF, (half + 1) * HALF)
            for c in range(NC):
                mm = mm3(pe, o, wt_tile(wth, c, t), wt_tile(wtl, c, t), src_h[:, c, cols], src_l[:, c, cols],
                         c == 0, c == NC - 1)
            return mm

        def turn_bank(k, b):
            return (pS if k in (attn.k, xattn.k) and b >= HB else pA)[b % 2]

        def turn_pe(pe, k, b):
            if k == 0:
                pe.wait_ge(x_loaded[b], 16)
            else:
                pe.wait_ge(normed, NORMS[k - 1] + b + 1)
            if b >= 2:
                pe.wait_ge(xt_lo, TURNS[k] + b - 1)
            for c in range(NC):
                t = pe.transpose(turn_bank(k, b)[:, c * P:(c + 1) * P], x[:, b, c * P:(c + 1) * P], ident)
            t.then_inc(xt_turned, 1)

        def turn_act(act, k, b):
            act.wait_ge(xt_turned, TURNS[k] + b + 1)
            act.activation(xTh[:, :, b * P:(b + 1) * P], four(turn_bank(k, b)), ACT.Copy).then_inc(xt_hi, 1)

        def turn_dve(dve, k, b):
            dve.wait_ge(xt_hi, TURNS[k] + b + 1)
            dve.tensor_tensor(xTl[:, :, b * P:(b + 1) * P], four(turn_bank(k, b)),
                              xTh[:, :, b * P:(b + 1) * P].bitcast(F32), ALU.subtract).then_inc(xt_lo, 1)

        def residual_bias(pool, k, b, loads):
            if b == 0:
                pool.wait_ge(row_in, 16 * loads)
            pool.wait_ge(xt_turned, TURNS[k] + b + 1)
            pool.tensor_tensor(x[:, b, :], x[:, b, :], row[:, 0:D], ALU.add).then_inc(res_ready, 1)

        def norm_stats(dve, k, b, summed=None):
            alone = k == 5 and b == B - 1

            def mean_variance(b):
                dve.wait_ge(stat_ready, NORMS[k] + b + 1)
                dve.bn_aggr(mv[:, b, :], stats[:, b, :]).then_inc(mv_ready, 1)

            if b % HB and not alone:
                mean_variance(b - 1)
            dve.wait_ge(*(summed or (added, ADDS[k] + b + 1)))
            dve.bn_stats(stats[:, b, :], x[:, b, :]).then_inc(stat_ready, 1)
            if b % HB == HB - 1 or (k == 5 and b == B - 2):
                mean_variance(b)
                h = slice(b, b + 1) if alone else slice(b // HB * HB, b + 1)
                dve.wait_ge(mv_ready, NORMS[k] + b + 1)
                if k < 2:
                    dve.tensor_scalar(shift[:, h], mv[:, h, 0], -1.0, None, ALU.mult)
                dve.tensor_scalar(vare[:, h], mv[:, h, 1], EPS, None, ALU.add).then_inc(var_ready, 1)

        def norm_pow(pool, k, half):
            h = slice(half * HB, (half + 1) * HB)
            if k == 5 and half:
                h = slice(HB, B - 1) if half == 1 else slice(B - 1, B)
            pool.wait_ge(var_ready, HALVES[k] + half + 1)
            pool.tensor_tensor(rstd[:, h], vare[:, h], cst[:, C_POW:C_POW + h.stop - h.start], ALU.pow).then_inc(rstd_ready, 1)

        def norm_shift(pool, k, half):
            h = slice(half * HB, (half + 1) * HB)
            pool.wait_ge(rstd_ready, HALVES[k] + half + 1)
            pool.tensor_tensor(shift[:, h], shift[:, h], rstd[:, h], ALU.mult).then_inc(shift_ready, 1)

        def norm_apply_act(act, k, bs):
            for b in bs:
                if b % HB == 0:
                    act.wait_ge(shift_ready, HALVES[k] + b // HB + 1)
                act.activation(x[:, b, :], x[:, b, :], ACT.Identity, bias=shift[:, b:b + 1], scale=rstd[:, b:b + 1])\
                    .then_inc(normed, 1)

        def norm_apply(dve, k, half, bs=None):
            dve.wait_ge(rstd_ready, HALVES[k] + half + 1)
            bs = bs or range(half * HB, (half + 1) * HB)
            if k == 5 and half:
                bs = range(HB, B - 1) if half == 1 else [B - 1]
            for b in bs:
                dve.tensor_scalar(x[:, b, :], x[:, b, :], mv[:, b, 0:1], rstd[:, b:b + 1], ALU.subtract, ALU.mult)\
                    .then_inc(normed, 1)

        class Softmax:
            def __init__(self, name, causal=False):
                self.scores = sem(name + "_scores")
                self.masked = sem(name + "_masked") if causal else None
                self.max = sem(name + "_max")
                self.bias = sem(name + "_bias")
                self.exp = sem(name + "_exp")
                self.recip = sem(name + "_recip")
                self.prob = sem(name + "_prob")

        def soft_max(dve, sf, u, n):
            dve.wait_ge(sf.scores, u + 1)
            dve.tensor_reduce(nmax[:, n, :], four(pS[n]), AX.X, ALU.max, negate=True).then_inc(sf.max, 1)
            dve.wait_ge(sf.max, u + 1)
            dve.tensor_scalar(nbias[:, n, :], nmax[:, n, :], SCALE, None, ALU.mult).then_inc(sf.bias, 1)

        def soft_exp(act, sf, u, n):
            act.wait_ge(sf.bias, u + 1)
            for h in range(4):
                c = slice(h * P, (h + 1) * P)
                a = act.activation(prob[:, n, c], pS[n][:, c], ACT.Exp, bias=nbias[:, n, h:h + 1],
                                   scale=SCALE, accum_out=esum[:, n, h:h + 1])
            a.then_inc(sf.exp, 1)

        def soft_recip(dve, sf, u, n):
            dve.wait_ge(sf.exp, u + 1)
            dve.reciprocal(rsum[:, n, :], esum[:, n, :]).then_inc(sf.recip, 1)

        def soft_norm(pool, sf, u, n):
            pool.wait_ge(sf.recip, u + 1)
            pool.tensor_tensor(four(prob[:, n, :]), four(prob[:, n, :]),
                               rsum[:, n, :].unsqueeze(2).to_broadcast([P, 4, P]), ALU.mult).then_inc(sf.prob, 1)

        l0 = Softmax("l0")
        a_ready, a_free = sem("l0_tile_ready"), sem("l0_tile_copied")
        l0_vturned, l0_vcopied = sem("l0_vturned"), sem("l0_vcopied")
        l0_pturned, l0_pcopied = sem("l0_pturned"), sem("l0_pcopied")
        l0_o, l0_ohi, l0_olo, l0_y = sem("l0_o"), sem("l0_ohi"), sem("l0_olo"), sem("l0_y")
        L0_TILES = [(t, half) for half in range(2) for t in (L0_K, L0_Q, L0_V)]

        def l0_bank(j):
            return pY if j < 3 else pA[j % 2]

        def l0_dst(t, half):
            c = slice(half * HALF, (half + 1) * HALF)
            return {L0_K: KT[:, c], L0_V: VT[:, half, :], L0_Q: qT[:, 0, c]}[t]

        x2_exp, x2_num, x2_rden = sem("x2_exp"), sem("x2_num"), sem("x2_rden")
        x2_mul, x2_turned = sem("x2_mul"), sem("x2_turned")

        f_ah, f_acopied, f_aturned, f_hm = (sem("f_" + n) for n in ("ah", "acopied", "aturned", "hm"))
        f_step = sem("f_step")
        f_turned, f_hi, f_lo, f_y = (sem("f_" + n) for n in ("turned", "hi", "lo", "y"))

        e_gate, e_gcopied, e_gturned = sem("e_gate"), sem("e_gcopied"), sem("e_gturned")
        e_up, e_diff, e_exp, e_hw = (sem("e_" + n) for n in ("up", "diff", "exp", "hw"))
        GATE_BANK = [pT[0], pA[0]]
        e_step = sem("e_step")
        e_scale = sem("e_scale")
        e_turned, e_hi, e_lo, e_y = (sem("e_" + n) for n in ("turned", "hi", "lo", "y"))

        def narrow_product(pe, bank, half, w0, n):
            xc = slice(half * HALF, (half + 1) * HALF)
            for c in range(NC):
                w = slice(w0 + c * P, w0 + c * P + n)
                mm = mm3(pe, bank[0:n, :], wth[:, w], wtl[:, w], xTh[:, c, xc], xTl[:, c, xc], c == 0, c == NC - 1)
            return mm

        def narrow_turn(pe, bank, half, n):
            for j in range(HB):
                t = pe.transpose(bank[:, j * P:j * P + n], prob[0:n, half, j * P:(j + 1) * P], ident[0:n, 0:n])
            return t

        def narrow_copy(act, bank, half, n):
            return act.activation(prob[0:n, half, :], bank[0:n, :], ACT.Copy)

        def cast4(ap, n):
            return ap.unsqueeze(2).to_broadcast([P, HB, n])

        def of_all(c, n):
            return cst[:, c:c + n].unsqueeze(1).to_broadcast([P, HB, n])

        def halves_of(bufs, half, rows=P):
            return bufs[2 * half][0:rows, :], bufs[2 * half + 1][0:rows, :]

        down_bufs = [PTh, PTl, OTh, OTl]

        def e_gates(pe, half):
            pe.wait_ge(xt_lo, TURNS[5] + (half + 1) * HB)
            if half == 0:
                pe.wait_ge(t_lo, SLOTS * NT)
            narrow_product(pe, GATE_BANK[half], half, NC * D, NE).then_inc(e_gate, 1)

        def e_gates_turn(pe, half):
            pe.wait_ge(e_gcopied, half + 1)
            narrow_turn(pe, GATE_BANK[half], half, NE).then_inc(e_gturned, 1)

        def e_gates_copy(act, half):
            act.wait_ge(e_gate, half + 1)
            narrow_copy(act, GATE_BANK[half], half, NE).then_inc(e_gcopied, 1)

        def e_hidden(pe, b):
            pe.wait_ge(xt_lo, TURNS[5] + b + 1)
            if b >= 2:
                pe.wait_ge(e_hw, b - 1)
            xc = slice(b * P, (b + 1) * P)
            for c in range(NC):
                w = slice(c * D, (c + 1) * D)
                mm = mm3(pe, pS[b % 2], xTh[:, c, xc], xTl[:, c, xc], wth[:, w], wtl[:, w], c == 0, c == NC - 1,
                         o_used if b == 1 and c == 0 else None)
            mm.then_inc(e_up, 1)

        def e_exps(act, half):
            act.wait_ge(e_diff, half + 1)
            act.activation(logit[:, :, :], logit[:, :, :], ACT.Exp).then_inc(e_exp, 1)

        def e_choose(dve, half):
            s0 = 14 * half
            lg = logit[:, :, :]
            bank = GATE_BANK[half].rearrange("p (j n) -> p j n", j=HB)[:, :, 0:NE]

            def first_best(n, src, one_hot, top, index):
                dve.tensor_reduce(top, src, AX.X, ALU.max).then_inc(e_step, 1)
                dve.wait_ge(e_step, n + 1)
                dve.tensor_tensor(below[:, :, :], src, cast4(top, NE), ALU.is_lt).then_inc(e_step, 1)
                dve.wait_ge(e_step, n + 2)
                dve.scalar_tensor_tensor(below[:, :, :], below[:, :, :], float(NE), of_all(C_IOTA, NE),
                                         ALU.mult, ALU.add).then_inc(e_step, 1)
                dve.wait_ge(e_step, n + 3)
                dve.tensor_reduce(index, below[:, :, :], AX.X, ALU.min).then_inc(e_step, 1)
                dve.wait_ge(e_step, n + 4)
                dve.tensor_tensor(one_hot, of_all(C_IOTA, NE), cast4(index, NE), ALU.is_equal).then_inc(e_step, 1)
                dve.wait_ge(e_step, n + 5)

            dve.wait_ge(e_gturned, half + 1)
            dve.tensor_reduce(best[:, 0, :], bank, AX.X, ALU.max, negate=True).then_inc(e_step, 1)
            dve.wait_ge(e_step, s0 + 1)
            dve.tensor_tensor(lg, bank, cast4(best[:, 0, :], NE), ALU.add).then_inc(e_diff, 1)
            dve.wait_ge(e_exp, half + 1)
            first_best(s0 + 1, lg, first[:, :, :], best[:, 1, :], best[:, 2, :])
            dve.scalar_tensor_tensor(second[:, :, :], first[:, :, :], -4.0, lg, ALU.mult, ALU.add)\
                .then_inc(e_step, 1)
            dve.wait_ge(e_step, s0 + 7)
            first_best(s0 + 7, second[:, :, :], second[:, :, :], best[:, 3, :], best[:, 4, :])
            dve.tensor_tensor(best[:, 5, :], best[:, 1, :], best[:, 3, :], ALU.add).then_inc(e_step, 1)
            dve.tensor_tensor(first[:, :, :], first[:, :, :], second[:, :, :], ALU.add).then_inc(e_step, 1)
            dve.wait_ge(e_step, s0 + 14)
            dve.reciprocal(best[:, 5, :], best[:, 5, :]).then_inc(e_scale, 1)
            dve.tensor_tensor(lg, lg, first[:, :, :], ALU.mult).then_inc(e_scale, 1)
            dve.wait_ge(e_scale, 3 * half + 2)
            dve.tensor_tensor(weight[:, half, :, :], lg, cast4(best[:, 5, :], NE), ALU.mult).then_inc(e_scale, 1)

        class Grouped:

            def __init__(self, name, slot, k, cross):
                self.slot, self.k, self.cross = slot, k, cross
                self.soft = Softmax(name, causal=not cross)
                self.tile_ready = sem(name + "_tile_ready")
                self.rope_m = None if cross else sem(name + "_rope_m")
                self.tile_done = sem(name + "_tile_done")
                self.vt = None if cross else sem(name + "_vt")
                self.turned = sem(name + "_turned")
                self.t_hi, self.t_lo = sem(name + "_t_hi"), sem(name + "_t_lo")
                self.o, self.o_hi, self.o_lo = sem(name + "_o"), sem(name + "_o_hi"), sem(name + "_o_lo")
                self.y = sem(name + "_y")
                self.y_added = sem(name + "_y_added")

        attn = Grouped("ga", SLOT_ATTN, 3, False)
        xattn = Grouped("gx", SLOT_XATTN, 4, True)
        TILES_OF = 2 * NT
        TURNS_AFTER = {3: (4, 5), 4: (6, 7)}
        NR = TILES_OF - 2
        NU = 2 + B
        STEP_TILES = [[0, 1, 2], [3, 4], [5], [6], [7], [8], [9], [10, 11]]
        def use(b):
            return b + 1 if b < 5 else b + 2
        V1_USE = 6

        def rope_index(j):
            return NR // 2 + j - (j > 5)

        def tile_dst(t, half):
            c = slice(half * HALF, (half + 1) * HALF)
            return KT[:, c] if t == K_TILE else VT[:, half, :] if t == V_TILE else qT[:, t - 1, c]

        def tile_evacuated(g, i, j):
            if g.cross:
                return g.tile_done, i * TILES_OF + NT + j + 1
            if j % NT == V_TILE:
                return g.vt, i * 2 + (2 if j < NT else 3)
            return g.rope_m, i * NR + rope_index(j) + 1

        def pe_first_tile(pe, g, k):
            pe.wait_ge(t_lo, g.slot * NT + k + 1)
            if k == (1 if g.cross else 0):
                pe.wait_ge(xt_lo, TURNS[g.k] + HB)
            if k >= 2:
                pe.wait_ge(g.tile_done if g.cross else g.rope_m, k - 1)
            sh, sl = (cTh, cTl) if g.cross and k in (K_TILE, V_TILE) else (xTh, xTl)
            tile_product(pe, pA[k % 2], k, 0, sh, sl).then_inc(g.tile_ready, 1)

        def pe_first(pe, g, tiles):
            for k in tiles:
                pe_first_tile(pe, g, k)

        def pe_rest(pe, g, tiles):
            for k in tiles:
                pe_first(pe, g, [k])
                for b in TURNS_AFTER.get(k, ()):
                    turn_pe(pe, g.k, b)

        def g_pe(pe, g, i, last, nxt):
            sf = g.soft

            def tile(j):
                t, half = j % NT, 0 if j >= NT else 1
                if j >= NT:
                    pe.wait_ge(t_lo, i * NT + (g.slot + 1) * NT + t + 1)
                if j >= 2:
                    pe.wait_ge(*tile_evacuated(g, i, j - 2))
                sh, sl = (cTh, cTl) if g.cross and t in (K_TILE, V_TILE) else (xTh, xTl)
                tile_product(pe, pA[j % 2], t, half, sh, sl).then_inc(g.tile_ready, 1)

            def tiles(n):
                for j in STEP_TILES[n]:
                    if not (last and j >= NT):
                        tile(j)

            def turn(n, src):
                for j in range(4):
                    t = pe.transpose(pT[n % 2][:, j * P:(j + 1) * P], src[:, j * P:(j + 1) * P], ident)
                t.then_inc(g.turned, 1)

            def turn_v(half):
                pe.wait_ge(*tile_evacuated(g, i, V_TILE - NT + half * NT)
                           if half or g.cross else (g.vt, i * 2 + 1))
                turn(V1_USE if half else 0, VT[:, half, :])

            def turn_p(b):
                pe.wait_ge(sf.prob, i * B + b + 1)
                turn(use(b), prob[:, b % 2, :])

            def scores(b):
                if g.cross:
                    pe.wait_ge(g.tile_done, i * TILES_OF + (NT if b >= HB else 0) + NT - 1)
                else:
                    pe.wait_ge(g.tile_done, i * NR + (NR if b >= HB else NR // 2))
                for h in range(REP):
                    mm = pe.matmul(pS[b % 2][:, h * P:(h + 1) * P], qT[:, h, b * P:(b + 1) * P],
                                   KT[:, b * P:(b + 1) * P], start=True, stop=True)
                    if b == 0 and h == 0:
                        mm.then_inc(o_used, 1)
                mm.then_inc(sf.scores, 1)

            def values(b):
                n = V1_USE if b == HB else use(b)
                pe.wait_ge(g.t_lo, i * NU + n + 1)
                mm3(pe, pO, Vh[:, b, :], Vl[:, b, :], PTh[:, :], PTl[:, :], True, True).then_inc(g.o, 1)

            def project(b):
                if b == 0:
                    pe.wait_ge(o_lo, i * NO + (g.slot + 1) * NO)
                pe.wait_ge(g.o_lo, i * B + b + 1)
                pe.wait_ge(g.y_added, i * B + b + 1)
                for h in range(REP):
                    c = slice(h * P, (h + 1) * P)
                    w = slice(h * D, (h + 1) * D)
                    mm = mm3(pe, pY, OTh[:, c], OTl[:, c], woh[:, w], wol[:, w], h == 0, h == REP - 1)
                mm.then_inc(g.y, 1)

            pe.wait_ge(xt_lo, TURNS[g.k] + B)
            scores(0)
            scores(1)
            tile(0)
            turn_v(0)
            tile(1)
            turn_p(0)
            tile(2)
            values(0)
            for b in range(1, B):
                if b < B - 1:
                    scores(b + 1)
                turn_p(b)
                if b == HB:
                    turn_v(1)
                if b < B - 1:
                    tiles(b)
                    if last and b == HB and not g.cross:
                        pe_first(pe, nxt[1], [0])
                    if last and b == 6:
                        if not g.cross:
                            pe.wait_ge(nxt[1].tile_done, 1)
                        turn_pe(pe, nxt[0], 0)
                        turn_pe(pe, nxt[0], 1)
                    project(b - 1)
                elif not last:
                    tile(10)
                    project(b - 1)
                else:
                    turn_pe(pe, nxt[0], 2)
                    turn_pe(pe, nxt[0], 3)
                    project(b - 1)
                values(b)
            if not last:
                tile(11)
            elif g.cross:
                e_gates(pe, 0)
            else:
                pe_first(pe, nxt[1], [1])
            project(B - 1)
            if last and nxt[1] is not None:
                pe_rest(pe, nxt[1], range(2, NT))

        def act_evacuate(act, g, t, half, bank, n, bias=None):
            act.wait_ge(g.tile_ready, n)
            if g.cross:
                act.activation(tile_dst(t, half), bank, ACT.Identity, bias=bias).then_inc(g.tile_done, 1)
            else:
                act.activation(tile_dst(t, half), bank, ACT.Copy).then_inc(g.vt, 1)

        def act_first(act, g, tiles):
            for k in tiles:
                if g.cross or k == V_TILE:
                    c = g.slot * 8 + k
                    act_evacuate(act, g, k, 0, pA[k % 2], k + 1, tbias[:, c:c + 1])

        def act_rest(act, g, tiles):
            for k in tiles:
                act_first(act, g, [k])
                for b in TURNS_AFTER.get(k, ()):
                    turn_act(act, g.k, b)

        def g_act(act, g, i, last, nxt):
            sf = g.soft

            def evacuate(j):
                t = j % NT
                if (last and j >= NT) or not (g.cross or t == V_TILE):
                    return
                c = i * 8 + ((g.slot + j // NT) * 8 + t)
                act_evacuate(act, g, t, 0 if j >= NT else 1, pA[j % 2], i * TILES_OF + (NT + j + 1),
                             tbias[:, bass.ds(c, 1)])

            def split_high(n, o):
                act.wait_ge(g.turned, i * NU + n + 1)
                act.activation(o, four(pT[n % 2]), ACT.Copy).then_inc(g.t_hi, 1)

            def split_v(half):
                split_high(V1_USE if half else 0, Vh[:, half * HB:(half + 1) * HB, :])

            def exps(b):
                n = b % 2
                if b >= 2:
                    act.wait_ge(g.turned, i * NU + use(b - 2) + 1)
                act.wait_ge(sf.bias, i * B + b + 1)
                for h in range(REP):
                    c = slice(h * P, (h + 1) * P)
                    src = pS[n][:, c] if g.cross else sm[:, n, c]
                    a = act.activation(prob[:, n, c], src, ACT.Exp, bias=nbias[:, n, h:h + 1],
                                       scale=SCALE, accum_out=esum[:, n, h:h + 1])
                a.then_inc(sf.exp, 1)

            def next_tile(k):
                split_tile_hi(act, i + (g.slot + 1), k, (g.tile_ready, i * TILES_OF + (NT + k + 1)))

            def out_chunks(ks):
                for k in ks:
                    split_out_hi(act, i + g.slot, k)

            out_chunks([0, 1])
            exps(0)
            evacuate(0)
            exps(1)
            split_v(0)
            evacuate(1)
            out_chunks([2, 3])
            split_high(use(0), four(PTh[:, :]))
            evacuate(2)
            next_tile(0)
            for b in range(B):
                if b:
                    split_high(use(b), four(PTh[:, :]))
                    if b == HB:
                        split_v(1)
                    if b < B - 1:
                        exps(b + 1)
                        for j in STEP_TILES[b]:
                            evacuate(j)
                        if b < NT:
                            next_tile(b)
                        if last and b == HB and not g.cross:
                            act_first(act, nxt[1], [0])
                        if last and b == 6:
                            turn_act(act, nxt[0], 0)
                            turn_act(act, nxt[0], 1)
                    else:
                        evacuate(10)
                        if last:
                            turn_act(act, nxt[0], 2)
                            turn_act(act, nxt[0], 3)
                act.wait_ge(g.o, i * B + b + 1)
                act.activation(OTh[:, :], pO, ACT.Copy).then_inc(g.o_hi, 1)
            evacuate(11)
            if last and g.cross:
                e_gates_copy(act, 0)
                e_exps(act, 0)
            if last and nxt[1] is not None:
                act_rest(act, nxt[1], range(1, NT))

        def dve_rope(dve, g, bank, ready, r, added_before):
            n = r % 2
            dve.wait_ge(g.tile_ready, ready)
            if added_before is not None:
                dve.wait_ge(g.tile_done, added_before)
            dve.tensor_tensor(four(m1[:, n, :]), four(bank), cosT, ALU.mult)
            for a in range(2):
                s, d = slice((1 - a) * 64, (2 - a) * 64), slice(a * 64, a * 64 + 64)
                sn = cst[s, C_SIN:C_SIN + P].unsqueeze(1).to_broadcast([64, HB, P])
                op = dve.tensor_tensor(four(m2[d, n, :]), four(bank[s, :]), sn, ALU.mult)
            op.then_inc(g.rope_m, 1)

        def dve_first(dve, g, tiles):
            for k in tiles:
                if not g.cross and k != V_TILE:
                    dve_rope(dve, g, pA[k % 2], k + 1, k, k - 1 if k >= 2 else None)

        def g_dve(dve, g, i, last, nxt):
            sf = g.soft

            def rope(j):
                if not (last and j >= NT) and not g.cross and j % NT != V_TILE:
                    r = rope_index(j)
                    dve_rope(dve, g, pA[j % 2], i * TILES_OF + (NT + j + 1), r, i * NR + (r - 1))

            def split_low(n, o, hi):
                dve.wait_ge(g.t_hi, i * NU + n + 1)
                dve.tensor_tensor(o, four(pT[n % 2]), hi.bitcast(F32), ALU.subtract).then_inc(g.t_lo, 1)

            def split_v(half):
                h = slice(half * HB, (half + 1) * HB)
                split_low(V1_USE if half else 0, Vl[:, h, :], Vh[:, h, :])

            def split_p(b):
                split_low(use(b), four(PTl[:, :]), four(PTh[:, :]))

            def out_low(b):
                dve.wait_ge(g.o_hi, i * B + b + 1)
                dve.tensor_tensor(OTl[:, :], pO, OTh[:, :].bitcast(F32), ALU.subtract).then_inc(g.o_lo, 1)

            def add(b):
                dve.wait_ge(g.y, i * B + b + 1)
                if g.cross:
                    dve.wait_ge(res_ready, BIASES[g.k] + b + 1)
                dve.tensor_tensor(x[:, b, :], pY, x[:, b, :], ALU.add).then_inc(g.y_added, 1)
                if last:
                    norm_stats(dve, g.k, b, (g.y_added, (GROUPS - 1) * B + b + 2))

            def maxima(b):
                n = b % 2
                dve.wait_ge(sf.scores, i * B + b + 1)
                src = four(pS[n])
                if not g.cross:
                    dve.tensor_tensor(four(sm[:, n, :]), src, causal, ALU.add).then_inc(sf.masked, 1)
                    dve.wait_ge(sf.masked, i * B + b + 1)
                    src = four(sm[:, n, :])
                dve.tensor_reduce(nmax[:, n, :], src, AX.X, ALU.max, negate=True).then_inc(sf.max, 1)
                dve.wait_ge(sf.max, i * B + b + 1)
                dve.tensor_scalar(nbias[:, n, :], nmax[:, n, :], SCALE, None, ALU.mult).then_inc(sf.bias, 1)

            def recip(b):
                dve.wait_ge(sf.exp, i * B + b + 1)
                dve.reciprocal(rsum[:, b % 2, :], esum[:, b % 2, :]).then_inc(sf.recip, 1)

            def out_chunks(ks):
                for k in ks:
                    split_out_lo(dve, i + g.slot, k)

            def turns(bs):
                for b in bs:
                    turn_dve(dve, nxt[0], b)

            maxima(0)
            maxima(1)
            recip(0)
            rope(0)
            recip(1)
            split_v(0)
            rope(1)
            split_p(0)
            out_chunks([0, 1])
            rope(2)
            out_chunks([2, 3])
            for b in range(1, B):
                out_low(b - 1)
                if b < B - 1:
                    maxima(b + 1)
                split_p(b)
                if b == HB:
                    split_v(1)
                if b < B - 1:
                    recip(b + 1)
                    for j in STEP_TILES[b]:
                        rope(j)
                    if last and b == 6:
                        turns((0, 1))
                        norm_apply(dve, g.k, 0, (2, 3))
                    add(b - 1)
                    if last and b == 5:
                        norm_apply(dve, g.k, 0, (0, 1))
                else:
                    if last:
                        turns((2, 3))
                    add(b - 1)
                    rope(10)
            out_low(B - 1)
            add(B - 1)
            if last and g.cross:
                e_choose(dve, 0)
            if last and nxt[1] is not None:
                norm_apply(dve, g.k, 1)
                turns(range(HB, B))

        def pool_rope(pool, g, t, half, r, value):
            pool.wait_ge(g.rope_m, value)
            pool.tensor_tensor(tile_dst(t, half), m1[:, r % 2, :], m2[:, r % 2, :], ALU.add).then_inc(g.tile_done, 1)

        def pool_first(pool, g, tiles):
            for k in tiles:
                if not g.cross and k != V_TILE:
                    pool_rope(pool, g, k, 0, k, k + 1)

        def g_pool(pool, g, i, last, nxt):
            sf = g.soft

            def rope(j):
                if not (last and j >= NT) and not g.cross and j % NT != V_TILE:
                    r = rope_index(j)
                    pool_rope(pool, g, j % NT, 0 if j >= NT else 1, r, i * NR + (r + 1))

            def norm(b):
                n = b % 2
                pool.wait_ge(sf.recip, i * B + b + 1)
                pool.tensor_tensor(four(prob[:, n, :]), four(prob[:, n, :]),
                                   rsum[:, n, :].unsqueeze(2).to_broadcast([P, 4, P]), ALU.mult).then_inc(sf.prob, 1)

            norm(0)
            rope(0)
            norm(1)
            rope(1)
            rope(2)
            split_tile_lo(pool, i + (g.slot + 1), 0)
            for b in range(1, B):
                if b < B - 1:
                    norm(b + 1)
                for j in STEP_TILES[b]:
                    rope(j)
                if b < NT:
                    split_tile_lo(pool, i + (g.slot + 1), b)
                if last and b == HB:
                    norm_pow(pool, g.k, 0)
            if last:
                norm_pow(pool, g.k, 1)

        def grouped(eng, one, g, nxt):
            with eng.Fori(0, GROUPS - 1) as i:
                one(eng, g, i, False, None)
            one(eng, g, GROUPS - 1, True, nxt)

        ctx_raw = qT[:, :, :].rearrange("p h t -> p (h t)").rearrange("p (b d) -> p b d", b=B)
        block = stack.enter_context(nc.Block())

        @block.sync
        def _(sp):
            sp.dma_start(ctx_raw[:, 0, :], ctx_in[0]).then_inc(ctx_loaded[0], 16)
            sp.dma_start(cst[:, C_ID:C_ID + P], consts[:, C_ID:C_ID + P]).then_inc(const_in, 16)
            for b in range(B):
                if b:
                    sp.dma_start(ctx_raw[:, b, :], ctx_in[b]).then_inc(ctx_loaded[b], 16)
                sp.dma_start(x[:, b, :], x_in[b]).then_inc(x_loaded[b], 16)
                if b == 0:
                    sp.dma_start(cst[:, C_COS:CONSTS], consts[:, C_COS:CONSTS]).then_inc(const_in, 16)
                if b < NT - 1:
                    load_tile_chunk(sp, 0, b)
                if b == 2:
                    sp.dma_start(tbias[:, :], biases).then_inc(bias_in, 16)
            sp.wait_ge(t_lo, 1)
            load_tile_chunk(sp, 0, NT - 1)
            sp.dma_start(row[:, 0:D], rows[R_BO0:R_BO0 + D].partition_broadcast(P)).then_inc(row_in, 16)
            sp.dma_start(row[:, D:D + NE], rows[R_GATE:R_GATE + NE].partition_broadcast(P)).then_inc(row_in, 16)
            with sp.Fori(0, SLOTS - 1) as s:
                load_out_part(sp, s)
                load_next_tile_part(sp, s)
            load_out_part(sp, SLOTS - 1)
            for b in range(B):
                sp.wait_ge(normed, NORMS[5] + b + 1)
                sp.dma_start(out[b], x[:, b, :]).then_inc(out_done, 16)
            sp.wait_ge(out_done, 16 * B)

        @block.tensor
        def _(pe):
            pe.wait_ge(const_in, 16)

            def ctx_turn(b):
                pe.wait_ge(c_exp, b + 1)
                if b >= 2:
                    pe.wait_ge(c_keys, b - 1)
                    pe.wait_ge(c_low, b - 1)
                for c in range(NC):
                    cc = slice(c * P, (c + 1) * P)
                    pe.transpose(pT[b % 2][:, cc], prob[:, b % 2, cc], ident)
                    t = pe.transpose(pS[b % 2][:, cc], ctx_raw[:, b, cc], ident)
                t.then_inc(c_turned, 1)

            def ctx_kv(b):
                pe.wait_ge(c_keys, b + 1)
                pe.wait_ge(c_copied, b + 1)
                if b:
                    pe.wait_ge(c_kvm, b)
                for c in range(NC):
                    cc = slice(c * P, (c + 1) * P)
                    mm = pe.matmul(pO[:, 0:P], sm[:, b % 2, cc], m1[:, b % 2, cc], start=(c == 0), stop=(c == NC - 1))
                mm.then_inc(c_kv, 1)

            def l0_tile(j):
                t, half = L0_TILES[j]
                pe.wait_ge(t_lo, t + 1)
                pe.wait_ge(xt_lo, TURNS[0] + HB * (half + 1) if j < 3 else B)
                if j in (1, 2) or j >= 5:
                    pe.wait_ge(a_free, j if j < 5 else j - 1)
                tile_product(pe, l0_bank(j), t, half, xTh, xTl).then_inc(a_ready, 1)

            def l0_scores(half):
                pe.wait_ge(a_free, 3 * half + 2)
                if half == 0:
                    pe.wait_ge(c_kvm, B)
                for j in range(HB):
                    b = half * HB + j
                    mm = pe.matmul(pS[half][:, j * P:(j + 1) * P], qT[:, 0, b * P:(b + 1) * P],
                                   KT[:, b * P:(b + 1) * P], start=True, stop=True)
                mm.then_inc(l0.scores, 1)

            def l0_vturn(half):
                pe.wait_ge(a_free, half * 3 + 3)
                for j in range(HB):
                    t = pe.transpose(pT[half][:, j * P:(j + 1) * P], VT[:, half, j * P:(j + 1) * P], ident)
                t.then_inc(l0_vturned, 1)

            def l0_pturn(half):
                pe.wait_ge(l0.prob, half + 1)
                pe.wait_ge(l0_vcopied, half + 1)
                for j in range(HB):
                    t = pe.transpose(pT[half][:, j * P:(j + 1) * P], prob[:, half, j * P:(j + 1) * P], ident)
                t.then_inc(l0_pturned, 1)

            def l0_values(half):
                pe.wait_ge(l0_pcopied, half + 1)
                if half:
                    pe.wait_ge(l0_olo, half)
                for j in range(HB):
                    c = slice(j * P, (j + 1) * P)
                    mm = pe.matmul(pO[:, c], m1[:, half, c], sm[:, half, c], start=True, stop=True)
                mm.then_inc(l0_o, 1)

            def l0_project(half, j):
                b = half * HB + j
                c, w = slice(j * P, (j + 1) * P), slice(L0_OUT * D, (L0_OUT + 1) * D)
                pe.wait_ge(l0_olo, half + 1)
                if b == 0:
                    pe.wait_ge(t_lo, L0_OUT + 1)
                    pe.wait_ge(a_free, 2 * 3)
                if b >= 2:
                    pe.wait_ge(added, ADDS[0] + b - 1)
                mm3(pe, pA[b % 2], OTh[:, c], OTl[:, c], wth[:, w], wtl[:, w], True, True).then_inc(l0_y, 1)

            for b in range(B):
                turn_pe(pe, 0, b)
                ctx_turn(b)
                if b:
                    ctx_kv(b - 1)
                if HB <= b < HB + 3:
                    l0_tile(b - HB)
            ctx_kv(B - 1)
            l0_tile(3)
            l0_scores(0)
            l0_vturn(0)
            l0_tile(4)
            l0_pturn(0)
            l0_tile(5)
            l0_values(0)
            l0_scores(1)
            l0_vturn(1)
            l0_project(0, 0)
            l0_project(0, 1)
            l0_project(0, 2)
            l0_pturn(1)
            l0_project(0, 3)
            l0_values(1)
            for j in range(HB):
                l0_project(1, j)

            def x2_product(b):
                pe.wait_ge(x2_exp, b + 1)
                if b >= 2:
                    pe.wait_ge(x2_mul, 2 * (b - 1))
                pair = 2 + 2 * (b % 2)
                for c in range(NC):
                    o = ps[:, pair + c // 2, (c % 2) * (P + XH):(c % 2 + 1) * (P + XH)]
                    mm = pe.matmul(o, prob[:, b % 2, c * P:(c + 1) * P], kvm[:, b, :], start=True, stop=True)
                mm.then_inc(x2_num, 1)

            def x2_turn(b):
                pe.wait_ge(x2_mul, 2 * (b + 1))
                if b >= 2:
                    pe.wait_ge(added, ADDS[1] + b - 1)
                for c in range(NC):
                    t = pe.transpose(ps[:, 6 + b % 2, c * P:(c + 1) * P], m2[:, b % 2, c * P:(c + 1) * P], ident)
                t.then_inc(x2_turned, 1)

            for b in range(B):
                x2_product(b)
                if b == B - 1:
                    turn_pe(pe, 2, 0)
                    turn_pe(pe, 2, 1)
                if b:
                    x2_turn(b - 1)
            turn_pe(pe, 2, 2)
            turn_pe(pe, 2, 3)
            x2_turn(B - 1)

            UP = [pS[0], pS[1], pO, pY]
            pe.wait_ge(t_lo, NT)
            pe.wait_ge(o_lo, NO)

            def f_ranks(half):
                pe.wait_ge(xt_lo, TURNS[2] + (half + 1) * HB)
                narrow_product(pe, pT[half], half, L0_RANKS * D, LR + NE0).then_inc(f_ah, 1)

            def f_ranks_turn(half):
                pe.wait_ge(f_acopied, half + 1)
                narrow_turn(pe, pT[half], half, LR + NE0).then_inc(f_aturned, 1)

            def f_up(b):
                pe.wait_ge(xt_lo, TURNS[2] + b + 1)
                if b >= 4:
                    pe.wait_ge(added, ADDS[2] + b - 3)
                xc = slice(b * P, (b + 1) * P)
                for c in range(NC):
                    w = slice(c * D, (c + 1) * D)
                    mm3(pe, UP[b % 4], xTh[:, c, xc], xTl[:, c, xc], woh[:, w], wol[:, w], c == 0, False)

            def f_turn(half):
                pe.wait_ge(f_hm, half + 1)
                for j in range(HB):
                    t = pe.transpose(pT[half][0:LR, j * P:(j + 1) * P], m1[:, half, j * LR:(j + 1) * LR], ident)
                t.then_inc(f_turned, 1)

            def f_down(b):
                pe.wait_ge(f_lo, b // HB + 1)
                c, w = slice((b % HB) * P, (b % HB + 1) * P), slice(L0_B * D, (L0_B + 1) * D)
                th, tl = halves_of(down_bufs, b // HB, LR)
                mm3(pe, UP[b % 4], th[:, c], tl[:, c], wth[0:LR, w], wtl[0:LR, w], False, True).then_inc(f_y, 1)

            f_ranks(0)
            f_up(0)
            f_ranks_turn(0)
            f_up(1)
            turn_pe(pe, 2, 4)
            turn_pe(pe, 2, 5)
            f_turn(0)
            turn_pe(pe, 2, 6)
            turn_pe(pe, 2, 7)
            for b in range(B):
                if b == HB:
                    f_turn(1)
                if b < B - 2:
                    f_up(b + 2)
                if b == 0:
                    f_ranks(1)
                if b == 1:
                    f_ranks_turn(1)
                if b >= B - 2:
                    for c in (0, 1) if b == B - 2 else (2, 3):
                        turn_pe(pe, attn.k, c)
                f_down(b)

            pe_rest(pe, attn, range(NT))
            grouped(pe, g_pe, attn, (xattn.k, xattn))
            grouped(pe, g_pe, xattn, (5, None))

            def e_turn(b):
                pe.wait_ge(e_hw, b + 1)
                if b >= 2:
                    pe.wait_ge(e_lo, b - 1)
                for c in range(NC):
                    t = pe.transpose(pT[b % 2][:, c * P:(c + 1) * P], m1[:, b % 2, c * P:(c + 1) * P], ident)
                t.then_inc(e_turned, 1)

            def e_down(b):
                pe.wait_ge(e_lo, b + 1)
                if b >= 2:
                    pe.wait_ge(added, ADDS[5] + b - 1)
                th, tl = halves_of(down_bufs, b % 2)
                for c in range(NC):
                    cc, w = slice(c * P, (c + 1) * P), slice(c * D, (c + 1) * D)
                    mm = mm3(pe, ps[:, 6 + b % 2, :], th[:, cc], tl[:, cc], woh[:, w], wol[:, w], c == 0, c == NC - 1)
                mm.then_inc(e_y, 1)

            e_gates_turn(pe, 0)
            e_hidden(pe, 0)
            e_hidden(pe, 1)
            e_turn(0)
            e_hidden(pe, 2)
            turn_pe(pe, 5, 4)
            turn_pe(pe, 5, 5)
            e_turn(1)
            turn_pe(pe, 5, 6)
            turn_pe(pe, 5, 7)
            e_hidden(pe, 3)
            e_gates(pe, 1)
            pe.wait_ge(o_lo, SLOTS * NO)
            e_down(0)
            for b in range(1, B):
                if b < B - 1:
                    e_turn(b + 1)
                if b < B - 3:
                    e_hidden(pe, b + 3)
                if b == 1:
                    e_gates_turn(pe, 1)
                e_down(b)

        @block.scalar
        def _(act):
            def ctx_exp(b):
                act.wait_ge(c_max, b + 1)
                if b >= 2:
                    act.wait_ge(c_turned, b - 1)
                act.activation(prob[:, b % 2, :], ctx_raw[:, b, :], ACT.Exp, bias=cmax[:, b:b + 1],
                               accum_out=csum[:, b:b + 1]).then_inc(c_exp, 1)

            def l0_evacuate(j):
                t, half = L0_TILES[j]
                act.wait_ge(a_ready, j + 1)
                act.activation(l0_dst(t, half), l0_bank(j), ACT.Identity, bias=tbias[:, t:t + 1]).then_inc(a_free, 1)

            def l0_vcopy(half):
                act.wait_ge(l0_vturned, half + 1)
                act.activation(m1[:, half, :], pT[half], ACT.Copy).then_inc(l0_vcopied, 1)

            def l0_pcopy(half):
                act.wait_ge(l0_pturned, half + 1)
                act.activation(sm[:, half, :], pT[half], ACT.Copy).then_inc(l0_pcopied, 1)

            def l0_out(half):
                act.wait_ge(l0_o, half + 1)
                if half:
                    act.wait_ge(l0_y, HB)
                act.activation(OTh[:, :], pO, ACT.Copy).then_inc(l0_ohi, 1)

            ctx_exp(0)
            for b in range(B):
                turn_act(act, 0, b)
                if b < B - 1:
                    ctx_exp(b + 1)
                act.wait_ge(c_turned, b + 1)
                act.activation(cTh[:, :, b * P:(b + 1) * P], four(pS[b % 2]), ACT.Copy).then_inc(c_act, 1)
                if b >= 2:
                    act.wait_ge(c_kv, b - 1)
                act.activation(sm[:, b % 2, :], pT[b % 2], ACT.Copy).then_inc(c_keys, 1)
                if b < NT - 1:
                    split_tile_hi(act, 0, b)
                if b == HB:
                    act.wait_ge(bias_in, 16)
                if HB <= b < HB + 3:
                    l0_evacuate(b - HB)
            l0_evacuate(3)
            soft_exp(act, l0, 0, 0)
            l0_vcopy(0)
            l0_evacuate(4)
            l0_pcopy(0)
            l0_evacuate(5)
            l0_out(0)
            soft_exp(act, l0, 1, 1)
            l0_vcopy(1)
            split_tile_hi(act, 0, NT - 1)
            split_out_hi(act, 0, 0)
            l0_pcopy(1)
            l0_out(1)
            act.wait_ge(res_ready, BIASES[0] + B)
            act.dma_start(row[:, 0:D], rows[R_B1:R_B1 + D].partition_broadcast(P)).then_inc(row_in, 16)
            for b in range(B):
                norm_apply_act(act, 0, [b])
                act.wait_ge(normed, NORMS[0] + b + 1)
                if b >= 2:
                    act.wait_ge(x2_num, b - 1)
                act.activation(prob[:, b % 2, :], x[:, b, :], ACT.Exp).then_inc(x2_exp, 1)
                if 1 <= b < NO:
                    split_out_hi(act, 0, b)
            norm_apply_act(act, 1, range(HB))
            def f_ranks_copy(half):
                act.wait_ge(f_ah, half + 1)
                narrow_copy(act, pT[half], half, LR + NE0).then_inc(f_acopied, 1)

            def f_split(half):
                act.wait_ge(f_turned, half + 1)
                act.activation(halves_of(down_bufs, half, LR)[0], pT[half][0:LR, :], ACT.Copy).then_inc(f_hi, 1)

            for b in range(HB):
                turn_act(act, 2, b)
            for k in range(L0_RANKS):
                split_tile_hi(act, SLOT_ATTN, k, (l0_y, B))
            f_ranks_copy(0)
            norm_apply_act(act, 1, range(HB, B))
            turn_act(act, 2, 4)
            turn_act(act, 2, 5)
            f_split(0)
            turn_act(act, 2, 6)
            turn_act(act, 2, 7)
            f_ranks_copy(1)
            for k in range(L0_RANKS, NT - 1):
                split_tile_hi(act, SLOT_ATTN, k, (f_ah, 2))
            f_split(1)
            act.wait_ge(res_ready, BIASES[2] + B)
            act.dma_start(row[:, 0:D], rows[R_BO5:R_BO5 + D].partition_broadcast(P)).then_inc(row_in, 16)
            for b in range(HB):
                turn_act(act, attn.k, b)
            split_tile_hi(act, SLOT_ATTN, NT - 1, (f_y, B))
            act_rest(act, attn, range(NT))
            grouped(act, g_act, attn, (xattn.k, xattn))
            grouped(act, g_act, xattn, (5, None))
            for k in range(NO):
                split_out_hi(act, SLOT_MOE, k)

            for b in range(B):
                if 1 <= b <= 2:
                    turn_act(act, 5, 2 * b + 2)
                    turn_act(act, 5, 2 * b + 3)
                act.wait_ge(e_turned, b + 1)
                act.activation(halves_of(down_bufs, b % 2)[0], pT[b % 2], ACT.Copy).then_inc(e_hi, 1)
                if b == 2:
                    e_gates_copy(act, 1)
                    e_exps(act, 1)

        @block.vector
        def _(dve):
            def ctx_max(b):
                dve.wait_ge(ctx_loaded[b], 16)
                dve.tensor_reduce(cmax[:, b:b + 1], ctx_raw[:, b, :], AX.X, ALU.max, negate=True).then_inc(c_max, 1)

            def ctx_kvm(b):
                dve.wait_ge(c_exp, b + 1)
                dve.reciprocal(crs[:, b:b + 1], csum[:, b:b + 1]).then_inc(c_rs, 1)
                dve.wait_ge(c_rs, b + 1)
                dve.wait_ge(c_kv, b + 1)
                dve.scalar_tensor_tensor(kvm[:, b, 0:P], pO[:, 0:P], crs[:, b:b + 1], cst[:, C_BLOCK:C_BLOCK + P],
                                         ALU.mult, ALU.mult).then_inc(c_kvm, 1)

            def l0_out_low(half):
                dve.wait_ge(l0_ohi, half + 1)
                dve.tensor_tensor(OTl[:, :], pO, OTh[:, :].bitcast(F32), ALU.subtract).then_inc(l0_olo, 1)

            def l0_add(b):
                dve.wait_ge(l0_y, b + 1)
                dve.wait_ge(res_ready, BIASES[0] + b + 1)
                dve.tensor_tensor(x[:, b, :], pA[b % 2], x[:, b, :], ALU.add).then_inc(added, 1)
                norm_stats(dve, 0, b)

            ctx_max(0)
            ctx_max(1)
            dve.wait_ge(const_in, 32)
            for b in range(B):
                op = dve.tensor_copy(kvm[:, b, P:P + XH], cst[:, C_GROUP:C_GROUP + XH])
            op.then_inc(c_set, 1)
            for b in range(B):
                if b < B - 2:
                    ctx_max(b + 2)
                turn_dve(dve, 0, b)
                dve.wait_ge(c_act, b + 1)
                dve.tensor_tensor(cTl[:, :, b * P:(b + 1) * P], four(pS[b % 2]),
                                  cTh[:, :, b * P:(b + 1) * P].bitcast(F32), ALU.subtract).then_inc(c_low, 1)
                if b:
                    ctx_kvm(b - 1)
            ctx_kvm(B - 1)
            soft_max(dve, l0, 0, 0)
            soft_recip(dve, l0, 0, 0)
            l0_out_low(0)
            soft_max(dve, l0, 1, 1)
            l0_add(0)
            soft_recip(dve, l0, 1, 1)
            for b in range(1, HB):
                l0_add(b)
            l0_out_low(1)
            for b in range(HB, B):
                l0_add(b)
            def x2_divide(b):
                pair = 2 + 2 * (b % 2)
                dve.wait_ge(x2_num, b + 1)
                both = ps[:, pair:pair + 2, 0:2 * (P + XH)].rearrange("p k (c w) -> p k c w", c=2)
                dve.reciprocal(rden[:, b % 2, :, :].rearrange("p (k c) g -> p k c g", k=2), both[:, :, :, P:P + XH])\
                    .then_inc(x2_rden, 1)
                dve.wait_ge(x2_rden, b + 1)
                if b >= 2:
                    dve.wait_ge(x2_turned, b - 1)
                for k in range(2):
                    o = m2[:, b % 2, 2 * k * P:2 * (k + 1) * P].rearrange("p (c g e) -> p c g e", c=2, g=XH)
                    i0 = both[:, k, :, 0:P].rearrange("p c (g e) -> p c g e", g=XH)
                    r = rden[:, b % 2, 2 * k:2 * k + 2, :].unsqueeze(3).to_broadcast([P, 2, XH, XD])
                    dve.tensor_tensor(o, i0, r, ALU.mult).then_inc(x2_mul, 1)

            x2_divide(0)
            for b in range(B):
                if b < B - 1:
                    x2_divide(b + 1)
                if b >= B - 2:
                    for c in (0, 1) if b == B - 2 else (2, 3):
                        turn_dve(dve, 2, c)
                dve.wait_ge(x2_turned, b + 1)
                dve.tensor_tensor(x[:, b, :], ps[:, 6 + b % 2, :], x[:, b, :], ALU.add).then_inc(added, 1)
                norm_stats(dve, 1, b)
            dve.wait_ge(row_in, 32)

            def f_choose(half):
                s0 = 6 * half
                four_seqs = pT[half].rearrange("p (j n) -> p j n", j=HB)
                lg, bl = logit[:, :, 0:NE0], below[:, :, 0:NE0]
                top, index = best[:, 0, :], best[:, 1, :]
                dve.wait_ge(f_aturned, half + 1)
                dve.tensor_tensor(lg, four_seqs[:, :, LR:LR + NE0],
                                  row[:, D:D + NE0].unsqueeze(1).to_broadcast([P, HB, NE0]), ALU.add)\
                    .then_inc(f_step, 1)
                dve.wait_ge(f_step, s0 + 1)
                dve.tensor_reduce(top, lg, AX.X, ALU.max).then_inc(f_step, 1)
                dve.wait_ge(f_step, s0 + 2)
                dve.tensor_tensor(bl, lg, cast4(top, NE0), ALU.is_lt).then_inc(f_step, 1)
                dve.wait_ge(f_step, s0 + 3)
                dve.scalar_tensor_tensor(bl, bl, float(NE), of_all(C_IOTA, NE0), ALU.mult, ALU.add).then_inc(f_step, 1)
                dve.wait_ge(f_step, s0 + 4)
                dve.tensor_reduce(index, bl, AX.X, ALU.min).then_inc(f_step, 1)
                dve.wait_ge(f_step, s0 + 5)
                dve.tensor_tensor(keep[:, :, :], of_all(C_SEG, LR), cast4(index, LR), ALU.is_le).then_inc(f_step, 1)
                dve.wait_ge(f_step, s0 + 6)
                dve.tensor_tensor(m1[:, half, 0:HB * LR].rearrange("p (j r) -> p j r", j=HB), keep[:, :, :],
                                  four_seqs[:, :, 0:LR], ALU.mult).then_inc(f_hm, 1)

            def f_split_low(half):
                dve.wait_ge(f_hi, half + 1)
                th, tl = halves_of(down_bufs, half, LR)
                dve.tensor_tensor(tl, pT[half][0:LR, :], th.bitcast(F32), ALU.subtract).then_inc(f_lo, 1)

            f_choose(0)
            turn_dve(dve, 2, 4)
            turn_dve(dve, 2, 5)
            f_split_low(0)
            turn_dve(dve, 2, 6)
            turn_dve(dve, 2, 7)
            for b in range(B):
                if b == HB:
                    f_split_low(1)
                if b == 1:
                    f_choose(1)
                if b >= B - 2:
                    for c in (0, 1) if b == B - 2 else (2, 3):
                        turn_dve(dve, attn.k, c)
                dve.wait_ge(f_y, b + 1)
                dve.wait_ge(res_ready, BIASES[2] + b + 1)
                dve.tensor_tensor(x[:, b, :], [pS[0], pS[1], pO, pY][b % 4], x[:, b, :], ALU.add).then_inc(added, 1)
                norm_stats(dve, 2, b)
                if b == 4:
                    norm_apply(dve, 2, 0)
            dve_first(dve, attn, range(2))
            norm_apply(dve, 2, 1)
            for k in range(2, NT):
                dve_first(dve, attn, [k])
                for b in TURNS_AFTER.get(k, ()):
                    turn_dve(dve, attn.k, b)
            for g in (attn, xattn):
                dve.sem_inc(g.y_added, 1)
            grouped(dve, g_dve, attn, (xattn.k, xattn))
            grouped(dve, g_dve, xattn, (5, None))

            def e_weigh(b):
                dve.wait_ge(e_up, b + 1)
                if b % HB == 0:
                    dve.wait_ge(e_scale, 3 * (b // HB) + 3)
                if b >= 2:
                    dve.wait_ge(e_turned, b - 1)
                dve.tensor_tensor(m1[:, b % 2, :].rearrange("p (e r) -> p e r", e=NE),
                                  pS[b % 2].rearrange("p (e r) -> p e r", e=NE),
                                  weight[:, b // HB, b % HB, :].unsqueeze(2).to_broadcast([P, NE, D // NE]),
                                  ALU.mult).then_inc(e_hw, 1)

            def e_split(b):
                dve.wait_ge(e_hi, b + 1)
                th, tl = halves_of(down_bufs, b % 2)
                dve.tensor_tensor(tl, pT[b % 2], th.bitcast(F32), ALU.subtract).then_inc(e_lo, 1)

            e_weigh(0)
            norm_apply(dve, xattn.k, 1)
            e_weigh(1)
            e_split(0)
            turn_dve(dve, 5, 4)
            turn_dve(dve, 5, 5)
            turn_dve(dve, 5, 6)
            turn_dve(dve, 5, 7)
            for b in range(B):
                if b < B - 2:
                    e_weigh(b + 2)
                if b < B - 1:
                    e_split(b + 1)
                if b == HB:
                    norm_apply(dve, 5, 0)
                dve.wait_ge(e_y, b + 1)
                dve.tensor_tensor(x[:, b, :], ps[:, 6 + b % 2, :], x[:, b, :], ALU.add).then_inc(added, 1)
                norm_stats(dve, 5, b)
                if b == 1:
                    e_choose(dve, 1)
            norm_apply(dve, 5, 1)
            norm_apply(dve, 5, 2)

        @block.gpsimd
        def _(pool):
            pool.wait_ge(const_in, 32)
            for b in range(B):
                bc = slice(b * P, (b + 1) * P)
                pool.wait_ge(c_low, b + 1)
                if b >= 2:
                    pool.wait_ge(c_kv, b - 1)
                pool.tensor_tensor(four(m1[:, b % 2, :]), cTh[:, :, bc].bitcast(F32), cTl[:, :, bc].bitcast(F32), ALU.add)\
                    .then_inc(c_copied, 1)
                if b < NT - 1:
                    split_tile_lo(pool, 0, b)
            for b in range(HB):
                residual_bias(pool, 0, b, 2)
            soft_norm(pool, l0, 0, 0)
            for b in range(HB, B):
                residual_bias(pool, 0, b, 2)
            soft_norm(pool, l0, 1, 1)
            split_tile_lo(pool, 0, NT - 1)
            split_out_lo(pool, 0, 0)
            norm_pow(pool, 0, 0)
            norm_shift(pool, 0, 0)
            split_out_lo(pool, 0, 1)
            norm_pow(pool, 0, 1)
            norm_shift(pool, 0, 1)
            split_out_lo(pool, 0, 2)
            split_out_lo(pool, 0, 3)
            norm_pow(pool, 1, 0)
            norm_shift(pool, 1, 0)
            for k in range(L0_RANKS):
                split_tile_lo(pool, SLOT_ATTN, k)
            norm_pow(pool, 1, 1)
            norm_shift(pool, 1, 1)
            for b in range(B):
                residual_bias(pool, 2, b, 3)
            for k in range(L0_RANKS, NT - 1):
                split_tile_lo(pool, SLOT_ATTN, k)
            norm_pow(pool, 2, 0)
            norm_pow(pool, 2, 1)
            split_tile_lo(pool, SLOT_ATTN, NT - 1)
            pool_first(pool, attn, range(NT))
            grouped(pool, g_pool, attn, (xattn.k, xattn))
            for b in range(B):
                residual_bias(pool, xattn.k, b, 4)
            grouped(pool, g_pool, xattn, (5, None))
            for k in range(NO):
                split_out_lo(pool, SLOT_MOE, k)
            norm_pow(pool, 5, 0)
            norm_pow(pool, 5, 1)
            norm_pow(pool, 5, 2)


def constants():
    import numpy as np

    c = np.zeros((P, CONSTS), np.float32)
    c[:, C_ID:C_ID + P] = np.eye(P)
    inv = 1.0 / 500000.0 ** (np.arange(0, HD, 2, dtype=np.float64) / HD)
    wavelen = 2.0 * np.pi / inv
    smooth = (1024 / wavelen - 1.0) / (4.0 - 1.0)
    scaled = np.where(wavelen > 1024 / 1.0, inv / 8.0, inv)
    mid = (wavelen <= 1024 / 1.0) & (wavelen >= 1024 / 4.0)
    scaled = np.where(mid, (1 - smooth) * inv / 8.0 + smooth * inv, scaled).astype(np.float32)
    emb = np.arange(P, dtype=np.float32)[:, None] * scaled[None, :]
    cos, sin = np.cos(emb).T, np.sin(emb).T
    c[:, C_COS:C_COS + P] = np.concatenate([cos, cos])
    c[:, C_SIN:C_SIN + P] = np.concatenate([sin, -sin])
    c[:, C_CAUSAL:C_CAUSAL + P] = np.where(np.tril(np.ones((P, P))) > 0, 0.0, NEG)
    head = np.arange(P) // XD
    c[:, C_BLOCK:C_BLOCK + P] = head[:, None] == head[None, :]
    c[:, C_GROUP:C_GROUP + XH] = head[:, None] == np.arange(XH)[None, :]
    c[:, C_SEG:C_SEG + LR] = np.searchsorted([8, 16, 32, 64], np.arange(LR), side="right")
    c[:, C_IOTA:C_IOTA + NE] = np.arange(NE)
    c[:, C_POW:C_POW + 8] = -0.5
    return c


def chunks(w):
    return w.reshape(-1, P, w.shape[1]).transpose(1, 0, 2)


def layout(a):
    import numpy as np

    wt = np.zeros((SLOTS, NT, P, D), np.float32)
    wo = np.zeros((SLOTS, NO, P, D), np.float32)
    bias = np.zeros((P, SLOTS, 8), np.float32)

    def tile(s, t, w):
        wt[s, t] = chunks(w).reshape(P, D)

    def columns(w, n):
        return w[:, n * P:(n + 1) * P]

    for t, n in ((L0_K, 1), (L0_V, 2), (L0_Q, 0)):
        tile(0, t, columns(a["L0_attn_Wqkv"], n))
        bias[:, 0, t] = a["L0_attn_bqkv"][n * P:(n + 1) * P]
    wt[0, L0_OUT] = a["L0_attn_Wo"]
    ranks = wt[0, L0_RANKS].reshape(P, NC, P)
    ranks[:, :, :LR] = chunks(a["L0_ffn_A"].T)
    ranks[:, :, LR:LR + NE0] = chunks(a["L0_ffn_gate_w"].T)
    wt[0, L0_B, :LR] = a["L0_ffn_B"].T
    wo[0] = a["L0_ffn_W"].T.reshape(NO, P, D)
    for g in range(GROUPS):
        s = SLOT_ATTN + g
        tile(s, K_TILE, columns(a["L1_attn_wk"], g))
        tile(s, V_TILE, columns(a["L1_attn_wv"], g))
        for h in range(REP):
            tile(s, 1 + h, columns(a["L1_attn_wq"], REP * g + h))
        wo[s] = a["L1_attn_wo"][g * D:(g + 1) * D].reshape(NO, P, D)
        s = SLOT_XATTN + g
        for t, n in ((K_TILE, g), (V_TILE, GROUPS + g)):
            tile(s, t, columns(a["L1_xattn_Wkv"], n))
            bias[:, s, t] = a["L1_xattn_bkv"][n * P:(n + 1) * P]
        for h in range(REP):
            n = REP * g + h
            tile(s, 1 + h, columns(a["L1_xattn_Wq"], n))
            bias[:, s, 1 + h] = a["L1_xattn_bq"][n * P:(n + 1) * P]
        wo[s] = a["L1_xattn_Wo"][g * D:(g + 1) * D].reshape(NO, P, D)
    s = SLOT_MOE
    wt[s, :NC] = a["L1_ffn_lora_A"].reshape(D, D).T.reshape(NC, P, D)
    wt[s, NC].reshape(P, NC, P)[:, :, :NE] = chunks(a["L1_ffn_gate_w"].T)
    wo[s] = a["L1_ffn_lora_B"].transpose(0, 2, 1).reshape(NO, P, D)
    rows = np.zeros((ROWS,), np.float32)
    rows[R_BO0:R_BO0 + D] = a["L0_attn_bo"]
    rows[R_B1:R_B1 + D] = a["L0_ffn_b"]
    rows[R_BO5:R_BO5 + D] = a["L1_xattn_bo"]
    rows[R_GATE:R_GATE + NE0] = a["L0_ffn_gate_b"]
    return {"x": a["x"], "ctx": a["ctx_4096"], "w_tile": wt, "w_out": wo,
            "biases": bias.reshape(P, SLOTS * 8), "consts": constants(), "rows": rows}


def kernel(**inputs):
    import numpy as np
    import concourse.bacc as bacc
    from concourse.bass_utils import run_bass_kernel_spmd

    arrays = {"in_" + k: np.ascontiguousarray(v) for k, v in layout({k: np.asarray(v) for k, v in inputs.items()}).items()}
    nc = bacc.Bacc("TRN2", target_bir_lowering=False, num_devices=1)
    aps = [nc.dram_tensor(n, a.shape, F32, kind="ExternalInput").ap() for n, a in arrays.items()]
    out = nc.dram_tensor("out", [B, P, D], F32, kind="ExternalOutput").ap()
    build(nc, *aps, out)
    r = run_bass_kernel_spmd(nc, [arrays], core_ids=[0])
    return r.results[0]["out"]
```
